# Optimizing a Trainium2 kernel written in Bass

```python
import numpy as np
import jax
import jax.numpy as jnp

def _softmax(x, axis=-1):
    return jax.nn.softmax(x, axis=axis)

def _gelu(x):
    return jax.nn.gelu(x, approximate=True)

def _silu(x):
    return jax.nn.silu(x)

def _sigmoid(x):
    return jax.nn.sigmoid(x)

def _layernorm(x, axis=-1, eps=1e-05):
    m = jnp.mean(x, axis=axis, keepdims=True)
    v = jnp.var(x, axis=axis, keepdims=True)
    return (x - m) / jnp.sqrt(v + eps)

def _scatter_add(tgt, idx, src, axis=0):
    return tgt.at[idx].add(src)

def _segment_sum(src, seg, n):
    return jax.ops.segment_sum(src, seg, n)
kernel_name = 'mk_gnn_ffn_d4_gnn_r16_268351'

def setup_inputs(seed: int=0):
    np.random.seed(seed)
    _w = jnp.asarray

    def _rec_inputs():
        import jax
        import jax.numpy as jnp
        _gk = jax.random.key(seed)
        x = -8.776e-05 + 1 * jax.random.normal(jax.random.fold_in(_gk, 1), (3125, 256), jnp.float32)
        src = jax.random.randint(jax.random.fold_in(_gk, 2), (50000,), 0, 3125, jnp.int32)
        dst = jax.random.randint(jax.random.fold_in(_gk, 3), (50000,), 0, 3125, jnp.int32)
        _o = jnp.argsort(dst, stable=True)
        src = src[_o]
        dst = dst[_o]
        edge_type_16 = jax.random.randint(jax.random.fold_in(_gk, 13), (50000,), 0, 16, jnp.int32)
        edge_weight1 = jax.random.uniform(jax.random.fold_in(_gk, 14), (50000, 1), jnp.float32, 0.0, 0.999998)
        return (x, src, dst, edge_type_16, edge_weight1)
    x, src, dst, edge_type_16, edge_weight1 = _rec_inputs()

    def _L0_gnn_setup():
        import jax, jax.numpy as jnp
        import numpy as np
        N_NODES = 1250
        N_EDGES = 20000
        H = 256
        R = 16
        B = 128
        SUB = H // B

        def _rel_graph_conv_bdd(x, src, dst, etype, norm, w, loop_w, bias):
            e = src.shape[0]
            n = x.shape[0]
            nb = w.shape[1]
            xs = x[src].reshape(e, nb, -1)
            we = w[etype]
            msg = jnp.einsum('ebi,ebio->ebo', xs, we)
            msg = msg.reshape(e, -1) * norm
            agg = jax.ops.segment_sum(msg, dst, num_segments=n)
            return agg + bias + x @ loop_w
        key = jax.random.key(seed)
        ks = jax.random.split(key, 11)
        scale = 1.0 / np.sqrt(H)
        return {'x': jax.random.normal(ks[0], (N_NODES, H), jnp.float32), 'src': jax.random.randint(ks[1], (N_EDGES,), 0, N_NODES), 'dst': jax.random.randint(ks[2], (N_EDGES,), 0, N_NODES), 'etype': jax.random.randint(ks[3], (N_EDGES,), 0, R), 'norm': jax.random.uniform(ks[4], (N_EDGES, 1), jnp.float32), 'w1': jax.random.normal(ks[5], (R, B, SUB, SUB), jnp.float32) * scale, 'loop_w1': jax.random.normal(ks[6], (H, H), jnp.float32) * scale, 'b1': jnp.zeros((H,), jnp.float32), 'w2': jax.random.normal(ks[7], (R, B, SUB, SUB), jnp.float32) * scale, 'loop_w2': jax.random.normal(ks[8], (H, H), jnp.float32) * scale, 'b2': jnp.zeros((H,), jnp.float32)}
    _L0_gnn_all = _L0_gnn_setup()
    _L0_gnn_in = {k: v for k, v in _L0_gnn_all.items() if k in ('w1', 'loop_w1', 'b1', 'w2', 'loop_w2', 'b2')}
    del _L0_gnn_all

    def _L0_ffn_setup():
        import jax, jax.numpy as jnp
        import numpy as np
        BN_EPS = 0.001

        def _bn(h, g, b, m, v):
            return g * (h - m) * jax.lax.rsqrt(v + BN_EPS) + b
        key = jax.random.key(seed)
        ks = jax.random.split(key, 8)
        B, F, Df = (256, 64, 256)
        E, H, D = (8, 256, 256)
        s1 = 1.0 / np.sqrt(Df)
        s2 = 1.0 / np.sqrt(H)
        return {'x': jax.random.normal(ks[0], (B, F, Df), jnp.float32), 'Wr': jax.random.normal(ks[1], (Df, E), jnp.float32) * s1, 'br': jnp.zeros((E,), jnp.float32), 'W1': jax.random.normal(ks[2], (E, Df, H), jnp.float32) * s1, 'b1': jnp.zeros((E, H), jnp.float32), 'g1': jnp.ones((E, H), jnp.float32), 'be1': jnp.zeros((E, H), jnp.float32), 'm1': jnp.zeros((E, H), jnp.float32), 'v1': jnp.ones((E, H), jnp.float32), 'W2': jax.random.normal(ks[3], (E, H, H), jnp.float32) * s2, 'b2': jnp.zeros((E, H), jnp.float32), 'g2': jnp.ones((E, H), jnp.float32), 'be2': jnp.zeros((E, H), jnp.float32), 'm2': jnp.zeros((E, H), jnp.float32), 'v2': jnp.ones((E, H), jnp.float32), 'Wo': jax.random.normal(ks[4], (E, H, D), jnp.float32) * s2, 'bo': jnp.zeros((E, D), jnp.float32)}
    _L0_ffn_all = _L0_ffn_setup()
    _L0_ffn_in = {k: v for k, v in _L0_ffn_all.items() if k in ('Wr', 'br', 'W1', 'b1', 'g1', 'be1', 'm1', 'v1', 'W2', 'b2', 'g2', 'be2', 'm2', 'v2', 'Wo', 'bo')}
    del _L0_ffn_all

    def _L1_gnn_setup():
        import jax, jax.numpy as jnp
        import numpy as np
        N, E, D = (625, 20000, 256)

        def _add_self_loops(src, dst, n):
            loop = jnp.arange(n, dtype=src.dtype)
            return (jnp.concatenate([src, loop]), jnp.concatenate([dst, loop]))

        def _gcn_conv(x, W, b, src, dst, n):
            xw = x @ W
            deg = jax.ops.segment_sum(jnp.ones(src.shape[0], x.dtype), dst, num_segments=n)
            dinv = jnp.where(deg > 0, jax.lax.rsqrt(deg), 0.0)
            norm = dinv[src] * dinv[dst]
            agg = jax.ops.segment_sum(xw[src] * norm[:, None], dst, num_segments=n)
            return agg + b

        def _gat_conv(x, W, a_src, a_dst, b, src, dst, n):
            xw = x @ W
            e = jax.nn.leaky_relu((xw @ a_src)[src] + (xw @ a_dst)[dst], 0.2)
            m = jax.ops.segment_max(e, dst, num_segments=n)
            ex = jnp.exp(e - m[dst])
            s = jax.ops.segment_sum(ex, dst, num_segments=n)
            alpha = ex / (s[dst] + 1e-16)
            agg = jax.ops.segment_sum(alpha[:, None] * xw[src], dst, num_segments=n)
            return agg + b
        key = jax.random.key(seed)
        ks = jax.random.split(key, 6)
        return {'event_emb': jax.random.normal(ks[0], (N, D), jnp.float32), 'edge_index': jax.random.randint(ks[1], (2, E), 0, N), 'W1': jax.random.normal(ks[2], (D, D), jnp.float32) / np.sqrt(D).astype(np.float32), 'b1': jnp.zeros((D,), jnp.float32), 'W2': jax.random.normal(ks[3], (D, D), jnp.float32) / np.sqrt(D).astype(np.float32), 'att_src': jax.random.normal(ks[4], (D,), jnp.float32) / np.sqrt(D).astype(np.float32), 'att_dst': jax.random.normal(ks[5], (D,), jnp.float32) / np.sqrt(D).astype(np.float32), 'b2': jnp.zeros((D,), jnp.float32)}
    _L1_gnn_all = _L1_gnn_setup()
    _L1_gnn_in = {k: v for k, v in _L1_gnn_all.items() if k in ('W1', 'b1', 'W2', 'att_src', 'att_dst', 'b2')}
    del _L1_gnn_all

    def _L1_ffn_setup():
        import math
        import jax, jax.numpy as jnp
        import numpy as np
        CAPACITY_FACTOR = 1.25
        TOP_K = 2
        LN_EPS = 1e-05

        def _layer_norm(x, gamma, beta):
            mu = jnp.mean(x, axis=-1, keepdims=True)
            var = jnp.var(x, axis=-1, keepdims=True)
            return (x - mu) * jax.lax.rsqrt(var + LN_EPS) * gamma + beta
        key = jax.random.key(seed)
        ks = jax.random.split(key, 4)
        B, S, D, F, E = (8, 256, 256, 512, 8)
        x = jax.random.normal(ks[0], (B, S, D), dtype=jnp.float32)
        Wr = jax.random.normal(ks[1], (D, E), dtype=jnp.float32) / np.sqrt(D)
        br = jnp.zeros((E,), jnp.float32)
        W1 = jax.random.normal(ks[2], (E, D, F), dtype=jnp.float32) / np.sqrt(D)
        b1 = jnp.zeros((E, F), jnp.float32)
        W2 = jax.random.normal(ks[3], (E, F, D), dtype=jnp.float32) / np.sqrt(F)
        b2 = jnp.zeros((E, D), jnp.float32)
        gamma = jnp.ones((D,), jnp.float32)
        beta = jnp.zeros((D,), jnp.float32)
        return {'x': x, 'Wr': Wr, 'br': br, 'W1': W1, 'b1': b1, 'W2': W2, 'b2': b2, 'gamma': gamma, 'beta': beta}
    _L1_ffn_all = _L1_ffn_setup()
    _L1_ffn_in = {k: v for k, v in _L1_ffn_all.items() if k in ('Wr', 'br', 'W1', 'b1', 'W2', 'b2', 'gamma', 'beta')}
    del _L1_ffn_all

    def _L2_gnn_setup():
        import jax, jax.numpy as jnp
        import numpy as np
        N = 6250
        E = 100000
        IN_FEATS = 256
        OUT_FEATS = 256
        MAXK = 32

        def _maxk(x, k):
            _, idx = jax.lax.top_k(x, k)
            rows = jnp.arange(x.shape[0])[:, None]
            mask = jnp.zeros_like(x).at[rows, idx].set(1.0)
            return x * mask
        key = jax.random.key(seed)
        k1, k2, k3, k4, k5 = jax.random.split(key, 5)
        feat = jax.random.normal(k1, (N, IN_FEATS), dtype=jnp.float32)
        W_self = jax.random.normal(k2, (IN_FEATS, OUT_FEATS), dtype=jnp.float32) * (1.0 / np.sqrt(IN_FEATS))
        W_neigh = jax.random.normal(k3, (IN_FEATS, OUT_FEATS), dtype=jnp.float32) * (1.0 / np.sqrt(IN_FEATS))
        src = jax.random.randint(k4, (E,), 0, N, dtype=jnp.int64)
        dst = jax.random.randint(k5, (E,), 0, N, dtype=jnp.int64)
        return {'feat': feat, 'W_self': W_self, 'W_neigh': W_neigh, 'src': src, 'dst': dst}
    _L2_gnn_all = _L2_gnn_setup()
    _L2_gnn_in = {k: v for k, v in _L2_gnn_all.items() if k in ('W_self', 'W_neigh')}
    del _L2_gnn_all

    def _L2_ffn_setup():
        import jax, jax.numpy as jnp
        import numpy as np
        TOP_K = 2
        key = jax.random.key(seed)
        ks = jax.random.split(key, 4)
        B, L, D, H, E = (8, 256, 256, 1024, 8)
        s = 0.02
        return {'x': jax.random.normal(ks[0], (B, L, D), jnp.float32), 'Wg': jax.random.normal(ks[1], (D, E), jnp.float32) * s, 'bg': jnp.zeros((E,), jnp.float32), 'W1': jax.random.normal(ks[2], (E, D, H), jnp.float32) * s, 'b1': jnp.zeros((E, H), jnp.float32), 'W2': jax.random.normal(ks[3], (E, H, D), jnp.float32) * s, 'b2': jnp.zeros((E, D), jnp.float32)}
    _L2_ffn_all = _L2_ffn_setup()
    _L2_ffn_in = {k: v for k, v in _L2_ffn_all.items() if k in ('Wg', 'bg', 'W1', 'b1', 'W2', 'b2')}
    del _L2_ffn_all

    def _L3_gnn_setup():
        import jax, jax.numpy as jnp
        import numpy as np
        N = 1250
        E = 20000
        D_IN = 256
        HID = 64
        HEADS = 4
        D_OUT = 256
        EPS = 1e-05
        SLOPE = 0.2

        def _gat(x, src, dst, W, a_src, a_dst, b, heads, ch, concat):
            n = x.shape[0]
            h = (x @ W).reshape(n, heads, ch)
            es = (h * a_src).sum(-1)
            ed = (h * a_dst).sum(-1)
            e = jax.nn.leaky_relu(es[src] + ed[dst], SLOPE)
            m = jax.ops.segment_max(e, dst, num_segments=n)
            w = jnp.exp(e - m[dst])
            den = jax.ops.segment_sum(w, dst, num_segments=n)
            alpha = w / den[dst]
            msg = h[src] * alpha[:, :, None]
            out = jax.ops.segment_sum(msg, dst, num_segments=n)
            out = out.reshape(n, heads * ch) if concat else out.mean(axis=1)
            return out + b

        def _layernorm(x, g, b):
            mu = x.mean(-1, keepdims=True)
            v = ((x - mu) ** 2).mean(-1, keepdims=True)
            return (x - mu) * jax.lax.rsqrt(v + EPS) * g + b
        key = jax.random.key(seed)
        ks = jax.random.split(key, 10)

        def glorot(k, shape):
            fan_in, fan_out = (shape[0], int(np.prod(shape[1:])))
            s = np.sqrt(2.0 / (fan_in + fan_out)).astype(np.float32)
            return jax.random.normal(k, shape, dtype=jnp.float32) * s
        x = jax.random.normal(ks[0], (N, D_IN), dtype=jnp.float32)
        edge_index = jax.random.randint(ks[1], (2, E), 0, N, dtype=jnp.int64)
        return {'x': x, 'edge_index': edge_index, 'W1': glorot(ks[2], (D_IN, HEADS * HID)), 'a1_src': glorot(ks[3], (HEADS, HID)), 'a1_dst': glorot(ks[4], (HEADS, HID)), 'b1': jnp.zeros((HEADS * HID,), jnp.float32), 'ln_g': jnp.ones((HEADS * HID,), jnp.float32), 'ln_b': jnp.zeros((HEADS * HID,), jnp.float32), 'W2': glorot(ks[5], (HEADS * HID, D_OUT)), 'a2_src': glorot(ks[6], (1, D_OUT)), 'a2_dst': glorot(ks[7], (1, D_OUT)), 'b2': jnp.zeros((D_OUT,), jnp.float32)}
    _L3_gnn_all = _L3_gnn_setup()
    _L3_gnn_in = {k: v for k, v in _L3_gnn_all.items() if k in ('W1', 'a1_src', 'a1_dst', 'b1', 'ln_g', 'ln_b', 'W2', 'a2_src', 'a2_dst', 'b2')}
    del _L3_gnn_all

    def _L3_ffn_setup():
        import jax, jax.numpy as jnp
        import numpy as np
        B, S, D = (8, 256, 256)
        H = 4 * D
        CAPACITY = 0.5
        key = jax.random.key(seed)
        ks = jax.random.split(key, 6)
        x = jax.random.normal(ks[0], (B, S, D), dtype=jnp.float32)
        attention_mask = jnp.zeros((B, 1, 1, S), dtype=jnp.float32)
        wr = jax.random.normal(ks[1], (D, 1), dtype=jnp.float32) * 0.02
        br = jnp.zeros((1,), dtype=jnp.float32)
        w1 = jax.random.normal(ks[2], (D, H), dtype=jnp.float32) * 0.02
        b1 = jnp.zeros((H,), dtype=jnp.float32)
        w2 = jax.random.normal(ks[3], (H, D), dtype=jnp.float32) * 0.02
        b2 = jnp.zeros((D,), dtype=jnp.float32)
        return {'x': x, 'attention_mask': attention_mask, 'wr': wr, 'br': br, 'w1': w1, 'b1': b1, 'w2': w2, 'b2': b2}
    _L3_ffn_all = _L3_ffn_setup()
    _L3_ffn_in = {k: v for k, v in _L3_ffn_all.items() if k in ('attention_mask', 'wr', 'br', 'w1', 'b1', 'w2', 'b2')}
    del _L3_ffn_all
    return {'x': x, 'src': src, 'dst': dst, 'edge_type_16': edge_type_16, 'edge_weight1': edge_weight1, 'L0_gnn_w1': _L0_gnn_in['w1'], 'L0_gnn_loop_w1': _L0_gnn_in['loop_w1'], 'L0_gnn_b1': _L0_gnn_in['b1'], 'L0_gnn_w2': _L0_gnn_in['w2'], 'L0_gnn_loop_w2': _L0_gnn_in['loop_w2'], 'L0_gnn_b2': _L0_gnn_in['b2'], 'L0_ffn_Wr': _L0_ffn_in['Wr'], 'L0_ffn_br': _L0_ffn_in['br'], 'L0_ffn_W1': _L0_ffn_in['W1'], 'L0_ffn_b1': _L0_ffn_in['b1'], 'L0_ffn_g1': _L0_ffn_in['g1'], 'L0_ffn_be1': _L0_ffn_in['be1'], 'L0_ffn_m1': _L0_ffn_in['m1'], 'L0_ffn_v1': _L0_ffn_in['v1'], 'L0_ffn_W2': _L0_ffn_in['W2'], 'L0_ffn_b2': _L0_ffn_in['b2'], 'L0_ffn_g2': _L0_ffn_in['g2'], 'L0_ffn_be2': _L0_ffn_in['be2'], 'L0_ffn_m2': _L0_ffn_in['m2'], 'L0_ffn_v2': _L0_ffn_in['v2'], 'L0_ffn_Wo': _L0_ffn_in['Wo'], 'L0_ffn_bo': _L0_ffn_in['bo'], 'L1_gnn_W1': _L1_gnn_in['W1'], 'L1_gnn_b1': _L1_gnn_in['b1'], 'L1_gnn_W2': _L1_gnn_in['W2'], 'L1_gnn_att_src': _L1_gnn_in['att_src'], 'L1_gnn_att_dst': _L1_gnn_in['att_dst'], 'L1_gnn_b2': _L1_gnn_in['b2'], 'L1_ffn_Wr': _L1_ffn_in['Wr'], 'L1_ffn_br': _L1_ffn_in['br'], 'L1_ffn_W1': _L1_ffn_in['W1'], 'L1_ffn_b1': _L1_ffn_in['b1'], 'L1_ffn_W2': _L1_ffn_in['W2'], 'L1_ffn_b2': _L1_ffn_in['b2'], 'L1_ffn_gamma': _L1_ffn_in['gamma'], 'L1_ffn_beta': _L1_ffn_in['beta'], 'L2_gnn_W_self': _L2_gnn_in['W_self'], 'L2_gnn_W_neigh': _L2_gnn_in['W_neigh'], 'L2_ffn_Wg': _L2_ffn_in['Wg'], 'L2_ffn_bg': _L2_ffn_in['bg'], 'L2_ffn_W1': _L2_ffn_in['W1'], 'L2_ffn_b1': _L2_ffn_in['b1'], 'L2_ffn_W2': _L2_ffn_in['W2'], 'L2_ffn_b2': _L2_ffn_in['b2'], 'L3_gnn_W1': _L3_gnn_in['W1'], 'L3_gnn_a1_src': _L3_gnn_in['a1_src'], 'L3_gnn_a1_dst': _L3_gnn_in['a1_dst'], 'L3_gnn_b1': _L3_gnn_in['b1'], 'L3_gnn_ln_g': _L3_gnn_in['ln_g'], 'L3_gnn_ln_b': _L3_gnn_in['ln_b'], 'L3_gnn_W2': _L3_gnn_in['W2'], 'L3_gnn_a2_src': _L3_gnn_in['a2_src'], 'L3_gnn_a2_dst': _L3_gnn_in['a2_dst'], 'L3_gnn_b2': _L3_gnn_in['b2'], 'L3_ffn_attention_mask': _L3_ffn_in['attention_mask'], 'L3_ffn_wr': _L3_ffn_in['wr'], 'L3_ffn_br': _L3_ffn_in['br'], 'L3_ffn_w1': _L3_ffn_in['w1'], 'L3_ffn_b1': _L3_ffn_in['b1'], 'L3_ffn_w2': _L3_ffn_in['w2'], 'L3_ffn_b2': _L3_ffn_in['b2']}

def reference(x, src, dst, edge_type_16, edge_weight1, L0_gnn_w1, L0_gnn_loop_w1, L0_gnn_b1, L0_gnn_w2, L0_gnn_loop_w2, L0_gnn_b2, L0_ffn_Wr, L0_ffn_br, L0_ffn_W1, L0_ffn_b1, L0_ffn_g1, L0_ffn_be1, L0_ffn_m1, L0_ffn_v1, L0_ffn_W2, L0_ffn_b2, L0_ffn_g2, L0_ffn_be2, L0_ffn_m2, L0_ffn_v2, L0_ffn_Wo, L0_ffn_bo, L1_gnn_W1, L1_gnn_b1, L1_gnn_W2, L1_gnn_att_src, L1_gnn_att_dst, L1_gnn_b2, L1_ffn_Wr, L1_ffn_br, L1_ffn_W1, L1_ffn_b1, L1_ffn_W2, L1_ffn_b2, L1_ffn_gamma, L1_ffn_beta, L2_gnn_W_self, L2_gnn_W_neigh, L2_ffn_Wg, L2_ffn_bg, L2_ffn_W1, L2_ffn_b1, L2_ffn_W2, L2_ffn_b2, L3_gnn_W1, L3_gnn_a1_src, L3_gnn_a1_dst, L3_gnn_b1, L3_gnn_ln_g, L3_gnn_ln_b, L3_gnn_W2, L3_gnn_a2_src, L3_gnn_a2_dst, L3_gnn_b2, L3_ffn_attention_mask, L3_ffn_wr, L3_ffn_br, L3_ffn_w1, L3_ffn_b1, L3_ffn_w2, L3_ffn_b2):
    import jax
    import jax.numpy as jnp

    def _L0_gnn_ref(x, src, dst, etype, norm, w1, loop_w1, b1, w2, loop_w2, b2):
        import jax, jax.numpy as jnp
        import numpy as np
        N_NODES = 1250
        N_EDGES = 20000
        H = 256
        R = 16
        B = 128
        SUB = H // B

        def _rel_graph_conv_bdd(x, src, dst, etype, norm, w, loop_w, bias):
            e = src.shape[0]
            n = x.shape[0]
            nb = w.shape[1]
            xs = x[src].reshape(e, nb, -1)
            we = w[etype]
            msg = jnp.einsum('ebi,ebio->ebo', xs, we)
            msg = msg.reshape(e, -1) * norm
            agg = jax.ops.segment_sum(msg, dst, num_segments=n)
            return agg + bias + x @ loop_w
        h = jax.nn.relu(_rel_graph_conv_bdd(x, src, dst, etype, norm, w1, loop_w1, b1))
        return _rel_graph_conv_bdd(h, src, dst, etype, norm, w2, loop_w2, b2)

    def _L0_ffn_ref(x, Wr, br, W1, b1, g1, be1, m1, v1, W2, b2, g2, be2, m2, v2, Wo, bo):
        import jax, jax.numpy as jnp
        import numpy as np
        BN_EPS = 0.001

        def _bn(h, g, b, m, v):
            return g * (h - m) * jax.lax.rsqrt(v + BN_EPS) + b
        feat = jnp.mean(x, axis=0)
        w = jax.nn.softmax(feat @ Wr + br, axis=-1)
        h = jnp.einsum('bfd,edh->bfeh', x, W1) + b1
        h = jax.nn.relu(_bn(h, g1, be1, m1, v1))
        h = jnp.einsum('bfeh,ehk->bfek', h, W2) + b2
        h = jax.nn.relu(_bn(h, g2, be2, m2, v2))
        y = jnp.einsum('bfeh,ehd->bfed', h, Wo) + bo
        return jnp.einsum('bfed,fe->bfd', y, w)

    def _L1_gnn_ref(event_emb, edge_index, W1, b1, W2, att_src, att_dst, b2):
        import jax, jax.numpy as jnp
        import numpy as np
        N, E, D = (625, 20000, 256)

        def _add_self_loops(src, dst, n):
            loop = jnp.arange(n, dtype=src.dtype)
            return (jnp.concatenate([src, loop]), jnp.concatenate([dst, loop]))

        def _gcn_conv(x, W, b, src, dst, n):
            xw = x @ W
            deg = jax.ops.segment_sum(jnp.ones(src.shape[0], x.dtype), dst, num_segments=n)
            dinv = jnp.where(deg > 0, jax.lax.rsqrt(deg), 0.0)
            norm = dinv[src] * dinv[dst]
            agg = jax.ops.segment_sum(xw[src] * norm[:, None], dst, num_segments=n)
            return agg + b

        def _gat_conv(x, W, a_src, a_dst, b, src, dst, n):
            xw = x @ W
            e = jax.nn.leaky_relu((xw @ a_src)[src] + (xw @ a_dst)[dst], 0.2)
            m = jax.ops.segment_max(e, dst, num_segments=n)
            ex = jnp.exp(e - m[dst])
            s = jax.ops.segment_sum(ex, dst, num_segments=n)
            alpha = ex / (s[dst] + 1e-16)
            agg = jax.ops.segment_sum(alpha[:, None] * xw[src], dst, num_segments=n)
            return agg + b
        n = event_emb.shape[0]
        src, dst = _add_self_loops(edge_index[0], edge_index[1], n)
        x = jax.nn.relu(_gcn_conv(event_emb, W1, b1, src, dst, n))
        x = jax.nn.relu(_gat_conv(x, W2, att_src, att_dst, b2, src, dst, n))
        return x

    def _L1_ffn_ref(x, Wr, br, W1, b1, W2, b2, gamma, beta):
        import math
        import jax, jax.numpy as jnp
        import numpy as np
        CAPACITY_FACTOR = 1.25
        TOP_K = 2
        LN_EPS = 1e-05

        def _layer_norm(x, gamma, beta):
            mu = jnp.mean(x, axis=-1, keepdims=True)
            var = jnp.var(x, axis=-1, keepdims=True)
            return (x - mu) * jax.lax.rsqrt(var + LN_EPS) * gamma + beta
        B, S, D = x.shape
        E = Wr.shape[1]
        N = B * S
        K = TOP_K
        logits = jnp.mean(x, axis=1) @ Wr + br
        routing_weights = jax.nn.softmax(logits, axis=-1)
        capacity = float(math.ceil(N * CAPACITY_FACTOR / E))
        expected_loads = routing_weights.sum(axis=0) * (N / B)
        scale = jnp.where(expected_loads > capacity, capacity / expected_loads, 1.0)
        routing_weights = jax.nn.softmax(routing_weights * scale, axis=-1)
        rw_tok = jnp.broadcast_to(routing_weights[:, None, :], (B, S, E)).reshape(N, E)
        top_w, top_i = jax.lax.top_k(rw_tok, K)
        top_w = jax.nn.softmax(top_w, axis=-1)
        xf = x.reshape(N, D)
        h = jax.nn.gelu(jnp.einsum('nd,edf->enf', xf, W1) + b1[:, None, :], approximate=False)
        y = jnp.einsum('enf,efd->end', h, W2) + b2[:, None, :]
        w_dense = jnp.zeros((N, E), x.dtype).at[jnp.arange(N)[:, None], top_i].add(top_w)
        out = jnp.einsum('ne,end->nd', w_dense, y).reshape(B, S, D)
        out = _layer_norm(out + x, gamma, beta)
        return out

    def _L2_gnn_ref(feat, W_self, W_neigh, src, dst):
        import jax, jax.numpy as jnp
        import numpy as np
        N = 6250
        E = 100000
        IN_FEATS = 256
        OUT_FEATS = 256
        MAXK = 32

        def _maxk(x, k):
            _, idx = jax.lax.top_k(x, k)
            rows = jnp.arange(x.shape[0])[:, None]
            mask = jnp.zeros_like(x).at[rows, idx].set(1.0)
            return x * mask
        n = feat.shape[0]
        h_self = feat @ W_self
        h_neigh = feat @ W_neigh
        h_sparse = _maxk(h_neigh, MAXK)
        msg = h_sparse[src]
        summed = jax.ops.segment_sum(msg, dst, num_segments=n)
        deg = jax.ops.segment_sum(jnp.ones((src.shape[0],), dtype=feat.dtype), dst, num_segments=n)
        neigh = summed / jnp.maximum(deg, 1.0)[:, None]
        return h_self + neigh

    def _L2_ffn_ref(x, Wg, bg, W1, b1, W2, b2):
        import jax, jax.numpy as jnp
        import numpy as np
        TOP_K = 2
        B, L, D = x.shape
        E = W1.shape[0]
        xf = x.reshape(-1, D)
        gate_logits = xf @ Wg + bg
        top_w, top_i = jax.lax.top_k(gate_logits, TOP_K)
        top_w = jax.nn.softmax(top_w, axis=-1)
        w_dense = jnp.sum(jax.nn.one_hot(top_i, E, dtype=xf.dtype) * top_w[..., None], axis=1)
        out = jnp.zeros_like(xf)
        for e in range(E):
            h = jax.nn.gelu(xf @ W1[e] + b1[e], approximate=False)
            out = out + w_dense[:, e:e + 1] * (h @ W2[e] + b2[e])
        return out.reshape(B, L, D)

    def _L3_gnn_ref(x, edge_index, W1, a1_src, a1_dst, b1, ln_g, ln_b, W2, a2_src, a2_dst, b2):
        import jax, jax.numpy as jnp
        import numpy as np
        N = 1250
        E = 20000
        D_IN = 256
        HID = 64
        HEADS = 4
        D_OUT = 256
        EPS = 1e-05
        SLOPE = 0.2

        def _gat(x, src, dst, W, a_src, a_dst, b, heads, ch, concat):
            n = x.shape[0]
            h = (x @ W).reshape(n, heads, ch)
            es = (h * a_src).sum(-1)
            ed = (h * a_dst).sum(-1)
            e = jax.nn.leaky_relu(es[src] + ed[dst], SLOPE)
            m = jax.ops.segment_max(e, dst, num_segments=n)
            w = jnp.exp(e - m[dst])
            den = jax.ops.segment_sum(w, dst, num_segments=n)
            alpha = w / den[dst]
            msg = h[src] * alpha[:, :, None]
            out = jax.ops.segment_sum(msg, dst, num_segments=n)
            out = out.reshape(n, heads * ch) if concat else out.mean(axis=1)
            return out + b

        def _layernorm(x, g, b):
            mu = x.mean(-1, keepdims=True)
            v = ((x - mu) ** 2).mean(-1, keepdims=True)
            return (x - mu) * jax.lax.rsqrt(v + EPS) * g + b
        loops = jnp.arange(N, dtype=edge_index.dtype)
        src = jnp.concatenate([edge_index[0], loops])
        dst = jnp.concatenate([edge_index[1], loops])
        h = _gat(x, src, dst, W1, a1_src, a1_dst, b1, HEADS, HID, True)
        h = jax.nn.relu(_layernorm(h, ln_g, ln_b))
        out = _gat(h, src, dst, W2, a2_src, a2_dst, b2, 1, D_OUT, False)
        return out

    def _L3_ffn_ref(x, attention_mask, wr, br, w1, b1, w2, b2):
        import jax, jax.numpy as jnp
        import numpy as np
        B, S, D = (8, 256, 256)
        H = 4 * D
        CAPACITY = 0.5
        b, s, d = x.shape
        weights = (jnp.einsum('bsd,do->bso', x, wr) + br)[..., 0]
        k = max(1, int(CAPACITY * s))
        kk = k - 1 if k > 1 else 1
        _, idx = jax.lax.top_k(weights, k)
        sel_idx = idx[:, :kk]
        sel = jnp.take_along_axis(x, sel_idx[:, :, None], axis=1)
        h = jax.nn.gelu(jnp.einsum('bkd,dh->bkh', sel, w1) + b1)
        y = jnp.einsum('bkh,hd->bkd', h, w2) + b2
        w_sel = jnp.take_along_axis(weights, sel_idx, axis=1)
        y = y * w_sel[..., None]
        batch_idx = jnp.arange(b)[:, None]
        processed = jnp.zeros_like(x).at[batch_idx, sel_idx].set(y)
        return processed + x
    edge_index = jnp.stack([src, dst])
    x = x + _L0_gnn_ref(_layernorm(x, axis=-1), src, dst, edge_type_16, edge_weight1, L0_gnn_w1, L0_gnn_loop_w1, L0_gnn_b1, L0_gnn_w2, L0_gnn_loop_w2, L0_gnn_b2)
    x = x + _L0_ffn_ref(_layernorm(x, axis=-1)[None], L0_ffn_Wr, L0_ffn_br, L0_ffn_W1, L0_ffn_b1, L0_ffn_g1, L0_ffn_be1, L0_ffn_m1, L0_ffn_v1, L0_ffn_W2, L0_ffn_b2, L0_ffn_g2, L0_ffn_be2, L0_ffn_m2, L0_ffn_v2, L0_ffn_Wo, L0_ffn_bo)[0]
    x = x + _L1_gnn_ref(_layernorm(x, axis=-1), edge_index, L1_gnn_W1, L1_gnn_b1, L1_gnn_W2, L1_gnn_att_src, L1_gnn_att_dst, L1_gnn_b2)
    x = x + _L1_ffn_ref(_layernorm(x, axis=-1)[None], L1_ffn_Wr, L1_ffn_br, L1_ffn_W1, L1_ffn_b1, L1_ffn_W2, L1_ffn_b2, L1_ffn_gamma, L1_ffn_beta)[0]
    x = x + _L2_gnn_ref(_layernorm(x, axis=-1), L2_gnn_W_self, L2_gnn_W_neigh, src, dst)
    x = x + _L2_ffn_ref(_layernorm(x, axis=-1)[None], L2_ffn_Wg, L2_ffn_bg, L2_ffn_W1, L2_ffn_b1, L2_ffn_W2, L2_ffn_b2)[0]
    x = x + _L3_gnn_ref(_layernorm(x, axis=-1), edge_index, L3_gnn_W1, L3_gnn_a1_src, L3_gnn_a1_dst, L3_gnn_b1, L3_gnn_ln_g, L3_gnn_ln_b, L3_gnn_W2, L3_gnn_a2_src, L3_gnn_a2_dst, L3_gnn_b2)
    x = x + _L3_ffn_ref(_layernorm(x, axis=-1)[None], L3_ffn_attention_mask, L3_ffn_wr, L3_ffn_br, L3_ffn_w1, L3_ffn_b1, L3_ffn_w2, L3_ffn_b2)[0]
    return x

_drawn_inputs = setup_inputs


def setup_inputs(seed=0):
    import zlib

    import numpy as np

    out = dict(_drawn_inputs(seed))
    spreads = {'L0_gnn_b1': (0.0, 0.1),
     'L0_gnn_b2': (0.0, 0.1),
     'L0_ffn_br': (0.0, 0.274),
     'L0_ffn_b1': (0.0, 0.36),
     'L0_ffn_g1': (1.0, 0.2),
     'L0_ffn_be1': (0.0, 0.354),
     'L0_ffn_m1': (0.0, 0.358),
     'L0_ffn_v1': (1.0, 0.6),
     'L0_ffn_b2': (0.0, 0.1),
     'L0_ffn_g2': (1.0, 0.2),
     'L0_ffn_be2': (0.0, 0.28),
     'L0_ffn_m2': (0.0, 0.1),
     'L0_ffn_v2': (1.0, 0.6),
     'L0_ffn_bo': (0.0, 0.1),
     'L1_gnn_b1': (0.0, 0.1),
     'L1_gnn_b2': (0.0, 0.1),
     'L1_ffn_br': (0.0, 0.1),
     'L1_ffn_b1': (0.0, 0.321),
     'L1_ffn_b2': (0.0, 0.1),
     'L1_ffn_gamma': (1.0, 0.2),
     'L1_ffn_beta': (0.0, 0.1),
     'L2_ffn_bg': (0.0, 0.295),
     'L2_ffn_b1': (0.0, 0.8),
     'L2_ffn_b2': (0.0, 0.272),
     'L3_gnn_b1': (0.0, 0.1),
     'L3_gnn_ln_g': (1.0, 0.2),
     'L3_gnn_ln_b': (0.0, 0.359),
     'L3_gnn_b2': (0.0, 0.1),
     'L3_ffn_b1': (0.0, 0.8),
     'L3_ffn_b2': (0.0, 0.8)}
    factors = {'L1_gnn_att_src': 8.0,
     'L1_gnn_att_dst': 22.714,
     'L3_gnn_a1_dst': 3.933,
     'L3_gnn_a2_dst': 8.0,
     'L3_ffn_wr': 6.138,
     'L3_ffn_w1': 8.0,
     'L3_ffn_w2': 8.0}
    for name, (base, spread) in spreads.items():
        noise = np.random.default_rng([zlib.crc32(name.encode()), seed]).standard_normal(out[name].shape)
        drawn = base * np.exp(spread * noise) if base else spread * noise
        out[name] = jnp.asarray(drawn.astype(out[name].dtype))
    for name, factor in factors.items():
        out[name] = (out[name] * factor).astype(out[name].dtype)
    return out
```

```python
from contextlib import ExitStack

import numpy as np
import concourse.bass as bass
from concourse import mybir

ALU = mybir.AluOpType
ACT = mybir.ActivationFunctionType
AX = mybir.AxisListType.X
F32 = mybir.dt.float32
BF16 = mybir.dt.bfloat16
I32 = mybir.dt.int32
U32 = mybir.dt.uint32

P = 128
D = 256
DC = D // P
N = 3125
NPT = 125
NT = N // NPT
NPAD = NT * P
E = 50000
EC = 392
R = 16
G = 4
KT = 416
NG = KT // G
UN = 5
TW = D + 4
BIG = float(2 ** 100)
MAXK = 32
LN_EPS = 1e-5
assert (E + NT * 127) // P <= KT and NG % 2 == 0 and NT % UN == 0


class Chain:

    def __init__(self, eng, sem):
        self.eng, self.sem, self.n = eng, sem, 0

    def __call__(self, ins):
        ins.then_inc(self.sem, 1)
        self.n += 1
        self.eng.wait_ge(self.sem, self.n)


def hold(eng, sem, count):
    eng.wait_ge(sem, count)
    eng.sem_inc(Net.passed[eng.engine], 1)


def start(eng, *sems):
    for sem in sems:
        eng.sem_inc(sem, 1)


def ahead(eng, sem, count):
    hold(eng, sem, count + 1)


class LoopChain:

    def __init__(self, eng, sem, i, per):
        self.eng, self.sem, self.i, self.per, self.n = eng, sem, i, per, 0

    def __call__(self, ins):
        ins.then_inc(self.sem, 1)
        self.n += 1
        hold(self.eng, self.sem, self.i * self.per + self.n)

    def end(self):
        assert self.n == self.per, f"this loop's body makes {self.n} steps, not {self.per}"


class Phase:

    def __init__(self, nc, tag):
        self.nc, self.tag, self.ctx, self.sems = nc, tag, ExitStack(), []

    def __enter__(self):
        return self

    def __exit__(self, *e):
        self.ctx.close()
        with self.nc.Block() as block:
            @block.sync
            def _(sp):
                for sem in self.sems:
                    sp.sem_clear(sem)

    def sb(self, name, shape, dt=F32):
        return self.ctx.enter_context(self.nc.sbuf_tensor(f"{self.tag}_{name}", shape, dt))

    def sem(self, name):
        self.sems.append(self.ctx.enter_context(self.nc.semaphore(f"{self.tag}_{name}")))
        return self.sems[-1]

    def by_rows(self, name):
        return [Net.ctx.enter_context(self.nc.semaphore(f"{self.tag}_{name}{h}")) for h in range(2)]

    def block(self):
        return self.ctx.enter_context(self.nc.Block())


class Net:

    passed = {}


def floor125(chain, v, q, tmp, qi, x):
    chain(v.tensor_scalar(qi, x, -62.0, 1.0 / NPT, ALU.add, ALU.mult))
    chain(v.tensor_copy(q, qi))
    chain(v.scalar_tensor_tensor(out=tmp, in0=q, scalar=-float(NPT), in1=x, op0=ALU.mult, op1=ALU.add))
    chain(v.scalar_tensor_tensor(out=q, in0=tmp, scalar=float(NPT), in1=q, op0=ALU.is_ge, op1=ALU.add))
    chain(v.tensor_scalar(tmp, tmp, 0.0, -1.0, ALU.is_lt, ALU.mult))
    chain(v.tensor_tensor(q, q, tmp, ALU.add))


def setup(K):
    nc = K.nc
    with Phase(nc, "setup") as ph:
        loaded, iota_done, consts = ph.sem("loaded"), ph.sem("iota_done"), ph.sem("consts")
        zeroed = ph.sem("zeroed")
        irow = ph.sb("irow", [P, P], I32)
        icol = ph.sb("icol", [P, 1], I32)
        block = ph.block()

        @block.gpsimd
        def _(pool):
            pool.iota(irow[:, :], [[1, P]], base=0, channel_multiplier=0).then_inc(iota_done, 1)
            pool.iota(icol[:, :], [[0, 1]], base=0, channel_multiplier=1).then_inc(iota_done, 1)

        @block.vector
        def _(dve):
            dve.memset(K.x[:, :, :], 0.0).then_inc(zeroed, 1)
            dve.wait_ge(iota_done, 2)
            dve.tensor_copy(K.col_f[:, :], icol[:, :]).then_inc(consts, 1)
            dve.tensor_copy(K.row_f[:, :], irow[:, :]).then_inc(consts, 1)
            dve.tensor_copy(K.row_b[:, :], irow[:, :]).then_inc(consts, 1)
            dve.memset(K.ones[:, :], 1.0).then_inc(consts, 1)
            dve.wait_ge(consts, 4)
            dve.tensor_scalar(K.ident[:, :], K.row_f[:, :], K.col_f[:, 0:1], None, ALU.is_equal).then_inc(consts, 1)
            dve.tensor_scalar(K.ident_b[:, :], K.row_f[:, :], K.col_f[:, 0:1], None, ALU.is_equal).then_inc(consts, 1)
            dve.tensor_scalar(K.before[:, :], K.row_f[:, :], K.col_f[:, 0:1], None, ALU.is_gt).then_inc(consts, 1)

        @block.sync
        def _(sp):
            x_rows = K.inp["x"].rearrange("(t p) d -> p t d", p=NPT)
            sp.wait_ge(zeroed, 1)
            sp.dma_start(K.x[0:112, :, :], x_rows[0:112]).then_inc(loaded, 16)
            sp.dma_start(K.x[112:NPT, :, :], x_rows[112:NPT]).then_inc(loaded, 16)
            sp.wait_ge(loaded, 32)


def sort_edges(K):
    nc = K.nc
    U = 14
    with Phase(nc, "sort") as ph:
        loaded, filled, defaults = ph.sem("loaded"), ph.sem("filled"), ph.sem("defaults")
        step, sums, iota_done = ph.sem("step"), ph.sem("sums"), ph.sem("iota_done")
        lstep, lstep2, lstep3 = ph.sem("lstep"), ph.sem("lstep2"), ph.sem("lstep3")
        placed, staged = ph.sem("placed"), ph.sem("staged")
        scattered = ph.by_rows("scattered")
        rec_back, drained = ph.sem("rec_back"), ph.sem("drained")
        dst_i, src_i, et_i, ti = (ph.sb(n, [P, EC], I32) for n in ("dst_i", "src_i", "et_i", "ti"))
        dst, src, bkt, rank, scan, tmp, tmp2, one = (
            ph.sb(n, [P, EC]) for n in ("dst", "src", "bkt", "rank", "scan", "tmp", "tmp2", "one"))
        w = ph.sb("w", [P, EC])
        rec = ph.sb("rec", [P, EC, 4])
        addr = ph.sb("addr", [P, EC], I32)
        ring_rec = ph.sb("ring_rec", [P, 2, U, 4])
        ring_addr = ph.sb("ring_addr", [P, 2, U], I32)
        rowtot = ph.sb("rowtot", [P, 2, NT])
        tiles, ends, offs = ph.sb("tiles", [P, NT]), ph.sb("ends", [P, NT]), ph.sb("offs", [P, NT])
        tiles_i = ph.sb("tiles_i", [P, NT], I32)
        kt_i, kt, dt = ph.sb("kt_i", [P, KT], I32), ph.sb("kt", [P, KT]), ph.sb("dt", [P, KT])
        ecol_i, ecol = ph.sb("ecol_i", [P, EC], I32), ph.sb("ecol", [P, EC])
        bnum_i, bnum = ph.sb("bnum_i", [P, NT], I32), ph.sb("bnum", [P, NT])
        rec_sb = ph.sb("rec_sb", [P, KT, 4])
        block = ph.block()
        tail = E - (P - 1) * EC
        ps_tot = K.ps[:, 0, 0:NT]
        ps_before = K.ps[:, 1, 0:NT]

        @block.sync
        def _(sp):
            sp.wait_ge(filled, 5)
            for name, tile in (("dst", dst_i), ("src", src_i), ("edge_type_16", et_i), ("edge_weight1", w)):
                v = K.inp[name]
                v = v.rearrange("e o -> (e o)") if name == "edge_weight1" else v
                whole = v[0:(P - 1) * EC].rearrange("(p j) -> p j", j=EC)
                last = v[(P - 1) * EC:E].rearrange("(p j) -> p j", p=1)
                sp.dma_start(tile[0:P - 1, :], whole).then_inc(loaded, 16)
                sp.dma_start(tile[P - 1:P, 0:tail], last).then_inc(loaded, 16)
            slots = K.rec_dram[0:KT * P, :].rearrange("(p k) c -> p k c", p=P)
            sp.dma_start(slots, rec_sb[:, :, :]).then_inc(defaults, 16)
            for h in range(2):
                sp.wait_ge(scattered[h], EC // 2 * 16)
            sp.dma_start(rec_sb[:, :, :], slots).then_inc(rec_back, 16)

        @block.gpsimd
        def _(pool):
            pool.iota(kt_i[:, :], [[1, KT]], base=0, channel_multiplier=0).then_inc(iota_done, 1)
            pool.iota(ecol_i[:, :], [[1, EC]], base=0, channel_multiplier=0).then_inc(iota_done, 1)
            pool.iota(bnum_i[:, :], [[1, NT]], base=0, channel_multiplier=0).then_inc(iota_done, 1)
            pool.wait_ge(defaults, 16)
            with pool.Fori(0, EC // (2 * U)) as i:
                for h in range(2):
                    hold(pool, staged, i * 2 + h + 1)
                    for u in range(U):
                        pool.indirect_dma_start(
                            K.rec_dram, bass.IndirectOffsetOnAxis(ring_addr[:, h, u:u + 1], 0),
                            ring_rec[:, h, u, :], None).then_inc(scattered[h], 16)

        @block.scalar
        def _(act):
            act.sem_inc(drained, 2)
            with act.Fori(0, EC // (2 * U)) as i:
                for h in range(2):
                    hold(act, scattered[h], (i + 1) * (U * 16))
                    act.sem_inc(drained, 1)

        @block.tensor
        def _(pe):
            pe.wait_ge(placed, 1)
            pe.matmul(ps_tot, K.ones[:, :], rowtot[:, 0, :], start=True, stop=True).then_inc(sums, 1)
            pe.matmul(ps_before, K.before[:, :], rowtot[:, 0, :], start=True, stop=True).then_inc(sums, 1)

        @block.vector
        def _(dve):
            link = Chain(dve, step)
            dve.memset(dst_i[:, :], N).then_inc(filled, 1)
            dve.memset(src_i[:, :], 0).then_inc(filled, 1)
            dve.memset(et_i[:, :], 0).then_inc(filled, 1)
            dve.memset(w[:, :], 0.0).then_inc(filled, 1)
            link(dve.memset(rec_sb[:, :, :], 0.0))
            dve.memset(rec_sb[:, :, 2:3], -1.0).then_inc(filled, 1)
            link(dve.memset(one[:, :], 1.0))
            link(dve.memset(rank[:, :], 0.0))
            dve.wait_ge(iota_done, 3)
            link(dve.tensor_copy(kt[:, :], kt_i[:, :]))
            link(dve.tensor_copy(ecol[:, :], ecol_i[:, :]))
            link(dve.tensor_copy(bnum[:, :], bnum_i[:, :]))
            dve.wait_ge(loaded, 8 * 16)
            link(dve.tensor_copy(dst[:, :], dst_i[:, :]))
            link(dve.tensor_copy(src[:, :], src_i[:, :]))
            floor125(link, dve, bkt[:, :], tmp[:, :], ti[:, :], dst[:, :])
            floor125(link, dve, tmp2[:, :], tmp[:, :], ti[:, :], src[:, :])
            link(dve.scalar_tensor_tensor(out=rec[:, :, 1], in0=tmp2[:, :], scalar=3.0, in1=src[:, :],
                                          op0=ALU.mult, op1=ALU.add))
            link(dve.tensor_copy(tmp[:, :], et_i[:, :]))
            link(dve.scalar_tensor_tensor(out=rec[:, :, 0], in0=rec[:, :, 1], scalar=float(R), in1=tmp[:, :],
                                          op0=ALU.mult, op1=ALU.add))
            link(dve.scalar_tensor_tensor(out=rec[:, :, 2], in0=bkt[:, :], scalar=-float(NPT), in1=dst[:, :],
                                          op0=ALU.mult, op1=ALU.add))
            link(dve.tensor_copy(rec[:, :, 3], w[:, :]))
            with dve.Fori(0, NT) as b:
                turn = LoopChain(dve, lstep, b, 5)
                turn(dve.tensor_scalar(tmp[:, :], bkt[:, :], bnum[:, bass.ds(b, 1)], None, ALU.is_equal))
                turn(dve.tensor_tensor_scan(scan[:, :], one[:, :], tmp[:, :], 0.0, ALU.mult, ALU.add))
                turn(dve.tensor_copy(rowtot[:, 0, bass.ds(b, 1)], scan[:, EC - 1:EC]))
                turn(dve.tensor_tensor(tmp[:, :], tmp[:, :], scan[:, :], ALU.mult))
                turn(dve.tensor_tensor(rank[:, :], rank[:, :], tmp[:, :], ALU.add))
                turn.end()
            dve.sem_inc(placed, 1)
            dve.wait_ge(sums, 2)
            link(dve.tensor_scalar(tiles_i[:, :], ps_tot, float(P - 1), None, ALU.add))
            link(dve.tensor_scalar(tiles_i[:, :], tiles_i[:, :], 7, None, ALU.logical_shift_right))
            link(dve.tensor_copy(tiles[:, :], tiles_i[:, :]))
            link(dve.tensor_tensor_scan(ends[:, :], one[:, 0:NT], tiles[:, :], 0.0, ALU.mult, ALU.add))
            link(dve.tensor_tensor(offs[:, :], ends[:, :], tiles[:, :], ALU.subtract))
            link(dve.tensor_scalar(offs[:, :], offs[:, :], float(P), -1.0, ALU.mult, ALU.add))
            link(dve.tensor_tensor(offs[:, :], offs[:, :], ps_before, ALU.add))
            with dve.Fori(0, NT) as b:
                turn = LoopChain(dve, lstep2, b, 2)
                turn(dve.tensor_scalar(tmp[:, :], bkt[:, :], bnum[:, bass.ds(b, 1)], offs[:, bass.ds(b, 1)],
                                       ALU.is_equal, ALU.mult))
                turn(dve.tensor_tensor(rank[:, :], rank[:, :], tmp[:, :], ALU.add))
                turn.end()
            link(dve.tensor_copy(ti[:, :], rank[:, :]))
            link(dve.tensor_scalar(ti[:, :], ti[:, :], 7, None, ALU.logical_shift_right))
            link(dve.tensor_copy(tmp[:, :], ti[:, :]))
            link(dve.scalar_tensor_tensor(out=rank[:, :], in0=tmp[:, :], scalar=-float(P), in1=rank[:, :],
                                          op0=ALU.mult, op1=ALU.add))
            link(dve.scalar_tensor_tensor(out=rank[:, :], in0=rank[:, :], scalar=float(KT), in1=tmp[:, :],
                                          op0=ALU.mult, op1=ALU.add))
            link(dve.tensor_scalar(ecol[:, :], ecol[:, :], float(KT * P), None, ALU.add))
            link(dve.scalar_tensor_tensor(out=tmp[:, :], in0=bkt[:, :], scalar=float(NT), in1=ecol[:, :],
                                          op0=ALU.is_equal, op1=ALU.mult))
            link(dve.tensor_tensor(rank[:, :], rank[:, :], tmp[:, :], ALU.add))
            link(dve.tensor_copy(addr[:, :], rank[:, :]))
            with dve.Fori(0, EC // (2 * U)) as i:
                turn = LoopChain(dve, lstep3, i, 2)
                for h in range(2):
                    hold(dve, drained, i * 2 + h + 1)
                    turn(dve.tensor_copy(ring_rec[:, h, :, :], rec[:, bass.ds((i * 2 + h) * U, U), :]))
                    dve.tensor_copy(ring_addr[:, h, :], addr[:, bass.ds((i * 2 + h) * U, U)]).then_inc(staged, 1)
                turn.end()
            link(dve.memset(dt[:, :], 0.0))
            with dve.Fori(0, NT - 1) as b:
                hold(dve, step, link.n + b)
                dve.scalar_tensor_tensor(out=dt[:, :], in0=kt[:, :], scalar=ends[:, bass.ds(b, 1)], in1=dt[:, :],
                                         op0=ALU.is_ge, op1=ALU.add).then_inc(step, 1)
            dve.wait_ge(step, link.n + NT - 1)
            dve.tensor_copy(K.tile_of[:, :], dt[:, :])
            dve.wait_ge(rec_back, 16)
            dve.tensor_copy(K.rel_row[:, :], rec_sb[:, :, 0])
            dve.tensor_copy(K.src_row[:, :], rec_sb[:, :, 1])
            dve.tensor_copy(K.slot_dst[:, :], rec_sb[:, :, 2])
            dve.tensor_copy(K.slot_w[:, :], rec_sb[:, :, 3])


def row_stats(turn, v, stats, mv, xs):
    for u, x in enumerate(xs):
        turn(v.bn_stats(stats[:, u, :], x))
        turn(v.bn_aggr(mv[:, u, :], stats[:, u, :]))


def relation_tables(K, tag, w_name, loop_name, pre, pre_steps, norm, bias_name=None):
    nc = K.nc
    with Phase(nc, tag) as ph:
        loaded, prep, dchain = ph.sem("loaded"), ph.sem("prep"), ph.sem("dchain")
        s_pre, s_tr, s_xt, s_mm = ph.sem("pre"), ph.sem("tr"), ph.sem("xt"), ph.sem("mm")
        ev_act, ev_dve, s_stored = ph.sem("ev_act"), ph.sem("ev_dve"), ph.sem("stored")
        w_rel = ph.sb("w_rel", [P, DC, R, 2])
        diag = ph.sb("diag", [P, DC, R, P])
        pair_i, pair_c, mask = ph.sb("pair_i", [P, P], I32), ph.sb("pair_c", [P, 1], I32), ph.sb("mask", [P, P])
        pair_f, pair_cf = ph.sb("pair_f", [P, P]), ph.sb("pair_cf", [P, 1])
        w_loop = ph.sb("w_loop", [P, DC, D])
        bias = ph.sb("bias", [P, D])
        xin, xt = ph.sb("xin", [P, UN, D]), ph.sb("xt", [P, UN, DC, P])
        stage = ph.sb("stage", [P, UN, R, DC, P])
        stats, mv = ph.sb("stats", [P, UN, 6]), ph.sb("mv", [P, UN, 2])
        s_var, s_rstd, s_free = ph.sem("var"), ph.sem("rstd"), ph.sem("free")
        block = ph.block()

        NQ = 9
        RG = R // 4
        ps_t = [K.ps[:, 0, 0:D], K.ps[:, 1, 0:D]]
        banks = [2, 3, 4, 5]

        @block.sync
        def _(sp):
            w = K.inp[w_name]
            for c in range(DC):
                for i in range(2):
                    pass
            with nc.allow_non_contiguous_dma(reason="small weights by block rows"):
                for c in range(DC):
                    sp.dma_start(w_rel[:, c, :, :], w.rearrange("r (c b) i o -> c (b i) r o", c=DC)[c]).then_inc(loaded, 16)
            sp.dma_start(w_loop[:, :, :], K.inp[loop_name].rearrange("(c p) n -> p c n", p=P)).then_inc(loaded, 16)
            sp.dma_start(bias[:, :], K.inp[bias_name or "L0_gnn_b1"].partition_broadcast(P)).then_inc(loaded, 16)
            with sp.Fori(0, NT // UN) as it:
                for u in range(UN):
                    t = it * UN + u
                    ahead(sp, ev_act, (t + 1) * 4)
                    ahead(sp, ev_dve, (t + 1) * 5)
                    sp.dma_start(K.rel_table[bass.ds(t * P, P), :, :].rearrange("p r f -> p (r f)"),
                                 stage[:, u, :, :, :].rearrange("p r c f -> p (r c f)")).then_inc(s_stored, 16)
            sp.wait_ge(s_stored, NT * 16)

        @block.vector
        def _(dve):
            start(dve, ev_dve)
            link = Chain(dve, prep)
            link(dve.tensor_copy(pair_i[:, :], K.row_f[:, :]))
            link(dve.tensor_scalar(pair_i[:, :], pair_i[:, :], 1, None, ALU.logical_shift_right))
            link(dve.tensor_copy(pair_f[:, :], pair_i[:, :]))
            link(dve.tensor_copy(pair_c[:, :], K.col_f[:, :]))
            link(dve.tensor_scalar(pair_c[:, :], pair_c[:, :], 1, None, ALU.logical_shift_right))
            link(dve.tensor_copy(pair_cf[:, :], pair_c[:, :]))
            link(dve.tensor_scalar(mask[:, :], pair_f[:, :], pair_cf[:, 0:1], None, ALU.is_equal))
            dve.wait_ge(loaded, 64)
            for c in range(DC):
                link(dve.tensor_tensor(
                    diag[:, c, :, :].rearrange("p r (b o) -> p r b o", o=2),
                    w_rel[:, c, :, :].unsqueeze(2).to_broadcast([P, R, P // 2, 2]),
                    mask[:, :].rearrange("p (b o) -> p b o", o=2).unsqueeze(1).to_broadcast([P, R, P // 2, 2]),
                    ALU.mult))
            prep_done = link.n
            with dve.Fori(0, NT // UN) as it:
                turn = LoopChain(dve, dchain, it, pre_steps)
                if norm:
                    row_stats(turn, dve, stats, mv, [K.x[:, it * UN + u, :] for u in range(UN)])
                    dve.tensor_scalar(mv[:, :, 1], mv[:, :, 1], LN_EPS, None, ALU.add).then_inc(s_var, 1)
                    hold(dve, s_rstd, it + 1)
                    turn(dve.reciprocal(mv[:, :, 1], mv[:, :, 1]))
                for u in range(UN):
                    pre(dve, turn, it * UN + u, u, xin[:, u, :], mv, bias).then_inc(s_pre, 1)
                for u in range(UN):
                    t = it * UN + u
                    ahead(dve, s_free, it)
                    for q in (1, 3, 5, 7, 8):
                        ahead(dve, s_mm, t * NQ + q + 1)
                        if q < 8:
                            rg, c = q // 2, q % 2
                            out = stage[:, u, rg * 4:rg * 4 + 4, c, :]
                            ps = K.ps[:, banks[q % 4], :].rearrange("p (r f) -> p r f", r=4)
                        else:
                            out, ps = K.loop_out[:, t, :], K.ps[:, 6, 0:D]
                        dve.tensor_copy(out, ps).then_inc(ev_dve, 1)
                turn.end()

        @block.scalar
        def _(act):
            start(act, s_xt, ev_act)
            with act.Fori(0, NT // UN) as it:
                if norm:
                    hold(act, s_var, it + 1)
                    act.sqrt(mv[:, :, 1], mv[:, :, 1]).then_inc(s_rstd, 1)
                for u in range(UN):
                    t = it * UN + u
                    hold(act, s_tr, t + 1)
                    if u == 0:
                        ahead(act, s_mm, it * (UN * NQ))
                    act.copy(xt[:, u, :, :], ps_t[u % 2].rearrange("p (c f) -> p c f", c=DC)).then_inc(s_xt, 1)
                    if u == 0:
                        ahead(act, s_free, it)
                    for q in (0, 2, 4, 6):
                        ahead(act, s_mm, t * NQ + q + 1)
                        rg, c = q // 2, q % 2
                        act.copy(stage[:, u, rg * 4:rg * 4 + 4, c, :],
                                 K.ps[:, banks[q % 4], :].rearrange("p (r f) -> p r f", r=4)).then_inc(ev_act, 1)

        @block.gpsimd
        def _(pool):
            start(pool, s_free)
            with pool.Fori(0, NT // UN) as it:
                hold(pool, s_stored, (it + 1) * (UN * 16))
                pool.sem_inc(s_free, 1)

        @block.tensor
        def _(pe):
            start(pe, s_mm)
            pe.wait_ge(prep, 7 + DC)
            pe.wait_ge(loaded, 64)
            with pe.Fori(0, NT // UN) as it:
                for u in range(UN):
                    t = it * UN + u
                    hold(pe, s_pre, t + 1)
                    ahead(pe, s_xt, t)
                    for c in range(DC):
                        mm = pe.transpose(ps_t[u % 2][:, c * P:(c + 1) * P], xin[:, u, c * P:(c + 1) * P], K.ident[:, :])
                    mm.then_inc(s_tr, 1)
                    ahead(pe, s_xt, t + 1)
                    for q in range(NQ - 1):
                        rg, c = q // 2, q % 2
                        if q >= 4:
                            ahead(pe, *((ev_act, t * 4 + q // 2 - 1) if q % 2 == 0 else (ev_dve, t * 5 + q // 2 - 1)))
                        else:
                            ahead(pe, *((ev_act, t * 4) if q % 2 == 0 else (ev_dve, t * 5)))
                        pe.matmul(K.ps[:, banks[q % 4], :], xt[:, u, c, :],
                                  diag[:, c, rg * 4:rg * 4 + 4, :].rearrange("p r f -> p (r f)"),
                                  start=True, stop=True).then_inc(s_mm, 1)
                    for c in range(DC):
                        mm = pe.matmul(K.ps[:, 6, 0:D], xt[:, u, c, :], w_loop[:, c, :], start=c == 0, stop=c == DC - 1)
                    mm.then_inc(s_mm, 1)


def edge_sum(K, tag, table, rows, weights, count=False):
    nc = K.nc
    with Phase(nc, tag) as ph:
        zeroed, s_idx, s_hot, s_mm, s_acc = (ph.sem(n) for n in ("zeroed", "idx", "hot", "mm", "acc"))
        s_one = ph.sem("one")
        gathered = ph.by_rows("gathered")
        ring_idx = ph.sb("ring_idx", [P, 2, G], I32)
        rows_in = ph.sb("rows_in", [P, 2, G, D])
        hot = ph.sb("hot", [P, 2, G, P])
        hot_b = ph.sb("hot_b", [P, 2, G, P], BF16)
        one_b = ph.sb("one_b", [P, 1], BF16)
        block = ph.block()
        per = G * (2 if count else 1)

        @block.scalar
        def _(act):
            with act.Fori(0, NG // 2) as it:
                for h in range(2):
                    g = it * 2 + h
                    ahead(act, s_mm, it * (2 * G))
                    act.copy(ring_idx[:, h, :], rows[:, bass.ds(g * G, G)]).then_inc(s_idx, 1)

        @block.gpsimd
        def _(pool):
            if count:
                pool.memset(one_b[:, :], 1.0).then_inc(s_one, 1)
            with pool.Fori(0, NG // 2) as it:
                for h in range(2):
                    g = it * 2 + h
                    hold(pool, s_idx, g + 1)
                    ahead(pool, s_mm, it * (2 * G))
                    for u in range(G):
                        pool.indirect_dma_start(rows_in[:, h, u, :], None, table,
                                                bass.IndirectOffsetOnAxis(ring_idx[:, h, u:u + 1], 0)
                                                ).then_inc(gathered[h], 16)

        def one_hot(dve, g, h, first):
            for u in range(G):
                k = g * G + u
                if weights is None:
                    ins = dve.tensor_scalar(hot[:, h, u, :], K.row_f[:, :], K.slot_dst[:, bass.ds(k, 1)], None, ALU.is_equal)
                else:
                    ins = dve.tensor_scalar(hot[:, h, u, :], K.row_f[:, :], K.slot_dst[:, bass.ds(k, 1)],
                                            weights[:, bass.ds(k, 1)], ALU.is_equal, ALU.mult)
                ins.then_inc(s_hot, 1)
                if count:
                    dve.tensor_scalar(hot_b[:, h, u, :], K.row_b[:, :], K.slot_dst[:, bass.ds(k, 1)], None,
                                      ALU.is_equal).then_inc(s_hot, 1)

        @block.vector
        def _(dve):
            start(dve, s_acc)
            dve.memset(K.acc[:, :, :], 0.0).then_inc(zeroed, 1)
            dve.memset(K.degree[:, :], 0.0).then_inc(zeroed, 1) if count else None
            dve.wait_ge(zeroed, 2 if count else 1)
            with dve.Fori(0, NG // 2) as it:
                for h in range(2):
                    g = it * 2 + h
                    one_hot(dve, g, h, it)
                for h in range(2):
                    g = it * 2 + h
                    tile = [nc.values_load(K.tile_of[0:1, bass.ds(g * G + u, 1)], engines=[dve.engine],
                                           min_val=0, max_val=NT - 1) for u in range(G)]
                    for u in range(G):
                        ahead(dve, s_mm, g * G + u + 1)
                        ahead(dve, s_acc, (g * G + u) * (2 if count else 1))
                        dve.tensor_tensor(K.acc[:, tile[u], 0:D], K.acc[:, tile[u], 0:D], K.ps[:, h * 4 + u, 0:D],
                                          ALU.add).then_inc(s_acc, 1)
                        if count:
                            dve.tensor_tensor(K.degree[:, bass.ds(tile[u], 1)], K.degree[:, bass.ds(tile[u], 1)],
                                              K.ps[:, h * 4 + u, D:D + 1], ALU.add).then_inc(s_acc, 1)

        @block.tensor
        def _(pe):
            start(pe, s_mm)
            if count:
                pe.wait_ge(s_one, 1)
            with pe.Fori(0, NG // 2) as it:
                for h in range(2):
                    g = it * 2 + h
                    hold(pe, gathered[h], (it + 1) * (16 * G))
                    hold(pe, s_hot, (g + 1) * per)
                    for u in range(G):
                        if h == 0 and u == 0:
                            ahead(pe, s_acc, it * (2 * per))
                        mm = pe.matmul(K.ps[:, h * 4 + u, 0:D], hot[:, h, u, :], rows_in[:, h, u, :], start=True, stop=True)
                        if count:
                            mm = pe.matmul(K.ps[:, h * 4 + u, D:D + 1], hot_b[:, h, u, :], one_b[:, :], start=False,
                                           stop=True, skip_group_check=True)
                        mm.then_inc(s_mm, 1)


def node_pass(K, tag, w_names, vectors, pre, pre_steps, norm=None, post=None, post_steps=0, act_post=None,
              table=None, keep_xt=False, keep_xn=False, batch_post=None, batch_steps=0, gate_cols=0, gates_exp=True,
              ones_cols=None):
    nc = K.nc
    wide = D * len(w_names) if w_names and not gate_cols else gate_cols
    with Phase(nc, tag) as ph:
        loaded, s_stored = ph.sem("loaded"), ph.sem("stored")
        dchain, s_var, s_rstd = ph.sem("dchain"), ph.sem("var"), ph.sem("rstd")
        s_pre, s_tr, s_xt, s_mm = ph.sem("pre"), ph.sem("tr"), ph.sem("xt"), ph.sem("mm")
        s_ones = ph.sem("ones")
        s_post, s_apost, s_kept, s_exp = ph.sem("post"), ph.sem("apost"), ph.sem("kept"), ph.sem("exp")
        w_sb = ph.sb("w", [P, DC, max(wide, 1)])
        vec = {n: ph.sb(f"vec_{n}", [P, c]) for n, c in vectors}
        xin, xt = ph.sb("xin", [P, UN, D]), ph.sb("xt", [P, UN, DC, P])
        stats, mv = ph.sb("stats", [P, UN, 6]), ph.sb("mv", [P, UN, 2])
        tools = Net()
        tools.vec, tools.mv, tools.ph, tools.xin = vec, mv, ph, xin
        tools.s_exp, tools.s_sum = s_exp, ph.sem("sum")
        tools.work = ph.sb("work", [P, UN, D])
        tools.work2 = ph.sb("work2", [P, UN, 64])
        tools.small = ph.sb("small", [P, UN, 4])
        block = ph.block()
        n_loads = (len(w_names) + len(vectors)) * 16
        ps_t = [K.ps[:, 0, 0:D], K.ps[:, 1, 0:D]]
        ps_y = [K.ps[:, 2 + u, :] for u in range(UN)]
        has_post, has_act, products = post is not None, act_post is not None, bool(w_names)

        @block.sync
        def _(sp):
            for n, name in enumerate(w_names):
                cols = wide // len(w_names)
                with nc.allow_non_contiguous_dma(reason="a weight vector by partitions"):
                    sp.dma_start(w_sb[:, :, n * cols:(n + 1) * cols],
                                 K.inp[name].rearrange("(c p) n -> p c n", p=P)).then_inc(loaded, 16)
            for name, c in vectors:
                v = K.inp[name]
                v = v.rearrange("h f -> (h f)") if len(v.shape) == 2 else v
                sp.dma_start(vec[name][:, :], v.partition_broadcast(P)).then_inc(loaded, 16)
            if table is not None:
                rows, ready = table
                if ones_cols is not None:
                    sp.wait_ge(s_ones, 1)
                with sp.Fori(0, NT // UN) as it:
                    if has_post:
                        ahead(sp, s_post, (it + 1) * UN)
                    if has_act:
                        ahead(sp, s_apost, (it + 1) * UN)
                    sp.dma_start(rows[bass.ds(it * (UN * P), UN * P), :].rearrange("(t p) f -> p t f", p=P),
                                 ready(it)).then_inc(s_stored, 16)
                sp.wait_ge(s_stored, NT // UN * 16)

        @block.vector
        def _(dve):
            start(dve, s_post)
            if ones_cols is not None:
                dve.memset(ones_cols, 1.0).then_inc(s_ones, 1)
            if n_loads:
                dve.wait_ge(loaded, n_loads)
            with dve.Fori(0, NT // UN) as it:
                turn = LoopChain(dve, dchain, it,
                                 pre_steps * UN + (2 * UN + 1) * (norm is not None) + post_steps * UN + batch_steps)
                if norm is not None:
                    row_stats(turn, dve, stats, mv, [norm(it * UN + u) for u in range(UN)])
                    dve.tensor_scalar(mv[:, :, 1], mv[:, :, 1], LN_EPS, None, ALU.add).then_inc(s_var, 1)
                    hold(dve, s_rstd, it + 1)
                    turn(dve.reciprocal(mv[:, :, 1], mv[:, :, 1]))
                for u in range(UN):
                    if keep_xn and u == 0:
                        ahead(dve, s_kept, it * (UN * 2 if keep_xt else UN))
                    pre(dve, turn, it * UN + u, u, xin[:, u, :], tools).then_inc(s_pre, 1)
                if has_post:
                    ahead(dve, s_post, it * UN)
                    for u in range(UN):
                        ahead(dve, s_mm, it * UN + u + 1)
                        post(dve, turn, it * UN + u, u, ps_y[u], tools).then_inc(s_post, 1)
                if batch_post is not None:
                    ahead(dve, s_mm, it * UN + UN)
                    batch_post(dve, turn, it, K.ps[:, 2:2 + UN, 0:gate_cols], tools).then_inc(s_post, 1)
                turn.end()

        @block.scalar
        def _(act):
            start(act, s_xt, s_apost)
            with act.Fori(0, NT // UN) as it:
                if norm is not None:
                    hold(act, s_var, it + 1)
                    act.sqrt(mv[:, :, 1], mv[:, :, 1]).then_inc(s_rstd, 1)
                for u in range(UN):
                    t = it * UN + u
                    hold(act, s_tr, t + 1)
                    if u == 0:
                        if products:
                            ahead(act, s_mm, it * UN)
                        if keep_xt:
                            ahead(act, s_kept, it * (UN * 2 if keep_xn else UN))
                    act.copy(xt[:, u, :, :], ps_t[u % 2].rearrange("p (c f) -> p c f", c=DC)).then_inc(s_xt, 1)
                if has_act:
                    for u in range(UN):
                        ahead(act, *((s_post, it * UN + u + 1) if has_post else (s_mm, it * UN + u + 1)))
                        act_post(act, it * UN + u, u, ps_y[u], tools).then_inc(s_apost, 1)
                if batch_post is not None and gates_exp:
                    hold(act, tools.s_sum, it + 1)
                    act.activation(tools.work2[:, :, 0:gate_cols], tools.work2[:, :, 0:gate_cols], ACT.Exp).then_inc(s_exp, 1)

        if keep_xt or keep_xn:
            @block.gpsimd
            def _(pool):
                start(pool, s_kept)
                with pool.Fori(0, NT // UN) as it:
                    for u in range(UN):
                        t = it * UN + u
                        if keep_xn:
                            hold(pool, s_pre, t + 1)
                            pool.tensor_copy(K.aux[:, t, :], xin[:, u, :]).then_inc(s_kept, 1)
                        if keep_xt:
                            ahead(pool, s_xt, t + 1)
                            pool.tensor_copy(K.xt[:, :, bass.ds(t * P, P)], xt[:, u, :, :]).then_inc(s_kept, 1)

        @block.tensor
        def _(pe):
            start(pe, s_mm)
            if n_loads:
                pe.wait_ge(loaded, n_loads)
            with pe.Fori(0, NT // UN) as it:
                for u in range(UN + 1):
                    if u < UN:
                        t = it * UN + u
                        hold(pe, s_pre, t + 1)
                        ahead(pe, s_xt, t - 1 if u > 1 else it * UN)
                        for c in range(DC):
                            mm = pe.transpose(ps_t[u % 2][:, c * P:(c + 1) * P], xin[:, u, c * P:(c + 1) * P], K.ident[:, :])
                        mm.then_inc(s_tr, 1)
                    if u > 0 and products:
                        v = u - 1
                        ahead(pe, s_xt, it * UN + v + 1)
                        if v == 0:
                            if has_post:
                                ahead(pe, s_post, it * UN)
                            if has_act:
                                ahead(pe, s_apost, it * UN)
                            if batch_post is not None:
                                ahead(pe, s_post, it)
                        for c in range(DC):
                            mm = pe.matmul(ps_y[v][:, 0:wide], xt[:, v, c, :], w_sb[:, c, :], start=c == 0, stop=c == DC - 1)
                        mm.then_inc(s_mm, 1)


def normed(K):
    def pre(dve, turn, t, u, xin, tools):
        return dve.tensor_scalar(xin, K.x[:, t, :], tools.mv[:, u, 0:1], tools.mv[:, u, 1:2], ALU.subtract, ALU.mult)
    return pre


def softmax_gates(K, bias_name, cols):
    def batch(dve, turn, it, ps, tools):
        logits = tools.work2[:, :, 0:cols]
        top = tools.small[:, :, 0]
        b = tools.vec[bias_name][:, :].unsqueeze(1).to_broadcast([P, UN, cols])
        turn(dve.tensor_tensor(logits, ps, b, ALU.add))
        turn(dve.tensor_reduce(top, logits, AX, ALU.max))
        dve.tensor_tensor(logits, logits, top.unsqueeze(2).to_broadcast([P, UN, cols]), ALU.subtract).then_inc(tools.s_sum, 1)
        hold(dve, tools.s_exp, it + 1)
        turn(dve.tensor_reduce(top, logits, AX, ALU.add))
        turn(dve.reciprocal(top, top))
        return dve.tensor_tensor(K.gate[:, bass.ds(it * UN, UN), :], logits, top.unsqueeze(2).to_broadcast([P, UN, cols]), ALU.mult)
    return batch


def dense_experts(K, tag):
    nc = K.nc
    NE = 8
    CH = UN * P
    HF = CH // 2
    with Phase(nc, tag) as ph:
        consts, prep, turned = ph.sem("consts"), ph.sem("prep"), ph.sem("turned")
        w_in = [ph.sem("w_in0"), ph.sem("w_in1")]
        s_one, s_h1, s_two, s_h2, s_out, s_add = (ph.sem(n) for n in ("one", "h1", "two", "h2", "out", "add"))
        s_gt, s_gc, s_go, s_fin, s_root = (ph.sem(n) for n in ("gt", "gc", "go", "fin", "root"))
        w1, w2, wo = (ph.sb(n, [P, 2, DC, D]) for n in ("w1", "w2", "wo"))
        bo = ph.sb("bo", [NE, D])
        raw = ph.sb("raw", [P, P])
        raw2 = ph.sb("raw2", [32, P])
        cst = ph.sb("cst", [P, 10, NE, DC])
        h1 = ph.sb("h1", [P, 2, DC, HF])
        h2 = ph.sb("h2", [P, DC, CH])
        gate_t, gate_c, s_copied = ph.sb("gate_t", [NE, 2, P]), ph.sb("gate_c", [P, NE]), ph.sem("copied")
        block = ph.block()
        ES = NE * DC
        order = ["b1", "g1", "be1", "m1", "v1", "b2", "g2", "be2", "m2", "v2"]
        B = {n: cst[:, i, :, :] for i, n in enumerate(order)}
        ps_one = [[K.ps[:, 0, 0:HF], K.ps[:, 1, 0:HF]], [K.ps[:, 2, 0:HF], K.ps[:, 3, 0:HF]]]
        ps_two = [[K.ps[:, 4, 0:HF], K.ps[:, 5, 0:HF]], [K.ps[:, 6, 0:HF], K.ps[:, 7, 0:HF]]]
        ps_out = [K.ps[:, 2, 0:D], K.ps[:, 3, 0:D]]
        NCH = NT // UN

        @block.sync
        def _(sp):
            for i, n in enumerate(order):
                rows = K.inp[f"L0_ffn_{n}"].rearrange("e (c p) -> (e c) p", p=P)
                dst = raw[i * ES:(i + 1) * ES, :] if i < 8 else raw2[(i - 8) * ES:(i - 7) * ES, :]
                sp.dma_start(dst, rows).then_inc(consts, 16)
            sp.dma_start(bo[:, :], K.inp["L0_ffn_bo"]).then_inc(consts, 16)
            with sp.Fori(0, NE // 2) as eo:
                for b in range(2):
                    ahead(sp, s_out, eo * (2 * NT) if b == 0 else eo * (2 * NT))
                    for name, w in (("W1", w1), ("W2", w2), ("Wo", wo)):
                        sp.dma_start(w[:, b, :, :], K.inp[f"L0_ffn_{name}"][bass.ds(eo * 2 + b, 1), :, :].rearrange(
                            "a (c p) n -> p (a c) n", p=P)).then_inc(w_in[b], 16)

        @block.vector
        def _(dve):
            start(dve, s_add, s_gc, s_fin)
            link = Chain(dve, prep)
            dve.wait_ge(turned, 2)
            flat = cst[:, :, :, :].rearrange("p a e c -> p (a e c)")
            link(dve.tensor_copy(flat[:, 0:8 * ES], K.ps[:, 0, 0:P]))
            link(dve.tensor_copy(flat[:, 8 * ES:10 * ES], K.ps[:, 1, 0:2 * ES]))
            for g, b, be, m, v in (("g1", "b1", "be1", "m1", "v1"), ("g2", "b2", "be2", "m2", "v2")):
                link(dve.tensor_scalar(B[v], B[v], 1e-3, None, ALU.add))
            dve.wait_ge(s_root, 2)
            for g, b, be, m, v in (("g1", "b1", "be1", "m1", "v1"), ("g2", "b2", "be2", "m2", "v2")):
                link(dve.reciprocal(B[v], B[v]))
                link(dve.tensor_tensor(B[g], B[g], B[v], ALU.mult))
                link(dve.tensor_tensor(B[b], B[b], B[m], ALU.subtract))
                link(dve.tensor_tensor(B[b], B[b], B[g], ALU.mult))
                link(dve.tensor_tensor(B[be], B[be], B[b], ALU.add))
            with dve.Fori(0, NE) as e:
                with dve.Fori(0, NCH) as ch:
                    n = e * NT + ch * UN
                    for u in range(UN):
                        t = ch * UN + u
                        ahead(dve, s_out, n + u + 1)
                        dve.scalar_tensor_tensor(out=K.x[:, t, :], in0=ps_out[u % 2],
                                                 scalar=K.gate[:, t, bass.ds(e, 1)],
                                                 in1=K.x[:, t, :], op0=ALU.mult, op1=ALU.add).then_inc(s_add, 1)
            with dve.Fori(0, NT) as t:
                ahead(dve, s_gt, t + 1)
                dve.tensor_copy(gate_t[:, 0, :], K.ps[0:NE, 0, 0:P]).then_inc(s_gc, 1)
                hold(dve, s_go, t + 1)
                dve.wait_ge(s_add, NE * NT + 1)
                dve.tensor_tensor(K.x[:, t, :], K.x[:, t, :], K.ps[:, 2, 0:D], ALU.add).then_inc(s_fin, 1)

        @block.scalar
        def _(act):
            start(act, s_h1, s_h2)
            act.wait_ge(prep, 4)
            act.sqrt(B["v1"], B["v1"]).then_inc(s_root, 1)
            act.sqrt(B["v2"], B["v2"]).then_inc(s_root, 1)
            act.wait_ge(prep, 14)
            with act.Fori(0, NE) as e:
                with act.Fori(0, NCH) as ch:
                    n = e * (NCH * 4) + ch * 4
                    for h in range(2):
                        for c in range(DC):
                            hold(act, s_one, n + h * 2 + c + 1)
                            ahead(act, s_two, n if h == 0 else n)
                            act.activation(h1[:, h, c, :], ps_one[h][c], ACT.Relu, bias=B["be1"][:, bass.ds(e, 1), c],
                                           scale=B["g1"][:, bass.ds(e, 1), c]).then_inc(s_h1, 1)
                    for h in range(2):
                        for c in range(DC):
                            ahead(act, s_two, n + h * 2 + c + 1)
                            ahead(act, s_out, e * NT + ch * UN)
                            act.activation(h2[:, c, h * HF:(h + 1) * HF], ps_two[h][c], ACT.Relu,
                                           bias=B["be2"][:, bass.ds(e, 1), c],
                                           scale=B["g2"][:, bass.ds(e, 1), c]).then_inc(s_h2, 1)

        @block.tensor
        def _(pe):
            start(pe, s_two, s_out, s_gt)
            pe.wait_ge(consts, 11 * 16)
            pe.transpose(K.ps[:, 0, 0:P], raw[:, :], K.ident[:, :]).then_inc(turned, 1)
            pe.transpose(K.ps[:, 1, 0:32], raw2[:, :], K.ident[0:32, 0:32]).then_inc(turned, 1)
            pe.wait_ge(prep, 2)
            with pe.Fori(0, NE // 2) as eo:
                for b in range(2):
                    hold(pe, w_in[b], (eo + 1) * 48)
                    with pe.Fori(0, NCH) as ch:
                        n = (eo * 2 + b) * (NCH * 4) + ch * 4
                        m = (eo * 2 + b) * NT + ch * UN
                        ahead(pe, s_h1, n)
                        for h in range(2):
                            if h == 1:
                                ahead(pe, s_add, m)
                            for oc in range(DC):
                                for c in range(DC):
                                    mm = pe.matmul(ps_one[h][oc], w1[:, b, c, oc * P:(oc + 1) * P],
                                                   K.xt[:, c, bass.ds(ch * CH + h * HF, HF)], start=c == 0, stop=c == DC - 1)
                                mm.then_inc(s_one, 1)
                        for h in range(2):
                            ahead(pe, s_h1, n + h * 2 + 2)
                            ahead(pe, s_h2, n)
                            for oc in range(DC):
                                for c in range(DC):
                                    mm = pe.matmul(ps_two[h][oc], w2[:, b, c, oc * P:(oc + 1) * P], h1[:, h, c, :],
                                                   start=c == 0, stop=c == DC - 1)
                                mm.then_inc(s_two, 1)
                        for u in range(UN):
                            ahead(pe, s_h2, n + (2 if (u + 1) * P <= HF else 4))
                            if u >= 2:
                                ahead(pe, s_add, m + u - 1)
                            for c in range(DC):
                                mm = pe.matmul(ps_out[u % 2], h2[:, c, u * P:(u + 1) * P], wo[:, b, c, :],
                                               start=c == 0, stop=c == DC - 1)
                            mm.then_inc(s_out, 1)
            pe.wait_ge(s_add, NE * NT + 1)
            with pe.Fori(0, NT) as t:
                ahead(pe, s_gc, t)
                hold(pe, s_copied, t + 1)
                pe.transpose(K.ps[0:NE, 0, 0:P], gate_c[:, :], K.ident[:, :]).then_inc(s_gt, 1)
                ahead(pe, s_gc, t + 1)
                ahead(pe, s_fin, t)
                pe.matmul(K.ps[:, 2, 0:D], gate_t[:, 0, :], bo[:, :], start=True, stop=True).then_inc(s_go, 1)

        @block.gpsimd
        def _(pool):
            with pool.Fori(0, NT) as t:
                ahead(pool, s_gt, t)
                pool.tensor_copy(gate_c[:, :], K.gate[:, t, :]).then_inc(s_copied, 1)


def heads_of(ap, heads):
    f = D // heads
    return ap[:, 0:heads * (f + 1)].rearrange("p (h f) -> p h f", h=heads)


def attention_rows(K, heads, src_name, dst_name):
    f = D // heads

    def act_post(act, t, u, ps, tools):
        return act.copy(heads_of(K.acc[:, t, :], heads)[:, :, 0:f], ps[:, 0:D].rearrange("p (h f) -> p h f", h=heads))

    def post(dve, turn, t, u, ps, tools):
        prod = tools.work[:, u, :].rearrange("p (h f) -> p h f", h=heads)
        turn(dve.tensor_tensor(tools.work[:, u, :], ps[:, 0:D], tools.vec[src_name][:, :], ALU.mult))
        turn(dve.tensor_reduce(heads_of(K.acc[:, t, :], heads)[:, :, f], prod, AX, ALU.add))
        turn(dve.tensor_tensor(tools.work[:, u, :], ps[:, 0:D], tools.vec[dst_name][:, :], ALU.mult))
        return dve.tensor_reduce(K.score_dst[:, t, 0:heads], prod, AX, ALU.add)

    return post, act_post, 3


def attention_sum(K, tag, heads, self_tiles):
    nc = K.nc
    f = D // heads
    W = heads * (f + 1) + (heads == 1)
    SL = 0.2
    with Phase(nc, tag) as ph:
        step, lchain, s_idx, s_mask, s_turn, s_maskt = (ph.sem(n) for n in ("step", "lchain", "idx", "mask", "turn", "maskt"))
        s_top, s_new, s_scale, s_back, s_exp_in, s_exp, s_w, s_out, s_acc = (
            ph.sem(n) for n in ("top", "new", "scale", "back", "exp_in", "exp", "weighted", "out", "acc"))
        s_red = ph.sem("reduced")
        gathered = ph.by_rows("gathered")
        ring_idx = ph.sb("ring_idx", [P, 2, G], I32)
        rows_in = ph.sb("rows_in", [P, 2, G, TW])
        away = ph.sb("away", [P, 2, G, P], BF16)
        hit_t = ph.sb("hit_t", [P, 2, G, P])
        hot = ph.sb("hot", [P, 2, G, P])
        msg = ph.sb("msg", [P, 2, G, TW])
        top_run = ph.sb("top_run", [P, NT, heads])
        top = ph.sb("top", [P, 2, heads, G])
        was, new, pair = (ph.sb(n, [P, 2, G, heads]) for n in ("was", "new", "pair"))
        back = ph.sb("back", [P, 2, G, 2, heads])
        scale = ph.sb("scale", [P, 2, G, heads])
        logit, weight = ph.sb("logit", [P, 2, G, heads]), ph.sb("weight", [P, 2, G, heads])
        block = ph.block()
        ps_turn = K.ps[:, 4, 0:G * P // 2].bitcast(BF16)
        ps_back = K.ps[:, 5, 0:2 * G * 2 * heads].rearrange("p (b g c h) -> p b g c h", b=2, g=G, c=2)
        ps_out = [K.ps[:, 6, 0:W], K.ps[:, 7, 0:W]]

        @block.scalar
        def _(act):
            start(act, s_maskt)
            with act.Fori(0, NG // 2) as it:
                for b in range(2):
                    g = it * 2 + b
                    ahead(act, s_out, it * (2 * G))
                    act.copy(ring_idx[:, b, :], K.src_row[:, bass.ds(g * G, G)]).then_inc(s_idx, 1)
                for b in range(2):
                    g = it * 2 + b
                    hold(act, s_turn, g + 1)
                    ahead(act, s_back, it * 2)
                    act.activation(hit_t[:, b, :, :].rearrange("p g e -> p (g e)"), ps_turn, ACT.Copy,
                                   bias=1.0, scale=1.0 / BIG).then_inc(s_maskt, 1)
                for b in range(2):
                    g = it * 2 + b
                    hold(act, s_new, g + 1)
                    act.activation(scale[:, b, :, :], pair[:, b, :, :], ACT.Exp).then_inc(s_scale, 1)
                    ahead(act, s_exp_in, g + 1)
                    act.activation(weight[:, b, :, :], logit[:, b, :, :], ACT.Exp).then_inc(s_exp, 1)

        @block.gpsimd
        def _(pool):
            with pool.Fori(0, NG // 2) as it:
                for b in range(2):
                    g = it * 2 + b
                    hold(pool, s_idx, g + 1)
                    ahead(pool, s_out, it * (2 * G))
                    for u in range(G):
                        pool.indirect_dma_start(rows_in[:, b, u, :], None, K.att_table,
                                                bass.IndirectOffsetOnAxis(ring_idx[:, b, u:u + 1], 0)
                                                ).then_inc(gathered[b], 16)

        @block.vector
        def _(dve):
            start(dve, s_acc, s_red, s_exp_in)
            link = Chain(dve, step)
            for h in range(heads):
                col = h * (f + 1) + f
                link(dve.tensor_copy(top_run[:, :, h], K.acc[:, :, col]))
                link(dve.memset(K.acc[:, :, col:col + 1], 1.0))
            if self_tiles < NT:
                link(dve.memset(K.acc[:, self_tiles:NT, :], 0.0))
                link(dve.memset(top_run[:, self_tiles:NT, :], -BIG))
            with dve.Fori(0, NG // 2) as it:
                turn = LoopChain(dve, lchain, it, 2 * (G * 4 + 4 + 3) + (2 * G * 1 if heads > 1 else 0))
                for b in range(2):
                    g = it * 2 + b
                    for u in range(G):
                        k = bass.ds(g * G + u, 1)
                        dve.tensor_scalar(away[:, b, u, :], K.row_b[:, :], K.slot_dst[:, k], -BIG,
                                          ALU.not_equal, ALU.mult).then_inc(s_mask, 1)
                for b in range(2):
                    g = it * 2 + b
                    tile = [nc.values_load(K.tile_of[0:1, bass.ds(g * G + u, 1)], engines=[dve.engine],
                                           min_val=0, max_val=NT - 1) for u in range(G)]
                    hold(dve, s_top, g + 1)
                    for h in range(heads):
                        ins = dve.tensor_reduce(top[:, b, h, :], K.ps[:, (b * 2 if heads == 1 else 0) + h, :].rearrange(
                            "p (g e) -> p g e", g=G), AX, ALU.max)
                        ins.then_inc(s_red, 1)
                    ahead(dve, s_red, (g + 1) * heads)
                    for u in range(G):
                        run = top_run[:, tile[u], :]
                        turn(dve.tensor_copy(was[:, b, u, :], run))
                        turn(dve.tensor_tensor(new[:, b, u, :], run, top[:, b, :, u], ALU.max))
                        turn(dve.tensor_copy(run, new[:, b, u, :]))
                        turn(dve.tensor_copy(back[:, b, u, 0, :], K.score_dst[:, tile[u], 0:heads]))
                    mine = back[:, b, :, 0, :]
                    turn(dve.tensor_tensor(new[:, b, :, :], new[:, b, :, :], mine, ALU.add))
                    turn(dve.tensor_tensor(was[:, b, :, :], was[:, b, :, :], mine, ALU.add))
                    turn(dve.scalar_tensor_tensor(out=back[:, b, :, 1, :], in0=new[:, b, :, :], scalar=SL,
                                                  in1=new[:, b, :, :], op0=ALU.mult, op1=ALU.max))
                    turn(dve.scalar_tensor_tensor(out=was[:, b, :, :], in0=was[:, b, :, :], scalar=SL,
                                                  in1=was[:, b, :, :], op0=ALU.mult, op1=ALU.max))
                    dve.tensor_tensor(pair[:, b, :, :], was[:, b, :, :], back[:, b, :, 1, :], ALU.subtract).then_inc(s_new, 1)
                for b in range(2):
                    g = it * 2 + b
                    ahead(dve, s_back, g + 1)
                    mine = rows_in[:, b, :, 0:heads * (f + 1)].rearrange("p g (h f) -> p g h f", h=heads)
                    turn(dve.tensor_tensor(logit[:, b, :, :], mine[:, :, :, f], ps_back[:, b, :, 0, :], ALU.add))
                    turn(dve.scalar_tensor_tensor(out=logit[:, b, :, :], in0=logit[:, b, :, :], scalar=SL,
                                                  in1=logit[:, b, :, :], op0=ALU.mult, op1=ALU.max))
                    turn(dve.tensor_tensor(logit[:, b, :, :], logit[:, b, :, :], ps_back[:, b, :, 1, :], ALU.subtract))
                    dve.tensor_scalar(logit[:, b, :, :], logit[:, b, :, :], 0.0, None, ALU.min).then_inc(s_exp_in, 1)
                for b in range(2):
                    g = it * 2 + b
                    hold(dve, s_exp, g + 1)
                    for u in range(G):
                        k = bass.ds(g * G + u, 1)
                        if heads == 1:
                            dve.tensor_scalar(hot[:, b, u, :], K.row_f[:, :], K.slot_dst[:, k], weight[:, b, u, 0:1],
                                              ALU.is_equal, ALU.mult).then_inc(s_w, 1)
                        else:
                            dve.tensor_scalar(hot[:, b, u, :], K.row_f[:, :], K.slot_dst[:, k], None,
                                              ALU.is_equal).then_inc(s_w, 1)
                            wide = weight[:, b, u, :].unsqueeze(2).to_broadcast([P, heads, f])
                            dve.tensor_tensor(heads_of(msg[:, b, u, :], heads)[:, :, 0:f],
                                              heads_of(rows_in[:, b, u, :], heads)[:, :, 0:f], wide, ALU.mult).then_inc(s_w, 1)
                            dve.tensor_copy(heads_of(msg[:, b, u, :], heads)[:, :, f], weight[:, b, u, :]).then_inc(s_w, 1)
                for b in range(2):
                    g = it * 2 + b
                    tile = [nc.values_load(K.tile_of[0:1, bass.ds(g * G + u, 1)], engines=[dve.engine],
                                           min_val=0, max_val=NT - 1) for u in range(G)]
                    hold(dve, s_scale, g + 1)
                    for u in range(G):
                        ahead(dve, s_out, g * G + u + 1)
                        ahead(dve, s_acc, g * G + u)
                        acc = K.acc[:, tile[u], 0:W]
                        if heads == 1:
                            dve.scalar_tensor_tensor(out=acc, in0=acc, scalar=scale[:, b, u, 0:1], in1=ps_out[u % 2],
                                                     op0=ALU.mult, op1=ALU.add).then_inc(s_acc, 1)
                        else:
                            wide = scale[:, b, u, :].unsqueeze(2).to_broadcast([P, heads, f + 1])
                            a3 = acc.rearrange("p (h f) -> p h f", h=heads)
                            turn(dve.tensor_tensor(a3, a3, wide, ALU.mult))
                            dve.tensor_tensor(acc, acc, ps_out[u % 2], ALU.add).then_inc(s_acc, 1)
                turn.end()

        @block.tensor
        def _(pe):
            start(pe, s_back, s_out)
            with pe.Fori(0, NG // 2) as it:
                for b in range(2):
                    g = it * 2 + b
                    hold(pe, s_mask, (g + 1) * G)
                    ahead(pe, s_maskt, g)
                    for u in range(G):
                        mm = pe.transpose(ps_turn[:, u * P:(u + 1) * P], away[:, b, u, :], K.ident_b[:, :])
                    mm.then_inc(s_turn, 1)
                    hold(pe, gathered[b], (it + 1) * (16 * G))
                    if heads > 1:
                        ahead(pe, s_red, g * heads)
                    else:
                        ahead(pe, s_red, it * 2)
                    for h in range(heads):
                        bank = K.ps[:, (b * 2 if heads == 1 else 0) + h, :]
                        for u in range(G):
                            pe.matmul(bank[:, u * P:(u + 1) * P], away[:, b, u, :], K.ident_b[:, :], start=True, stop=False)
                            col = h * (f + 1) + f
                            mm = pe.matmul(bank[:, u * P:(u + 1) * P],
                                           rows_in[:, b, u, col:col + 1].to_broadcast([P, P]), K.ident[:, :],
                                           start=False, stop=True)
                    mm.then_inc(s_top, 1)
                for b in range(2):
                    g = it * 2 + b
                    ahead(pe, s_maskt, g + 1)
                    hold(pe, s_new, g + 1)
                    ahead(pe, s_exp_in, g)
                    for u in range(G):
                        mm = pe.matmul(ps_back[:, b, u, :, :].rearrange("p c h -> p (c h)"), hit_t[:, b, u, :],
                                       back[:, b, u, :, :].rearrange("p c h -> p (c h)"), start=True, stop=True)
                    mm.then_inc(s_back, 1)
                for b in range(2):
                    g = it * 2 + b
                    hold(pe, s_w, (g + 1) * (G * (1 if heads == 1 else 3)))
                    for u in range(G):
                        ahead(pe, s_acc, g * G + u - 1 if u or b else it * (2 * G))
                        pe.matmul(ps_out[u % 2], hot[:, b, u, :], (rows_in if heads == 1 else msg)[:, b, u, 0:W],
                                  start=True, stop=True).then_inc(s_out, 1)


def attention_out(K, heads, bias, relu):
    f = D // heads

    def emit(dve, turn, t, out, small):
        rows = heads_of(K.acc[:, t, :], heads)
        den = rows[:, :, f] if heads > 1 else K.acc[:, t, D + 1:D + 2]
        turn(dve.tensor_scalar(small[:, 0:heads], den, 0.5, None, ALU.max))
        turn(dve.reciprocal(small[:, 0:heads], small[:, 0:heads]))
        o3 = out.rearrange("p (h f) -> p h f", h=heads)
        turn(dve.tensor_tensor(o3, rows[:, :, 0:f], small[:, 0:heads].unsqueeze(2).to_broadcast([P, heads, f]), ALU.mult))
        ins = dve.tensor_tensor(out, out, bias, ALU.add)
        if relu:
            turn(ins)
            ins = dve.tensor_scalar(out, out, 0.0, None, ALU.max)
        return ins

    return emit, 3 + relu


def add_to_x(K, tag, vectors, emit, steps, to_aux=False):
    nc = K.nc
    with Phase(nc, tag) as ph:
        loaded, chain = ph.sem("loaded"), ph.sem("chain")
        vec = {n: ph.sb(f"vec_{n}", [P, c]) for n, c in vectors}
        work, small = ph.sb("work", [P, UN, D]), ph.sb("small", [P, UN, 4])
        block = ph.block()

        @block.sync
        def _(sp):
            for name, c in vectors:
                sp.dma_start(vec[name][:, :], K.inp[name].partition_broadcast(P)).then_inc(loaded, 16)

        @block.vector
        def _(dve):
            if vectors:
                dve.wait_ge(loaded, 16 * len(vectors))
            with dve.Fori(0, NT // UN) as it:
                turn = LoopChain(dve, chain, it, (steps + 1 + (not to_aux)) * UN)
                for u in range(UN):
                    t = it * UN + u
                    if to_aux:
                        turn(emit(vec)(dve, turn, t, K.aux[:, t, :], small[:, u, :]))
                        continue
                    turn(emit(vec)(dve, turn, t, work[:, u, :], small[:, u, :]))
                    turn(dve.tensor_tensor(K.x[:, t, :], K.x[:, t, :], work[:, u, :], ALU.add))
                turn.end()


def degree_roots(K):
    with Phase(K.nc, "dinv") as ph:
        a, b = ph.sem("a"), ph.sem("b")
        block = ph.block()

        @block.vector
        def _(dve):
            dve.tensor_scalar(K.dinv[:, :], K.degree[:, :], 1.0, None, ALU.add).then_inc(a, 1)
            dve.wait_ge(b, 1)
            dve.reciprocal(K.dinv[:, :], K.dinv[:, :]).then_inc(a, 1)

        @block.scalar
        def _(act):
            act.wait_ge(a, 1)
            act.sqrt(K.dinv[:, :], K.dinv[:, :]).then_inc(b, 1)


def residual(K, tag, bias_name):
    nc = K.nc
    with Phase(nc, tag) as ph:
        loaded, step = ph.sem("loaded"), ph.sem("step")
        bias = ph.sb("bias", [P, D])
        block = ph.block()

        @block.sync
        def _(sp):
            sp.dma_start(bias[:, :], K.inp[bias_name].partition_broadcast(P)).then_inc(loaded, 16)

        @block.vector
        def _(dve):
            link = Chain(dve, step)
            link(dve.tensor_tensor(K.x[:, :, :], K.x[:, :, :], K.acc[:, :, 0:D], ALU.add))
            link(dve.tensor_tensor(K.x[:, :, :], K.x[:, :, :], K.loop_out[:, :, :], ALU.add))
            dve.wait_ge(loaded, 16)
            link(dve.tensor_tensor(K.x[:, :, :], K.x[:, :, :], bias[:, :].unsqueeze(1).to_broadcast([P, NT, D]), ALU.add))


def wide_experts(K, tag, turns, pairs, HC, act, load, target):
    nc = K.nc
    CH = UN * P
    HF = CH // 2
    NCH = NT // UN
    with Phase(nc, tag) as ph:
        w_in = [ph.sem(f"w_in{b}") for b in range(pairs)]
        s_one, s_h, s_out, s_bias, s_add, s_index = (ph.sem(n) for n in ("one", "h", "out", "bias", "add", "index"))
        w1 = ph.sb("w1", [P, pairs, DC, HC * P])
        w2 = ph.sb("w2", [P, pairs, HC, D])
        b1, b2 = ph.sb("b1", [P, pairs, HC]), ph.sb("b2", [P, pairs, D])
        h = ph.sb("h", [P, HC, CH])
        y = ph.sb("y", [P, 2, D])
        block = ph.block()
        ps_one = [K.ps[:, i, 0:HF] for i in range(4)]
        ps_out = [K.ps[:, 4 + i, 0:D] for i in range(2)]

        @block.sync
        def _(sp):
            with sp.Fori(0, turns) as eo:
                for b in range(pairs):
                    ahead(sp, s_add, eo * (pairs * NT))
                    with nc.allow_non_contiguous_dma(reason="biases by partitions"):
                        load(sp, eo, b, w1[:, b, :, :], w2[:, b, :, :], b1[:, b, :], b2[:, b, :], w_in[b])

        @block.vector
        def _(dve):
            start(dve, s_add, s_bias)
            with dve.Fori(0, turns) as eo:
                for b in range(pairs):
                    hold(dve, w_in[b], (eo + 1) * 64)
                    with dve.Fori(0, NCH) as ch:
                        n = (eo * pairs + b) * NT + ch * UN
                        for u in range(UN):
                            t = ch * UN + u
                            ahead(dve, s_out, n + u + 1)
                            ahead(dve, s_add, n + u - 1 if u else n)
                            dve.tensor_tensor(y[:, u % 2, :], ps_out[u % 2], b2[:, b, :], ALU.add).then_inc(s_bias, 1)
                            ahead(dve, s_bias, n + u + 1)
                            dve.scalar_tensor_tensor(out=target[:, t, :], in0=y[:, u % 2, :],
                                                     scalar=K.gate[:, t, bass.ds(eo * pairs + b, 1)],
                                                     in1=target[:, t, :], op0=ALU.mult, op1=ALU.add).then_inc(s_add, 1)

        @block.scalar
        def _(sc):
            with sc.Fori(0, turns) as eo:
                for b in range(pairs):
                    hold(sc, w_in[b], (eo + 1) * 64)
                    with sc.Fori(0, NCH) as ch:
                        n = ((eo * pairs + b) * NCH + ch) * (HC * 2)
                        m = (eo * pairs + b) * NT + ch * UN
                        ahead(sc, s_out, m)
                        for hc in range(HC):
                            for half in range(2):
                                hold(sc, s_one, n + hc * 2 + half + 1)
                                sc.activation(h[:, hc, half * HF:(half + 1) * HF], ps_one[(hc * 2 + half) % 4], act,
                                              bias=b1[:, b, hc:hc + 1]).then_inc(s_h, 1)

        @block.tensor
        def _(pe):
            start(pe, s_out)
            with pe.Fori(0, turns) as eo:
                for b in range(pairs):
                    hold(pe, w_in[b], (eo + 1) * 64)
                    with pe.Fori(0, NCH) as ch:
                        n = ((eo * pairs + b) * NCH + ch) * (HC * 2)
                        m = (eo * pairs + b) * NT + ch * UN
                        for hc in range(HC):
                            for half in range(2):
                                q = hc * 2 + half
                                if q >= 4:
                                    hold(pe, s_h, n + q - 3)
                                for c in range(DC):
                                    mm = pe.matmul(ps_one[q % 4], w1[:, b, c, hc * P:(hc + 1) * P],
                                                   K.xt[:, c, bass.ds(ch * CH + half * HF, HF)], start=c == 0, stop=c == DC - 1)
                                mm.then_inc(s_one, 1)
                        hold(pe, s_h, n + HC * 2)
                        for u in range(UN):
                            ahead(pe, s_bias, m + u - 1 if u > 1 else m)
                            for hc in range(HC):
                                mm = pe.matmul(ps_out[u % 2], h[:, hc, u * P:(u + 1) * P], w2[:, b, hc, :],
                                               start=hc == 0, stop=hc == HC - 1)
                            mm.then_inc(s_out, 1)


def route_two(K, tag):
    nc = K.nc
    NE, CAP = 8, float(-(-N * 5 // (4 * 8)))
    with Phase(nc, tag) as ph:
        loaded, step, s_logits, s_in, s_exp = (ph.sem(n) for n in ("loaded", "step", "logits", "in", "exp"))
        wr, br = ph.sb("wr", [P, DC, NE]), ph.sb("br", [P, NE])
        total = ph.sb("total", [P, DC])
        p, el, best = ph.sb("p", [P, NE]), ph.sb("el", [P, NE]), ph.sb("best", [P, 8])
        one, pair, index = ph.sb("one", [P, 1]), ph.sb("pair", [P, 2]), ph.sb("index", [P, 8], U32)
        s_total = ph.sem("total")
        block = ph.block()

        @block.sync
        def _(sp):
            sp.dma_start(wr[:, :, :], K.inp["L1_ffn_Wr"].rearrange("(c p) e -> p c e", p=P)).then_inc(loaded, 16)
            sp.dma_start(br[:, :], K.inp["L1_ffn_br"].partition_broadcast(P)).then_inc(loaded, 16)

        @block.tensor
        def _(pe):
            pe.wait_ge(loaded, 32)
            pe.wait_ge(s_total, 1)
            for c in range(DC):
                mm = pe.matmul(K.ps[:, 0, 0:NE], total[:, c:c + 1].to_broadcast([P, P]), wr[:, c, :], start=c == 0, stop=c == DC - 1)
            mm.then_inc(s_logits, 1)

        @block.scalar
        def _(sc):
            for i, a in enumerate((p[:, :], p[:, :], pair[:, 1:2])):
                sc.wait_ge(s_in, i + 1)
                sc.activation(a, a, ACT.Exp).then_inc(s_exp, 1)

        @block.vector
        def _(dve):
            link = Chain(dve, step)
            real = K.xt[:, :, :].rearrange("p c (t n) -> p c t n", n=P)[:, :, :, 0:NPT]
            dve.tensor_reduce(total[:, :], real, mybir.AxisListType.XY, ALU.add).then_inc(s_total, 1)
            dve.wait_ge(s_logits, 1)
            link(dve.scalar_tensor_tensor(out=p[:, :], in0=K.ps[:, 0, 0:NE], scalar=1.0 / N, in1=br[:, :], op0=ALU.mult, op1=ALU.add))

            def softmax(i):
                link(dve.tensor_reduce(one[:, :], p[:, :], AX, ALU.max))
                dve.tensor_scalar(p[:, :], p[:, :], one[:, 0:1], None, ALU.subtract).then_inc(s_in, 1)
                dve.wait_ge(s_exp, i)
                link(dve.tensor_reduce(one[:, :], p[:, :], AX, ALU.add))
                link(dve.reciprocal(one[:, :], one[:, :]))
                link(dve.tensor_scalar(p[:, :], p[:, :], one[:, 0:1], None, ALU.mult))

            softmax(1)
            link(dve.tensor_scalar(el[:, :], p[:, :], float(N), CAP, ALU.mult, ALU.max))
            link(dve.reciprocal(el[:, :], el[:, :]))
            link(dve.scalar_tensor_tensor(out=p[:, :], in0=el[:, :], scalar=CAP, in1=p[:, :], op0=ALU.mult, op1=ALU.mult))
            softmax(2)
            link(dve.max(best[:, :], p[:, :]))
            link(dve.max_index(index[:, :], best[:, :], p[:, :]))
            link(dve.tensor_copy(K.pick[:, :], index[:, 0:2]))
            link(dve.memset(pair[:, 0:1], 1.0))
            dve.tensor_tensor(pair[:, 1:2], best[:, 1:2], best[:, 0:1], ALU.subtract).then_inc(s_in, 1)
            dve.wait_ge(s_exp, 3)
            link(dve.tensor_scalar(one[:, :], pair[:, 1:2], 1.0, None, ALU.add))
            link(dve.reciprocal(one[:, :], one[:, :]))
            link(dve.tensor_scalar(pair[:, :], pair[:, :], one[:, 0:1], None, ALU.mult))
            link(dve.tensor_copy(K.gate[:, :, 0:2], pair[:, :].unsqueeze(1).to_broadcast([P, NT, 2])))


def add_normed(K, tag, gamma_name, beta_name):
    nc = K.nc
    with Phase(nc, tag) as ph:
        loaded, chain, s_var, s_rstd = (ph.sem(n) for n in ("loaded", "chain", "var", "rstd"))
        gamma, beta = ph.sb("gamma", [P, D]), ph.sb("beta", [P, D])
        stats, mv = ph.sb("stats", [P, UN, 6]), ph.sb("mv", [P, UN, 2])
        block = ph.block()

        @block.sync
        def _(sp):
            sp.dma_start(gamma[:, :], K.inp[gamma_name].partition_broadcast(P)).then_inc(loaded, 16)
            sp.dma_start(beta[:, :], K.inp[beta_name].partition_broadcast(P)).then_inc(loaded, 16)

        @block.scalar
        def _(sc):
            with sc.Fori(0, NT // UN) as it:
                hold(sc, s_var, it + 1)
                sc.sqrt(mv[:, :, 1], mv[:, :, 1]).then_inc(s_rstd, 1)

        @block.vector
        def _(dve):
            dve.wait_ge(loaded, 32)
            with dve.Fori(0, NT // UN) as it:
                turn = LoopChain(dve, chain, it, 2 * UN + 1 + 4)
                row_stats(turn, dve, stats, mv, [K.aux[:, it * UN + u, :] for u in range(UN)])
                dve.tensor_scalar(mv[:, :, 1], mv[:, :, 1], LN_EPS, None, ALU.add).then_inc(s_var, 1)
                hold(dve, s_rstd, it + 1)
                turn(dve.reciprocal(mv[:, :, 1], mv[:, :, 1]))
                rows = K.aux[:, bass.ds(it * UN, UN), :]
                wide = [P, UN, D]
                turn(dve.tensor_tensor(rows, rows, mv[:, :, 0].unsqueeze(2).to_broadcast(wide), ALU.subtract))
                turn(dve.tensor_tensor(rows, rows, mv[:, :, 1].unsqueeze(2).to_broadcast(wide), ALU.mult))
                turn(dve.tensor_tensor(rows, rows, gamma[:, :].unsqueeze(1).to_broadcast(wide), ALU.mult))
                x_rows = K.x[:, bass.ds(it * UN, UN), :]
                turn(dve.tensor_tensor(x_rows, x_rows, rows, ALU.add))
                turn.end()
            dve.tensor_tensor(K.x[:, :, :], K.x[:, :, :], beta[:, :].unsqueeze(1).to_broadcast([P, NT, D]), ALU.add)


def top_two_gates(K, bias_name, cols):
    def batch(dve, turn, it, ps, tools):
        logits, best, marked = (tools.work2[:, :, i * 8:i * 8 + 8] for i in range(3))
        top = tools.small[:, :, 0]
        wide = [P, UN, cols]
        b = tools.vec[bias_name][:, :].unsqueeze(1).to_broadcast(wide)
        turn(dve.tensor_tensor(logits, ps, b, ALU.add))
        for u in range(UN):
            turn(dve.max(best[:, u, :], logits[:, u, :]))
        turn(dve.tensor_copy(top, best[:, :, 0]))
        turn(dve.memset(best[:, :, 2:8], BIG))
        for u in range(UN):
            turn(dve.match_replace(marked[:, u, :], best[:, u, :], logits[:, u, :], -BIG))
        dve.tensor_tensor(logits, logits, top.unsqueeze(2).to_broadcast(wide), ALU.subtract).then_inc(tools.s_sum, 1)
        hold(dve, tools.s_exp, it + 1)
        turn(dve.scalar_tensor_tensor(out=logits, in0=marked, scalar=-BIG, in1=logits, op0=ALU.is_equal, op1=ALU.mult))
        turn(dve.tensor_reduce(top, logits, AX, ALU.add))
        turn(dve.reciprocal(top, top))
        return dve.tensor_tensor(K.gate[:, bass.ds(it * UN, UN), :], logits, top.unsqueeze(2).to_broadcast(wide), ALU.mult)
    return batch, 6 + 2 * UN


def largest_gates(K, tag, count):
    nc = K.nc
    with Phase(nc, tag) as ph:
        step, lchain, s_row, s_copied, s_diag = (ph.sem(n) for n in ("step", "lchain", "row", "copied", "diag"))
        diag, rows = ph.sb("diag", [P, NT, NPT]), ph.sb("rows", [P, NT, NPT])
        earlier = ph.sb("earlier", [P, 2 * N])
        found, value, rank = ph.sb("found", [P, N]), ph.sb("value", [P, NT]), ph.sb("rank", [P, NT])
        block = ph.block()
        flat, flat_diag = rows[:, :, :].rearrange("p t n -> p (t n)"), diag[:, :, :].rearrange("p t n -> p (t n)")
        cuts = [(c, min(c + 4 * NPT, N)) for c in range(0, N, 4 * NPT)]

        @block.tensor
        def _(pe):
            pe.wait_ge(s_diag, 1)
            for i, (a, b) in enumerate(cuts):
                pe.matmul(K.ps[:, i, 0:b - a], K.ones[:, :], flat_diag[:, a:b], start=True, stop=True).then_inc(s_row, 1)

        @block.scalar
        def _(sc):
            for i, (a, b) in enumerate(cuts):
                sc.wait_ge(s_row, i + 1)
                sc.copy(flat[:, a:b], K.ps[:, i, 0:b - a]).then_inc(s_copied, 1)

        @block.vector
        def _(dve):
            link = Chain(dve, step)
            wide = [P, NT, NPT]
            eye = K.ident[:, 0:NPT].unsqueeze(1).to_broadcast(wide)
            dve.tensor_tensor(diag[:, :, :], eye, K.token_w[:, :].unsqueeze(2).to_broadcast(wide), ALU.mult).then_inc(s_diag, 1)
            link(dve.memset(earlier[:, 0:N], 1.0))
            link(dve.memset(earlier[:, N:2 * N], 0.0))
            link(dve.tensor_scalar(earlier[:, N:N + NPT], K.row_f[:, 0:NPT], K.col_f[:, 0:1], None, ALU.is_lt))
            link(dve.tensor_tensor(K.x[:, :, :], K.x[:, :, :], K.aux[:, :, :], ALU.add))
            dve.wait_ge(s_copied, len(cuts))
            link(dve.tensor_tensor(diag[:, :, :], rows[:, :, :], eye, ALU.mult))
            link(dve.tensor_reduce(value[:, :], diag[:, :, :], AX, ALU.add))
            with dve.Fori(0, NT) as t:
                turn = LoopChain(dve, lchain, t, 3)
                mine = value[:, bass.ds(t, 1)]
                turn(dve.scalar_tensor_tensor(out=found[:, :], in0=flat, scalar=mine, in1=earlier[:, bass.ds(N - t * NPT, N)],
                                              op0=ALU.is_equal, op1=ALU.mult))
                turn(dve.scalar_tensor_tensor(out=found[:, :], in0=flat, scalar=mine, in1=found[:, :],
                                              op0=ALU.is_gt, op1=ALU.add))
                turn(dve.tensor_reduce(rank[:, bass.ds(t, 1)], found[:, :], AX, ALU.add))
                turn.end()
            dve.scalar_tensor_tensor(out=K.gate[:, :, 0], in0=rank[:, :], scalar=float(count), in1=K.token_w[:, :],
                                     op0=ALU.is_lt, op1=ALU.mult)


def store(K, out):
    nc = K.nc
    with Phase(nc, "store") as ph:
        stored = ph.sem("stored")
        block = ph.block()

        @block.sync
        def _(sp):
            rows = out.rearrange("(t p) d -> p t d", p=NPT)
            sp.dma_start(rows[0:112], K.x[0:112, :, :]).then_inc(stored, 16)
            sp.dma_start(rows[112:NPT], K.x[112:NPT, :, :]).then_inc(stored, 16)
            sp.wait_ge(stored, 32)


def build(nc, inp, out, upto=99):
    K = Net()
    K.nc, K.inp = nc, inp
    ctx = ExitStack()
    with ctx:
        def sb(name, shape, dt=F32):
            return ctx.enter_context(nc.sbuf_tensor(name, shape, dt))

        Net.ctx = ctx
        Net.passed = {e.engine: ctx.enter_context(nc.semaphore(f"passed_{name}")) for name, e in (
            ("sp", nc.sync), ("act", nc.scalar), ("pe", nc.tensor), ("dve", nc.vector), ("pool", nc.gpsimd))}
        K.ps = ctx.enter_context(nc.psum_tensor("ps", [P, 8, 512], F32))
        K.x = sb("x_nodes", [P, NT, D])
        K.acc = sb("acc", [P, NT, TW])
        K.loop_out = K.aux = sb("aux", [P, NT, D])
        K.row_f, K.row_b = sb("row_f", [P, P]), sb("row_b", [P, P], BF16)
        K.col_f = sb("col_f", [P, 1])
        K.ident, K.ident_b = sb("ident", [P, P]), sb("ident_b", [P, P], BF16)
        K.before, K.ones = sb("before", [P, P]), sb("ones", [P, P])
        K.tile_of, K.rel_row, K.src_row = (sb(n, [P, KT], I32) for n in ("tile_of", "rel_row", "src_row"))
        K.slot_dst, K.slot_w = sb("slot_dst", [P, KT]), sb("slot_w", [P, KT])
        K.degree = sb("degree", [P, NT])
        K.rec_dram = nc.dram_tensor("rec_dram", [KT * P + EC, 4], F32).ap()
        K.rel_table = nc.dram_tensor("rel_table", [NPAD, R, D], F32).ap()
        K.node_table = nc.dram_tensor("node_table", [NPAD, D], F32).ap()
        K.att_table = nc.dram_tensor("att_table", [NPAD, TW], F32).ap()
        K.dinv = sb("dinv", [P, NT])
        K.score_dst = sb("score_dst", [P, NT, 4])
        rel_rows = K.rel_table.rearrange("n r f -> (n r) f")
        setup(K)
        sort_edges(K)

        def pre_norm(dve, turn, t, u, xin, mv, bias):
            return dve.tensor_scalar(xin, K.x[:, t, :], mv[:, u, 0:1], mv[:, u, 1:2], ALU.subtract, ALU.mult)

        def pre_hidden(dve, turn, t, u, xin, mv, bias):
            turn(dve.tensor_tensor(xin, K.acc[:, t, 0:D], bias[:, :], ALU.add))
            turn(dve.tensor_tensor(xin, xin, K.loop_out[:, t, :], ALU.add))
            return dve.tensor_scalar(xin, xin, 0.0, None, ALU.max)

        relation_tables(K, "rel1", "L0_gnn_w1", "L0_gnn_loop_w1", pre_norm, 2 * UN + 1, True)
        edge_sum(K, "sum1", rel_rows, K.rel_row, K.slot_w, count=True)
        relation_tables(K, "rel2", "L0_gnn_w2", "L0_gnn_loop_w2", pre_hidden, 2 * UN, False)
        edge_sum(K, "sum2", rel_rows, K.rel_row, K.slot_w)
        residual(K, "res0", "L0_gnn_b2")
        if upto >= 1:
            K.xt = sb("xt_nodes", [P, DC, NPAD])
            K.gate = sb("gate", [P, NT, 8])
            node_pass(K, "prep0", ["L0_ffn_Wr"], [("L0_ffn_br", 8)], normed(K), 0, norm=lambda t: K.x[:, t, :],
                      keep_xt=True, batch_post=softmax_gates(K, "L0_ffn_br", 8), batch_steps=4, gate_cols=8)
            dense_experts(K, "experts0")
        if upto >= 2:
            degree_roots(K)

            def scaled(dve, turn, t, u, ps, tools):
                return dve.tensor_scalar(K.aux[:, t, :], ps[:, 0:D], K.dinv[:, bass.ds(t, 1)], None, ALU.mult)

            def aux_rows(it):
                return K.aux[:, bass.ds(it * UN, UN), :]

            def acc_rows(it):
                return K.acc[:, bass.ds(it * UN, UN), :]

            node_pass(K, "gcn", ["L1_gnn_W1"], [], normed(K), 0, norm=lambda t: K.x[:, t, :], post=scaled,
                      table=(K.node_table, aux_rows))
            edge_sum(K, "sum3", K.node_table, K.src_row, None)

            def gcn_out(dve, turn, t, u, xin, tools):
                turn(dve.tensor_tensor(xin, K.acc[:, t, 0:D], K.aux[:, t, :], ALU.add))
                turn(dve.scalar_tensor_tensor(out=xin, in0=xin, scalar=K.dinv[:, bass.ds(t, 1)],
                                              in1=tools.vec["L1_gnn_b1"][:, :], op0=ALU.mult, op1=ALU.add))
                return dve.tensor_scalar(xin, xin, 0.0, None, ALU.max)

            post, act_post, n = attention_rows(K, 1, "L1_gnn_att_src", "L1_gnn_att_dst")
            node_pass(K, "gat1", ["L1_gnn_W2"], [("L1_gnn_b1", D), ("L1_gnn_att_src", D), ("L1_gnn_att_dst", D)],
                      gcn_out, 2, post=post, post_steps=n, act_post=act_post, table=(K.att_table, acc_rows),
                      ones_cols=K.acc[:, :, D + 1:TW])
            attention_sum(K, "att1", 1, NT)
            out1 = lambda vec: attention_out(K, 1, vec["L1_gnn_b2"][:, :], True)[0]
            add_to_x(K, "res1", [("L1_gnn_b2", D)], out1, 4)
        if upto >= 3:
            K.pick = sb("pick", [P, 2], I32)
            node_pass(K, "prep1", [], [], normed(K), 0, norm=lambda t: K.x[:, t, :], keep_xt=True, keep_xn=True)
            route_two(K, "route1")

            def load_picked(sp, eo, b, w1, w2, b1, b2, sem):
                e = nc.values_load(K.pick[0:1, b:b + 1], engines=[sp.engine], min_val=0, max_val=7)[0] if False else \
                    nc.values_load(K.pick[0:1, b:b + 1], engines=[sp.engine], min_val=0, max_val=7)
                one = bass.ds(e, 1)
                sp.dma_start(w1, K.inp["L1_ffn_W1"][one, :, :].rearrange("a (c p) n -> p (a c) n", p=P)).then_inc(sem, 16)
                sp.dma_start(w2, K.inp["L1_ffn_W2"][one, :, :].rearrange("a (c p) n -> p (a c) n", p=P)).then_inc(sem, 16)
                sp.dma_start(b1, K.inp["L1_ffn_b1"][one, :].rearrange("a (c p) -> p (a c)", p=P)).then_inc(sem, 16)
                sp.dma_start(b2, K.inp["L1_ffn_b2"][one, :].to_broadcast([P, D])).then_inc(sem, 16)

            wide_experts(K, "ffn1", 1, 2, 4, ACT.Gelu, load_picked, K.aux)
            add_normed(K, "res1b", "L1_ffn_gamma", "L1_ffn_beta")
        if upto >= 4:
            def max_k(dve, turn, t, u, ps, tools):
                h, best = tools.work[:, u, :], tools.work2[:, u, 0:8]
                turn(dve.tensor_tensor(K.x[:, t, :], K.x[:, t, :], ps[:, D:2 * D], ALU.add))
                turn(dve.tensor_copy(h, ps[:, 0:D]))
                for _ in range(MAXK // 8):
                    turn(dve.max(best, h))
                    turn(dve.match_replace(h, best, h, -BIG))
                return dve.scalar_tensor_tensor(out=K.aux[:, t, :], in0=h, scalar=-BIG, in1=ps[:, 0:D],
                                                op0=ALU.is_equal, op1=ALU.mult)

            def mean(dve, turn, t, out, small):
                turn(dve.tensor_scalar(small[:, 0:1], K.degree[:, bass.ds(t, 1)], 1.0, None, ALU.max))
                turn(dve.reciprocal(small[:, 0:1], small[:, 0:1]))
                return dve.tensor_scalar(out, K.acc[:, t, 0:D], small[:, 0:1], None, ALU.mult)

            node_pass(K, "sage", ["L2_gnn_W_neigh", "L2_gnn_W_self"], [], normed(K), 0, norm=lambda t: K.x[:, t, :],
                      post=max_k, post_steps=2 + MAXK // 4, table=(K.node_table, aux_rows))
            edge_sum(K, "sum4", K.node_table, K.src_row, None)
            add_to_x(K, "res2", [], lambda vec: mean, 2)
        if upto >= 5:
            def load_expert(sp, eo, b, w1, w2, b1, b2, sem):
                one = bass.ds(eo * 2 + b, 1)
                sp.dma_start(w1, K.inp["L2_ffn_W1"][one, :, :].rearrange("a (c p) n -> p (a c) n", p=P)).then_inc(sem, 16)
                sp.dma_start(w2, K.inp["L2_ffn_W2"][one, :, :].rearrange("a (c p) n -> p (a c) n", p=P)).then_inc(sem, 16)
                sp.dma_start(b1, K.inp["L2_ffn_b1"][one, :].rearrange("a (c p) -> p (a c)", p=P)).then_inc(sem, 16)
                sp.dma_start(b2, K.inp["L2_ffn_b2"][one, :].to_broadcast([P, D])).then_inc(sem, 16)

            gates, n = top_two_gates(K, "L2_ffn_bg", 8)
            node_pass(K, "prep2", ["L2_ffn_Wg"], [("L2_ffn_bg", 8)], normed(K), 0, norm=lambda t: K.x[:, t, :],
                      keep_xt=True, batch_post=gates, batch_steps=n, gate_cols=8)
            wide_experts(K, "ffn2", 4, 2, 8, ACT.Gelu, load_expert, K.x)
        if upto >= 6:
            LOOPED = 1250 // NPT
            post, act_post, n = attention_rows(K, 4, "L3_gnn_a1_src", "L3_gnn_a1_dst")
            node_pass(K, "gat2", ["L3_gnn_W1"], [("L3_gnn_a1_src", D), ("L3_gnn_a1_dst", D)], normed(K), 0,
                      norm=lambda t: K.x[:, t, :], post=post, post_steps=n, act_post=act_post, table=(K.att_table, acc_rows))
            attention_sum(K, "att2", 4, LOOPED)
            out2 = lambda vec: attention_out(K, 4, vec["L3_gnn_b1"][:, :], False)[0]
            add_to_x(K, "mid", [("L3_gnn_b1", D)], out2, 3, to_aux=True)

            def mid_norm(dve, turn, t, u, xin, tools):
                turn(dve.tensor_scalar(xin, K.aux[:, t, :], tools.mv[:, u, 0:1], tools.mv[:, u, 1:2], ALU.subtract, ALU.mult))
                turn(dve.tensor_tensor(xin, xin, tools.vec["L3_gnn_ln_g"][:, :], ALU.mult))
                turn(dve.tensor_tensor(xin, xin, tools.vec["L3_gnn_ln_b"][:, :], ALU.add))
                return dve.tensor_scalar(xin, xin, 0.0, None, ALU.max)

            post, act_post, n = attention_rows(K, 1, "L3_gnn_a2_src", "L3_gnn_a2_dst")
            node_pass(K, "gat3", ["L3_gnn_W2"], [(f"L3_gnn_{v}", D) for v in ("ln_g", "ln_b", "a2_src", "a2_dst")],
                      mid_norm, 3, norm=lambda t: K.aux[:, t, :], post=post, post_steps=n, act_post=act_post,
                      table=(K.att_table, acc_rows), ones_cols=K.acc[:, :, D + 1:TW])
            attention_sum(K, "att3", 1, LOOPED)
            out3 = lambda vec: attention_out(K, 1, vec["L3_gnn_b2"][:, :], False)[0]
            add_to_x(K, "res3", [("L3_gnn_b2", D)], out3, 3)
        if upto >= 7:
            K.token_w = sb("token_w", [P, NT])

            def token_weights(dve, turn, it, ps, tools):
                return dve.tensor_tensor(K.token_w[:, bass.ds(it * UN, UN)], ps[:, :, 0],
                                         tools.vec["L3_ffn_br"][:, :].to_broadcast([P, UN]), ALU.add)

            def load_only(sp, eo, b, w1, w2, b1, b2, sem):
                sp.dma_start(w1, K.inp["L3_ffn_w1"].rearrange("(c p) n -> p c n", p=P)).then_inc(sem, 16)
                sp.dma_start(w2, K.inp["L3_ffn_w2"].rearrange("(c p) n -> p c n", p=P)).then_inc(sem, 16)
                sp.dma_start(b1, K.inp["L3_ffn_b1"].rearrange("(c p) -> p c", p=P)).then_inc(sem, 16)
                sp.dma_start(b2, K.inp["L3_ffn_b2"].partition_broadcast(P)).then_inc(sem, 16)

            node_pass(K, "prep3", ["L3_ffn_wr"], [("L3_ffn_br", 1)], normed(K), 0, norm=lambda t: K.x[:, t, :],
                      keep_xt=True, keep_xn=True, batch_post=token_weights, gate_cols=1, gates_exp=False)
            largest_gates(K, "pick", N // 2 - 1)
            wide_experts(K, "ffn3", 1, 1, 8, ACT.Gelu_apprx_tanh, load_only, K.x)
        store(K, out)




def kernel(**inputs):
    import numpy as _np
    import concourse.bacc as _bacc
    from concourse import mybir as _mybir
    from concourse.bass_utils import run_bass_kernel_spmd as _run

    nc = _bacc.Bacc("TRN2", target_bir_lowering=False, num_devices=1)
    arrays, inp = {}, {}
    for name, value in inputs.items():
        if name == "L3_ffn_attention_mask":
            continue
        a = _np.ascontiguousarray(value)
        arrays[f"in_{name}"] = a
        inp[name] = nc.dram_tensor(f"in_{name}", list(a.shape), _mybir.dt.from_np(a.dtype), kind="ExternalInput").ap()
    out = nc.dram_tensor("out_0", [N, D], F32, kind="ExternalOutput").ap()
    build(nc, inp, out)
    r = _run(nc, [arrays], core_ids=[0])
    return r.results[0]["out_0"]
```

```python
from contextlib import ExitStack

import numpy as np
import concourse.bass as bass
from concourse import mybir

ALU = mybir.AluOpType
ACT = mybir.ActivationFunctionType
AX = mybir.AxisListType.X
F32 = mybir.dt.float32
BF16 = mybir.dt.bfloat16
I32 = mybir.dt.int32
U32 = mybir.dt.uint32

P = 128
D = 256
DC = D // P
N = 3125
NPT = 125
NT = N // NPT
NPAD = NT * P
E = 50000
EC = 392
R = 16
G = 4
PAIR = 2
KT = 440
NG = KT // G
RING = 5
UN = 5
TW = D + 4
BIG = float(2 ** 100)
MAXK = 32
LN_EPS = 1e-5
assert (E + NT * (PAIR * P - 1)) // (PAIR * P) * PAIR <= KT and NG % RING == 0 and NT % UN == 0


class Chain:

    def __init__(self, eng, sem):
        self.eng, self.sem, self.n = eng, sem, 0

    def __call__(self, ins):
        ins.then_inc(self.sem, 1)
        self.n += 1
        self.eng.wait_ge(self.sem, self.n)


def hold(eng, sem, count):
    eng.wait_ge(sem, count)
    eng.sem_inc(Net.passed[eng.engine], 1)


def start(eng, *sems):
    for sem in sems:
        eng.sem_inc(sem, 1)


def ahead(eng, sem, count):
    hold(eng, sem, count + 1)


class LoopChain:

    def __init__(self, eng, sem, i, per):
        self.eng, self.sem, self.i, self.per, self.n = eng, sem, i, per, 0

    def __call__(self, ins):
        ins.then_inc(self.sem, 1)
        self.n += 1
        hold(self.eng, self.sem, self.i * self.per + self.n)

    def end(self):
        assert self.n == self.per, f"this loop's body makes {self.n} steps, not {self.per}"


class Phase:

    def __init__(self, nc, tag):
        self.nc, self.tag, self.ctx, self.sems = nc, tag, ExitStack(), []

    def __enter__(self):
        return self

    def __exit__(self, *e):
        self.ctx.close()
        with self.nc.Block() as block:
            @block.sync
            def _(sp):
                for sem in self.sems:
                    sp.sem_clear(sem)

    def sb(self, name, shape, dt=F32):
        return self.ctx.enter_context(self.nc.sbuf_tensor(f"{self.tag}_{name}", shape, dt))

    def sem(self, name):
        self.sems.append(self.ctx.enter_context(self.nc.semaphore(f"{self.tag}_{name}")))
        return self.sems[-1]

    def by_rows(self, name, n):
        return [Net.ctx.enter_context(self.nc.semaphore(f"{self.tag}_{name}{h}")) for h in range(n)]

    def block(self):
        return self.ctx.enter_context(self.nc.Block())


class Net:

    passed = {}


def floor125(chain, v, q, tmp, qi, x):
    chain(v.tensor_scalar(qi, x, -62.0, 1.0 / NPT, ALU.add, ALU.mult))
    chain(v.tensor_copy(q, qi))
    chain(v.scalar_tensor_tensor(out=tmp, in0=q, scalar=-float(NPT), in1=x, op0=ALU.mult, op1=ALU.add))
    chain(v.scalar_tensor_tensor(out=q, in0=tmp, scalar=float(NPT), in1=q, op0=ALU.is_ge, op1=ALU.add))
    chain(v.tensor_scalar(tmp, tmp, 0.0, -1.0, ALU.is_lt, ALU.mult))
    chain(v.tensor_tensor(q, q, tmp, ALU.add))


def setup(K):
    nc = K.nc
    with Phase(nc, "setup") as ph:
        loaded, iota_done, consts = ph.sem("loaded"), ph.sem("iota_done"), ph.sem("consts")
        zeroed = ph.sem("zeroed")
        irow = ph.sb("irow", [P, P], I32)
        icol = ph.sb("icol", [P, 1], I32)
        block = ph.block()

        @block.gpsimd
        def _(pool):
            pool.iota(irow[:, :], [[1, P]], base=0, channel_multiplier=0).then_inc(iota_done, 1)
            pool.iota(icol[:, :], [[0, 1]], base=0, channel_multiplier=1).then_inc(iota_done, 1)

        @block.vector
        def _(dve):
            dve.memset(K.x[:, :, :], 0.0).then_inc(zeroed, 1)
            dve.wait_ge(iota_done, 2)
            dve.tensor_copy(K.col_f[:, :], icol[:, :]).then_inc(consts, 1)
            dve.tensor_copy(K.row_f[:, :], irow[:, :]).then_inc(consts, 1)
            dve.tensor_copy(K.row_b[:, :], irow[:, :]).then_inc(consts, 1)
            dve.memset(K.ones[:, :], 1.0).then_inc(consts, 1)
            dve.wait_ge(consts, 4)
            dve.tensor_scalar(K.ident[:, :], K.row_f[:, :], K.col_f[:, 0:1], None, ALU.is_equal).then_inc(consts, 1)
            dve.tensor_scalar(K.ident_b[:, :], K.row_f[:, :], K.col_f[:, 0:1], None, ALU.is_equal).then_inc(consts, 1)
            dve.tensor_scalar(K.before[:, :], K.row_f[:, :], K.col_f[:, 0:1], None, ALU.is_gt).then_inc(consts, 1)

        @block.sync
        def _(sp):
            x_rows = K.inp["x"].rearrange("(t p) d -> p t d", p=NPT)
            sp.wait_ge(zeroed, 1)
            sp.dma_start(K.x[0:112, :, :], x_rows[0:112]).then_inc(loaded, 16)
            sp.dma_start(K.x[112:NPT, :, :], x_rows[112:NPT]).then_inc(loaded, 16)
            sp.wait_ge(loaded, 32)


def sort_edges(K):
    nc = K.nc
    U = 14
    with Phase(nc, "sort") as ph:
        loaded, filled, defaults = ph.sem("loaded"), ph.sem("filled"), ph.sem("defaults")
        step, sums, iota_done = ph.sem("step"), ph.sem("sums"), ph.sem("iota_done")
        lstep, lstep2, lstep3 = ph.sem("lstep"), ph.sem("lstep2"), ph.sem("lstep3")
        placed, staged = ph.sem("placed"), ph.sem("staged")
        scattered = ph.by_rows("scattered", 2)
        rec_back, drained = ph.sem("rec_back"), ph.sem("drained")
        dst_i, src_i, et_i, ti = (ph.sb(n, [P, EC], I32) for n in ("dst_i", "src_i", "et_i", "ti"))
        dst, src, bkt, rank, scan, tmp, tmp2, one = (
            ph.sb(n, [P, EC]) for n in ("dst", "src", "bkt", "rank", "scan", "tmp", "tmp2", "one"))
        w = ph.sb("w", [P, EC])
        rec = ph.sb("rec", [P, EC, 4])
        addr = ph.sb("addr", [P, EC], I32)
        ring_rec = ph.sb("ring_rec", [P, 2, U, 4])
        ring_addr = ph.sb("ring_addr", [P, 2, U], I32)
        rowtot = ph.sb("rowtot", [P, 2, NT])
        tiles, ends, offs = ph.sb("tiles", [P, NT]), ph.sb("ends", [P, NT]), ph.sb("offs", [P, NT])
        tiles_i = ph.sb("tiles_i", [P, NT], I32)
        kt_i, kt, dt = ph.sb("kt_i", [P, KT], I32), ph.sb("kt", [P, KT]), ph.sb("dt", [P, KT])
        ecol_i, ecol = ph.sb("ecol_i", [P, EC], I32), ph.sb("ecol", [P, EC])
        bnum_i, bnum = ph.sb("bnum_i", [P, NT], I32), ph.sb("bnum", [P, NT])
        rec_sb = ph.sb("rec_sb", [P, KT, 4])
        block = ph.block()
        tail = E - (P - 1) * EC
        ps_tot = K.ps[:, 0, 0:NT]
        ps_before = K.ps[:, 1, 0:NT]

        @block.sync
        def _(sp):
            sp.wait_ge(filled, 5)
            for name, tile in (("dst", dst_i), ("src", src_i), ("edge_type_16", et_i), ("edge_weight1", w)):
                v = K.inp[name]
                v = v.rearrange("e o -> (e o)") if name == "edge_weight1" else v
                whole = v[0:(P - 1) * EC].rearrange("(p j) -> p j", j=EC)
                last = v[(P - 1) * EC:E].rearrange("(p j) -> p j", p=1)
                sp.dma_start(tile[0:P - 1, :], whole).then_inc(loaded, 16)
                sp.dma_start(tile[P - 1:P, 0:tail], last).then_inc(loaded, 16)
            slots = K.rec_dram[0:KT * P, :].rearrange("(p k) c -> p k c", p=P)
            sp.dma_start(slots, rec_sb[:, :, :]).then_inc(defaults, 16)
            for h in range(2):
                sp.wait_ge(scattered[h], EC // 2 * 16)
            sp.dma_start(rec_sb[:, :, :], slots).then_inc(rec_back, 16)

        @block.gpsimd
        def _(pool):
            pool.iota(kt_i[:, :], [[1, KT]], base=0, channel_multiplier=0).then_inc(iota_done, 1)
            pool.iota(ecol_i[:, :], [[1, EC]], base=0, channel_multiplier=0).then_inc(iota_done, 1)
            pool.iota(bnum_i[:, :], [[1, NT]], base=0, channel_multiplier=0).then_inc(iota_done, 1)
            pool.wait_ge(defaults, 16)
            with pool.Fori(0, EC // (2 * U)) as i:
                for h in range(2):
                    hold(pool, staged, i * 2 + h + 1)
                    for u in range(U):
                        pool.indirect_dma_start(
                            K.rec_dram, bass.IndirectOffsetOnAxis(ring_addr[:, h, u:u + 1], 0),
                            ring_rec[:, h, u, :], None).then_inc(scattered[h], 16)

        @block.scalar
        def _(act):
            act.sem_inc(drained, 2)
            with act.Fori(0, EC // (2 * U)) as i:
                for h in range(2):
                    hold(act, scattered[h], (i + 1) * (U * 16))
                    act.sem_inc(drained, 1)

        @block.tensor
        def _(pe):
            pe.wait_ge(placed, 1)
            pe.matmul(ps_tot, K.ones[:, :], rowtot[:, 0, :], start=True, stop=True).then_inc(sums, 1)
            pe.matmul(ps_before, K.before[:, :], rowtot[:, 0, :], start=True, stop=True).then_inc(sums, 1)

        @block.vector
        def _(dve):
            link = Chain(dve, step)
            dve.memset(dst_i[:, :], N).then_inc(filled, 1)
            dve.memset(src_i[:, :], 0).then_inc(filled, 1)
            dve.memset(et_i[:, :], 0).then_inc(filled, 1)
            dve.memset(w[:, :], 0.0).then_inc(filled, 1)
            link(dve.memset(rec_sb[:, :, :], 0.0))
            dve.memset(rec_sb[:, :, 2:3], -1.0).then_inc(filled, 1)
            link(dve.memset(one[:, :], 1.0))
            link(dve.memset(rank[:, :], 0.0))
            dve.wait_ge(iota_done, 3)
            link(dve.tensor_copy(kt[:, :], kt_i[:, :]))
            link(dve.tensor_copy(ecol[:, :], ecol_i[:, :]))
            link(dve.tensor_copy(bnum[:, :], bnum_i[:, :]))
            dve.wait_ge(loaded, 8 * 16)
            link(dve.tensor_copy(dst[:, :], dst_i[:, :]))
            link(dve.tensor_copy(src[:, :], src_i[:, :]))
            floor125(link, dve, bkt[:, :], tmp[:, :], ti[:, :], dst[:, :])
            floor125(link, dve, tmp2[:, :], tmp[:, :], ti[:, :], src[:, :])
            link(dve.scalar_tensor_tensor(out=rec[:, :, 1], in0=tmp2[:, :], scalar=3.0, in1=src[:, :],
                                          op0=ALU.mult, op1=ALU.add))
            link(dve.tensor_copy(tmp[:, :], et_i[:, :]))
            link(dve.scalar_tensor_tensor(out=rec[:, :, 0], in0=rec[:, :, 1], scalar=float(R), in1=tmp[:, :],
                                          op0=ALU.mult, op1=ALU.add))
            link(dve.scalar_tensor_tensor(out=rec[:, :, 2], in0=bkt[:, :], scalar=-float(NPT), in1=dst[:, :],
                                          op0=ALU.mult, op1=ALU.add))
            link(dve.tensor_copy(rec[:, :, 3], w[:, :]))
            with dve.Fori(0, NT) as b:
                turn = LoopChain(dve, lstep, b, 5)
                turn(dve.tensor_scalar(tmp[:, :], bkt[:, :], bnum[:, bass.ds(b, 1)], None, ALU.is_equal))
                turn(dve.tensor_tensor_scan(scan[:, :], one[:, :], tmp[:, :], 0.0, ALU.mult, ALU.add))
                turn(dve.tensor_copy(rowtot[:, 0, bass.ds(b, 1)], scan[:, EC - 1:EC]))
                turn(dve.tensor_tensor(tmp[:, :], tmp[:, :], scan[:, :], ALU.mult))
                turn(dve.tensor_tensor(rank[:, :], rank[:, :], tmp[:, :], ALU.add))
                turn.end()
            dve.sem_inc(placed, 1)
            dve.wait_ge(sums, 2)
            link(dve.tensor_scalar(tiles_i[:, :], ps_tot, float(PAIR * P - 1), None, ALU.add))
            link(dve.tensor_scalar(tiles_i[:, :], tiles_i[:, :], 8, None, ALU.logical_shift_right))
            link(dve.tensor_scalar(tiles[:, :], tiles_i[:, :], float(PAIR), None, ALU.mult))
            link(dve.tensor_tensor_scan(ends[:, :], one[:, 0:NT], tiles[:, :], 0.0, ALU.mult, ALU.add))
            link(dve.tensor_tensor(offs[:, :], ends[:, :], tiles[:, :], ALU.subtract))
            link(dve.tensor_scalar(offs[:, :], offs[:, :], float(P), -1.0, ALU.mult, ALU.add))
            link(dve.tensor_tensor(offs[:, :], offs[:, :], ps_before, ALU.add))
            with dve.Fori(0, NT) as b:
                turn = LoopChain(dve, lstep2, b, 2)
                turn(dve.tensor_scalar(tmp[:, :], bkt[:, :], bnum[:, bass.ds(b, 1)], offs[:, bass.ds(b, 1)],
                                       ALU.is_equal, ALU.mult))
                turn(dve.tensor_tensor(rank[:, :], rank[:, :], tmp[:, :], ALU.add))
                turn.end()
            link(dve.tensor_copy(ti[:, :], rank[:, :]))
            link(dve.tensor_scalar(ti[:, :], ti[:, :], 7, None, ALU.logical_shift_right))
            link(dve.tensor_copy(tmp[:, :], ti[:, :]))
            link(dve.scalar_tensor_tensor(out=rank[:, :], in0=tmp[:, :], scalar=-float(P), in1=rank[:, :],
                                          op0=ALU.mult, op1=ALU.add))
            link(dve.scalar_tensor_tensor(out=rank[:, :], in0=rank[:, :], scalar=float(KT), in1=tmp[:, :],
                                          op0=ALU.mult, op1=ALU.add))
            link(dve.tensor_scalar(ecol[:, :], ecol[:, :], float(KT * P), None, ALU.add))
            link(dve.scalar_tensor_tensor(out=tmp[:, :], in0=bkt[:, :], scalar=float(NT), in1=ecol[:, :],
                                          op0=ALU.is_equal, op1=ALU.mult))
            link(dve.tensor_tensor(rank[:, :], rank[:, :], tmp[:, :], ALU.add))
            link(dve.tensor_copy(addr[:, :], rank[:, :]))
            with dve.Fori(0, EC // (2 * U)) as i:
                turn = LoopChain(dve, lstep3, i, 2)
                for h in range(2):
                    hold(dve, drained, i * 2 + h + 1)
                    turn(dve.tensor_copy(ring_rec[:, h, :, :], rec[:, bass.ds((i * 2 + h) * U, U), :]))
                    dve.tensor_copy(ring_addr[:, h, :], addr[:, bass.ds((i * 2 + h) * U, U)]).then_inc(staged, 1)
                turn.end()
            link(dve.memset(dt[:, :], 0.0))
            with dve.Fori(0, NT - 1) as b:
                hold(dve, step, link.n + b)
                dve.scalar_tensor_tensor(out=dt[:, :], in0=kt[:, :], scalar=ends[:, bass.ds(b, 1)], in1=dt[:, :],
                                         op0=ALU.is_ge, op1=ALU.add).then_inc(step, 1)
            dve.wait_ge(step, link.n + NT - 1)
            dve.tensor_copy(K.tile_of[:, :], dt[:, :])
            dve.wait_ge(rec_back, 16)
            dve.tensor_copy(K.rel_row[:, :], rec_sb[:, :, 0])
            dve.tensor_copy(K.src_row[:, :], rec_sb[:, :, 1])
            dve.tensor_copy(K.slot_dst[:, :], rec_sb[:, :, 2])
            dve.tensor_copy(K.slot_w[:, :], rec_sb[:, :, 3])


def edge_rows(K):
    nc = K.nc
    CB = KT // 4
    with Phase(nc, "edge_rows") as ph:
        step, turned, copied, stored = (ph.sem(n) for n in ("step", "turned", "copied", "stored"))
        whole, src_p = ph.sb("whole", [P, KT], I32), ph.sb("src_p", [P, KT])
        out = ph.sb("out", [CB, 2, 4, P], BF16)
        block = ph.block()

        @block.vector
        def _(dve):
            link = Chain(dve, step)
            link(dve.tensor_scalar(whole[:, :], K.src_row[:, :], 7, None, ALU.logical_shift_right))
            link(dve.tensor_copy(K.src_tile[:, :], whole[:, :]))
            link(dve.tensor_copy(src_p[:, :], K.src_row[:, :]))
            link(dve.scalar_tensor_tensor(out=src_p[:, :], in0=K.src_tile[:, :], scalar=-float(P), in1=src_p[:, :],
                                          op0=ALU.mult, op1=ALU.add))
            link(dve.tensor_copy(K.tile_f[:, :], K.tile_of[:, :]))
            for i in range(2):
                for c in range(4):
                    dve.wait_ge(turned, i * 4 + c + 1)
                    dve.tensor_copy(out[:, i, c, :], K.ps[0:CB, i * 4 + c, 0:P]).then_inc(copied, 1)

        @block.tensor
        def _(pe):
            pe.wait_ge(step, 4)
            for i, rows in enumerate((src_p, K.slot_dst)):
                for c in range(4):
                    pe.transpose(K.ps[0:CB, i * 4 + c, 0:P], rows[:, c * CB:(c + 1) * CB], K.ident[:, :]).then_inc(turned, 1)

        @block.sync
        def _(sp):
            sp.wait_ge(copied, 8)
            for i in range(2):
                sp.dma_start(K.pair_rows[i].rearrange("(c k) e -> k c e", k=CB), out[:, i, :, :]).then_inc(stored, 16)
            sp.wait_ge(stored, 32)


def row_stats(turn, v, stats, mv, xs):
    for u, x in enumerate(xs):
        turn(v.bn_stats(stats[:, u, :], x))
        turn(v.bn_aggr(mv[:, u, :], stats[:, u, :]))


def relation_tables(K, tag, w_name, loop_name, pre, pre_steps, norm, bias_name=None):
    nc = K.nc
    with Phase(nc, tag) as ph:
        loaded, prep, dchain = ph.sem("loaded"), ph.sem("prep"), ph.sem("dchain")
        s_pre, s_tr, s_xt, s_mm = ph.sem("pre"), ph.sem("tr"), ph.sem("xt"), ph.sem("mm")
        ev_act, ev_dve, s_stored = ph.sem("ev_act"), ph.sem("ev_dve"), ph.sem("stored")
        w_rel = ph.sb("w_rel", [P, DC, R, 2])
        diag = ph.sb("diag", [P, DC, R, P])
        pair_i, pair_c, mask = ph.sb("pair_i", [P, P], I32), ph.sb("pair_c", [P, 1], I32), ph.sb("mask", [P, P])
        pair_f, pair_cf = ph.sb("pair_f", [P, P]), ph.sb("pair_cf", [P, 1])
        w_loop = ph.sb("w_loop", [P, DC, D])
        bias = ph.sb("bias", [P, D])
        xin, xt = ph.sb("xin", [P, UN, D]), ph.sb("xt", [P, UN, DC, P])
        stage = ph.sb("stage", [P, UN, R, DC, P])
        stats, mv = ph.sb("stats", [P, UN, 6]), ph.sb("mv", [P, UN, 2])
        s_var, s_rstd, s_free = ph.sem("var"), ph.sem("rstd"), ph.sem("free")
        block = ph.block()

        NQ = 9
        RG = R // 4
        ps_t = [K.ps[:, 0, 0:D], K.ps[:, 1, 0:D]]
        banks = [2, 3, 4, 5]

        @block.sync
        def _(sp):
            w = K.inp[w_name]
            for c in range(DC):
                for i in range(2):
                    pass
            with nc.allow_non_contiguous_dma(reason="small weights by block rows"):
                for c in range(DC):
                    sp.dma_start(w_rel[:, c, :, :], w.rearrange("r (c b) i o -> c (b i) r o", c=DC)[c]).then_inc(loaded, 16)
            sp.dma_start(w_loop[:, :, :], K.inp[loop_name].rearrange("(c p) n -> p c n", p=P)).then_inc(loaded, 16)
            sp.dma_start(bias[:, :], K.inp[bias_name or "L0_gnn_b1"].partition_broadcast(P)).then_inc(loaded, 16)
            with sp.Fori(0, NT // UN) as it:
                for u in range(UN):
                    t = it * UN + u
                    ahead(sp, ev_act, (t + 1) * 4)
                    ahead(sp, ev_dve, (t + 1) * 5)
                    sp.dma_start(K.rel_table[bass.ds(t * P, P), :, :].rearrange("p r f -> p (r f)"),
                                 stage[:, u, :, :, :].rearrange("p r c f -> p (r c f)")).then_inc(s_stored, 16)
            sp.wait_ge(s_stored, NT * 16)

        @block.vector
        def _(dve):
            start(dve, ev_dve)
            link = Chain(dve, prep)
            link(dve.tensor_copy(pair_i[:, :], K.row_f[:, :]))
            link(dve.tensor_scalar(pair_i[:, :], pair_i[:, :], 1, None, ALU.logical_shift_right))
            link(dve.tensor_copy(pair_f[:, :], pair_i[:, :]))
            link(dve.tensor_copy(pair_c[:, :], K.col_f[:, :]))
            link(dve.tensor_scalar(pair_c[:, :], pair_c[:, :], 1, None, ALU.logical_shift_right))
            link(dve.tensor_copy(pair_cf[:, :], pair_c[:, :]))
            link(dve.tensor_scalar(mask[:, :], pair_f[:, :], pair_cf[:, 0:1], None, ALU.is_equal))
            dve.wait_ge(loaded, 64)
            for c in range(DC):
                link(dve.tensor_tensor(
                    diag[:, c, :, :].rearrange("p r (b o) -> p r b o", o=2),
                    w_rel[:, c, :, :].unsqueeze(2).to_broadcast([P, R, P // 2, 2]),
                    mask[:, :].rearrange("p (b o) -> p b o", o=2).unsqueeze(1).to_broadcast([P, R, P // 2, 2]),
                    ALU.mult))
            prep_done = link.n
            with dve.Fori(0, NT // UN) as it:
                turn = LoopChain(dve, dchain, it, pre_steps)
                if norm:
                    row_stats(turn, dve, stats, mv, [K.x[:, it * UN + u, :] for u in range(UN)])
                    dve.tensor_scalar(mv[:, :, 1], mv[:, :, 1], LN_EPS, None, ALU.add).then_inc(s_var, 1)
                    hold(dve, s_rstd, it + 1)
                    turn(dve.reciprocal(mv[:, :, 1], mv[:, :, 1]))
                for u in range(UN):
                    pre(dve, turn, it * UN + u, u, xin[:, u, :], mv, bias).then_inc(s_pre, 1)
                for u in range(UN):
                    t = it * UN + u
                    ahead(dve, s_free, it)
                    for q in (1, 3, 5, 7, 8):
                        ahead(dve, s_mm, t * NQ + q + 1)
                        if q < 8:
                            rg, c = q // 2, q % 2
                            out = stage[:, u, rg * 4:rg * 4 + 4, c, :]
                            ps = K.ps[:, banks[q % 4], :].rearrange("p (r f) -> p r f", r=4)
                        else:
                            out, ps = K.loop_out[:, t, :], K.ps[:, 6, 0:D]
                        dve.tensor_copy(out, ps).then_inc(ev_dve, 1)
                turn.end()

        @block.scalar
        def _(act):
            start(act, s_xt, ev_act)
            with act.Fori(0, NT // UN) as it:
                if norm:
                    hold(act, s_var, it + 1)
                    act.sqrt(mv[:, :, 1], mv[:, :, 1]).then_inc(s_rstd, 1)
                for u in range(UN):
                    t = it * UN + u
                    hold(act, s_tr, t + 1)
                    if u == 0:
                        ahead(act, s_mm, it * (UN * NQ))
                    act.copy(xt[:, u, :, :], ps_t[u % 2].rearrange("p (c f) -> p c f", c=DC)).then_inc(s_xt, 1)
                    if u == 0:
                        ahead(act, s_free, it)
                    for q in (0, 2, 4, 6):
                        ahead(act, s_mm, t * NQ + q + 1)
                        rg, c = q // 2, q % 2
                        act.copy(stage[:, u, rg * 4:rg * 4 + 4, c, :],
                                 K.ps[:, banks[q % 4], :].rearrange("p (r f) -> p r f", r=4)).then_inc(ev_act, 1)

        @block.gpsimd
        def _(pool):
            start(pool, s_free)
            with pool.Fori(0, NT // UN) as it:
                hold(pool, s_stored, (it + 1) * (UN * 16))
                pool.sem_inc(s_free, 1)

        @block.tensor
        def _(pe):
            start(pe, s_mm)
            pe.wait_ge(prep, 7 + DC)
            pe.wait_ge(loaded, 64)
            with pe.Fori(0, NT // UN) as it:
                for u in range(UN):
                    t = it * UN + u
                    hold(pe, s_pre, t + 1)
                    ahead(pe, s_xt, t)
                    for c in range(DC):
                        mm = pe.transpose(ps_t[u % 2][:, c * P:(c + 1) * P], xin[:, u, c * P:(c + 1) * P], K.ident[:, :])
                    mm.then_inc(s_tr, 1)
                    ahead(pe, s_xt, t + 1)
                    for q in range(NQ - 1):
                        rg, c = q // 2, q % 2
                        if q >= 4:
                            ahead(pe, *((ev_act, t * 4 + q // 2 - 1) if q % 2 == 0 else (ev_dve, t * 5 + q // 2 - 1)))
                        else:
                            ahead(pe, *((ev_act, t * 4) if q % 2 == 0 else (ev_dve, t * 5)))
                        pe.matmul(K.ps[:, banks[q % 4], :], xt[:, u, c, :],
                                  diag[:, c, rg * 4:rg * 4 + 4, :].rearrange("p r f -> p (r f)"),
                                  start=True, stop=True).then_inc(s_mm, 1)
                    for c in range(DC):
                        mm = pe.matmul(K.ps[:, 6, 0:D], xt[:, u, c, :], w_loop[:, c, :], start=c == 0, stop=c == DC - 1)
                    mm.then_inc(s_mm, 1)


def edge_sum(K, tag, table, rows, weights, count=False, heads=0):
    nc = K.nc
    SLOTS = RING * G
    GP = G // PAIR
    BANKS = RING
    W = heads * (D // heads + 1) if heads else D
    TCOLS = TW if heads else D
    with Phase(nc, tag) as ph:
        zeroed, s_idx, s_hot, s_mm, s_acc = (ph.sem(n) for n in ("zeroed", "idx", "hot", "mm", "acc"))
        s_one, s_deg = ph.sem("one"), ph.sem("deg")
        gathered = ph.by_rows("gathered", RING)
        ring_idx = ph.sb("ring_idx", [P, RING, G], I32)
        rows_in = ph.sb("rows_in", [P, RING, G, TCOLS])
        hot = ph.sb("hot", [P, RING, G, P])
        hot_b, one_b = ph.sb("hot_b", [P, RING, G, P], BF16), ph.sb("one_b", [P, 1], BF16)
        msg = ph.sb("msg", [P, RING, G, W]) if heads > 1 else rows_in
        block = ph.block()
        per = 2 if count or heads > 1 else 1

        @block.scalar
        def _(act):
            with act.Fori(0, NG // RING) as it:
                for b in range(RING):
                    g = it * RING + b
                    hold(act, s_mm, (g + 1) * G)
                    act.copy(ring_idx[:, b, :], rows[:, bass.ds(g * G, G)]).then_inc(s_idx, 1)

        @block.gpsimd
        def _(pool):
            if count:
                pool.memset(one_b[:, :], 1.0).then_inc(s_one, 1)
            with pool.Fori(0, NG // RING) as it:
                for b in range(RING):
                    g = it * RING + b
                    hold(pool, s_idx, g + 1)
                    hold(pool, s_mm, (g + 1) * G)
                    for u in range(G):
                        pool.indirect_dma_start(rows_in[:, b, u, :], None, table,
                                                bass.IndirectOffsetOnAxis(ring_idx[:, b, u:u + 1], 0)
                                                ).then_inc(gathered[b], 16)

        def one_hot(dve, it, b):
            g = it * RING + b
            hold(dve, s_mm, (g + 1) * G)
            if heads > 1:
                hold(dve, gathered[b], (it + 1) * (16 * G))
            for u in range(G):
                k = g * G + u
                dst = K.slot_dst[:, bass.ds(k, 1)]
                if weights is None or heads > 1:
                    ins = dve.tensor_scalar(hot[:, b, u, :], K.row_f[:, :], dst, None, ALU.is_equal)
                else:
                    w = weights[:, bass.ds(k, 1), 0] if heads else weights[:, bass.ds(k, 1)]
                    ins = dve.tensor_scalar(hot[:, b, u, :], K.row_f[:, :], dst, w, ALU.is_equal, ALU.mult)
                ins.then_inc(s_hot, 1)
                if heads > 1:
                    wide = weights[:, bass.ds(k, 1), :].rearrange("p a h -> p (a h)").unsqueeze(2).to_broadcast([P, heads, W // heads])
                    dve.tensor_tensor(heads_of(msg[:, b, u, :], heads), heads_of(rows_in[:, b, u, :], heads), wide,
                                      ALU.mult).then_inc(s_hot, 1)
                if count:
                    dve.tensor_scalar(hot_b[:, b, u, :], K.row_b[:, :], dst, None, ALU.is_equal).then_inc(s_hot, 1)

        def add(dve, it, b):
            g = it * RING + b
            for q in range(GP):
                n = g * GP + q
                bank = (b * GP + q) % BANKS
                tile = nc.values_load(K.tile_of[0:1, bass.ds(g * G + q * PAIR, 1)], engines=[dve.engine], min_val=0,
                                      max_val=NT - 1, skip_runtime_bounds_check_because="it counts NT - 1 comparisons")
                hold(dve, s_mm, n * PAIR + PAIR + SLOTS)
                hold(dve, s_acc, n + BANKS)
                dve.tensor_tensor(K.acc[:, tile, 0:W], K.acc[:, tile, 0:W], K.ps[:, bank, 0:W], ALU.add).then_inc(s_acc, 1)
                if count:
                    hold(dve, s_deg, n + BANKS)
                    dve.tensor_tensor(K.degree[:, bass.ds(tile, 1)], K.degree[:, bass.ds(tile, 1)],
                                      K.ps[:, bank, D:D + 1], ALU.add).then_inc(s_deg, 1)

        @block.vector
        def _(dve):
            dve.sem_inc(s_acc, BANKS)
            dve.sem_inc(s_deg, BANKS)
            if not heads:
                dve.memset(K.acc[:, :, :], 0.0).then_inc(zeroed, 1)
                if count:
                    dve.memset(K.degree[:, :], 0.0).then_inc(zeroed, 1)
                dve.wait_ge(zeroed, 2 if count else 1)
            with dve.Fori(0, NG // RING) as it:
                if heads > 1:
                    for b in range(RING):
                        one_hot(dve, it, b)
                        add(dve, it, b)
                else:
                    for b in range(RING):
                        one_hot(dve, it, b)
                    for b in range(RING):
                        add(dve, it, b)

        @block.tensor
        def _(pe):
            pe.sem_inc(s_mm, SLOTS)
            if count:
                pe.wait_ge(s_one, 1)
            with pe.Fori(0, NG // RING) as it:
                for b in range(RING):
                    g = it * RING + b
                    hold(pe, gathered[b], (it + 1) * (16 * G))
                    hold(pe, s_hot, (g + 1) * (G * per))
                    for q in range(GP):
                        n = g * GP + q
                        bank = (b * GP + q) % BANKS
                        hold(pe, s_acc, n + 1)
                        if count:
                            hold(pe, s_deg, n + 1)
                        for i in range(PAIR):
                            u = q * PAIR + i
                            mm = pe.matmul(K.ps[:, bank, 0:W], hot[:, b, u, :], msg[:, b, u, 0:W],
                                           start=i == 0, stop=i == PAIR - 1)
                            if not count:
                                mm.then_inc(s_mm, 1)
                        for i in range(PAIR if count else 0):
                            u = q * PAIR + i
                            pe.matmul(K.ps[:, bank, D:D + 1], hot_b[:, b, u, :], one_b[:, :], start=i == 0,
                                      stop=i == PAIR - 1, skip_group_check=True).then_inc(s_mm, 1)


def node_pass(K, tag, w_names, vectors, pre, pre_steps, norm=None, post=None, post_steps=0, act_post=None,
              table=None, keep_xt=False, keep_xn=False, batch_post=None, batch_steps=0, gate_cols=0, gates_exp=True,
              ones_cols=None):
    nc = K.nc
    wide = D * len(w_names) if w_names and not gate_cols else gate_cols
    with Phase(nc, tag) as ph:
        loaded, s_stored = ph.sem("loaded"), ph.sem("stored")
        dchain, s_var, s_rstd = ph.sem("dchain"), ph.sem("var"), ph.sem("rstd")
        s_pre, s_tr, s_xt, s_mm = ph.sem("pre"), ph.sem("tr"), ph.sem("xt"), ph.sem("mm")
        s_ones = ph.sem("ones")
        s_post, s_apost, s_kept, s_exp = ph.sem("post"), ph.sem("apost"), ph.sem("kept"), ph.sem("exp")
        w_sb = ph.sb("w", [P, DC, max(wide, 1)])
        vec = {n: ph.sb(f"vec_{n}", [P, c]) for n, c in vectors}
        xin, xt = ph.sb("xin", [P, UN, D]), ph.sb("xt", [P, UN, DC, P])
        stats, mv = ph.sb("stats", [P, UN, 6]), ph.sb("mv", [P, UN, 2])
        tools = Net()
        tools.vec, tools.mv, tools.ph, tools.xin = vec, mv, ph, xin
        tools.s_exp, tools.s_sum = s_exp, ph.sem("sum")
        tools.work = ph.sb("work", [P, UN, D])
        tools.work2 = ph.sb("work2", [P, UN, 64])
        tools.small = ph.sb("small", [P, UN, 4])
        block = ph.block()
        n_loads = (len(w_names) + len(vectors)) * 16
        ps_t = [K.ps[:, 0, 0:D], K.ps[:, 1, 0:D]]
        ps_y = [K.ps[:, 2 + u, :] for u in range(UN)]
        has_post, has_act, products = post is not None, act_post is not None, bool(w_names)

        @block.sync
        def _(sp):
            for n, name in enumerate(w_names):
                cols = wide // len(w_names)
                with nc.allow_non_contiguous_dma(reason="a weight vector by partitions"):
                    sp.dma_start(w_sb[:, :, n * cols:(n + 1) * cols],
                                 K.inp[name].rearrange("(c p) n -> p c n", p=P)).then_inc(loaded, 16)
            for name, c in vectors:
                v = K.inp[name]
                v = v.rearrange("h f -> (h f)") if len(v.shape) == 2 else v
                sp.dma_start(vec[name][:, :], v.partition_broadcast(P)).then_inc(loaded, 16)
            if table is not None:
                rows, ready = table
                if ones_cols is not None:
                    sp.wait_ge(s_ones, 1)
                with sp.Fori(0, NT // UN) as it:
                    if has_post:
                        ahead(sp, s_post, (it + 1) * UN)
                    if has_act:
                        ahead(sp, s_apost, (it + 1) * UN)
                    sp.dma_start(rows[bass.ds(it * (UN * P), UN * P), :].rearrange("(t p) f -> p t f", p=P),
                                 ready(it)).then_inc(s_stored, 16)
                sp.wait_ge(s_stored, NT // UN * 16)

        @block.vector
        def _(dve):
            start(dve, s_post)
            if ones_cols is not None:
                dve.memset(ones_cols, 1.0).then_inc(s_ones, 1)
            if n_loads:
                dve.wait_ge(loaded, n_loads)
            with dve.Fori(0, NT // UN) as it:
                turn = LoopChain(dve, dchain, it,
                                 pre_steps * UN + (2 * UN + 1) * (norm is not None) + post_steps * UN + batch_steps)
                if norm is not None:
                    row_stats(turn, dve, stats, mv, [norm(it * UN + u) for u in range(UN)])
                    dve.tensor_scalar(mv[:, :, 1], mv[:, :, 1], LN_EPS, None, ALU.add).then_inc(s_var, 1)
                    hold(dve, s_rstd, it + 1)
                    turn(dve.reciprocal(mv[:, :, 1], mv[:, :, 1]))
                for u in range(UN):
                    if keep_xn and u == 0:
                        ahead(dve, s_kept, it * (UN * 2 if keep_xt else UN))
                    pre(dve, turn, it * UN + u, u, xin[:, u, :], tools).then_inc(s_pre, 1)
                if has_post:
                    ahead(dve, s_post, it * UN)
                    for u in range(UN):
                        ahead(dve, s_mm, it * UN + u + 1)
                        post(dve, turn, it * UN + u, u, ps_y[u], tools).then_inc(s_post, 1)
                if batch_post is not None:
                    ahead(dve, s_mm, it * UN + UN)
                    batch_post(dve, turn, it, K.ps[:, 2:2 + UN, 0:gate_cols], tools).then_inc(s_post, 1)
                turn.end()

        @block.scalar
        def _(act):
            start(act, s_xt, s_apost)
            with act.Fori(0, NT // UN) as it:
                if norm is not None:
                    hold(act, s_var, it + 1)
                    act.sqrt(mv[:, :, 1], mv[:, :, 1]).then_inc(s_rstd, 1)
                for u in range(UN):
                    t = it * UN + u
                    hold(act, s_tr, t + 1)
                    if u == 0:
                        if products:
                            ahead(act, s_mm, it * UN)
                        if keep_xt:
                            ahead(act, s_kept, it * (UN * 2 if keep_xn else UN))
                    act.copy(xt[:, u, :, :], ps_t[u % 2].rearrange("p (c f) -> p c f", c=DC)).then_inc(s_xt, 1)
                if has_act:
                    for u in range(UN):
                        ahead(act, *((s_post, it * UN + u + 1) if has_post else (s_mm, it * UN + u + 1)))
                        act_post(act, it * UN + u, u, ps_y[u], tools).then_inc(s_apost, 1)
                if batch_post is not None and gates_exp:
                    hold(act, tools.s_sum, it + 1)
                    act.activation(tools.work2[:, :, 0:gate_cols], tools.work2[:, :, 0:gate_cols], ACT.Exp).then_inc(s_exp, 1)

        if keep_xt or keep_xn:
            @block.gpsimd
            def _(pool):
                start(pool, s_kept)
                with pool.Fori(0, NT // UN) as it:
                    for u in range(UN):
                        t = it * UN + u
                        if keep_xn:
                            hold(pool, s_pre, t + 1)
                            pool.tensor_copy(K.aux[:, t, :], xin[:, u, :]).then_inc(s_kept, 1)
                        if keep_xt:
                            ahead(pool, s_xt, t + 1)
                            pool.tensor_copy(K.xt[:, :, bass.ds(t * P, P)], xt[:, u, :, :]).then_inc(s_kept, 1)

        @block.tensor
        def _(pe):
            start(pe, s_mm)
            if n_loads:
                pe.wait_ge(loaded, n_loads)
            with pe.Fori(0, NT // UN) as it:
                for u in range(UN + 1):
                    if u < UN:
                        t = it * UN + u
                        hold(pe, s_pre, t + 1)
                        ahead(pe, s_xt, t - 1 if u > 1 else it * UN)
                        for c in range(DC):
                            mm = pe.transpose(ps_t[u % 2][:, c * P:(c + 1) * P], xin[:, u, c * P:(c + 1) * P], K.ident[:, :])
                        mm.then_inc(s_tr, 1)
                    if u > 0 and products:
                        v = u - 1
                        ahead(pe, s_xt, it * UN + v + 1)
                        if v == 0:
                            if has_post:
                                ahead(pe, s_post, it * UN)
                            if has_act:
                                ahead(pe, s_apost, it * UN)
                            if batch_post is not None:
                                ahead(pe, s_post, it)
                        for c in range(DC):
                            mm = pe.matmul(ps_y[v][:, 0:wide], xt[:, v, c, :], w_sb[:, c, :], start=c == 0, stop=c == DC - 1)
                        mm.then_inc(s_mm, 1)


def normed(K):
    def pre(dve, turn, t, u, xin, tools):
        return dve.tensor_scalar(xin, K.x[:, t, :], tools.mv[:, u, 0:1], tools.mv[:, u, 1:2], ALU.subtract, ALU.mult)
    return pre


def softmax_gates(K, bias_name, cols):
    def batch(dve, turn, it, ps, tools):
        logits = tools.work2[:, :, 0:cols]
        top = tools.small[:, :, 0]
        b = tools.vec[bias_name][:, :].unsqueeze(1).to_broadcast([P, UN, cols])
        turn(dve.tensor_tensor(logits, ps, b, ALU.add))
        turn(dve.tensor_reduce(top, logits, AX, ALU.max))
        dve.tensor_tensor(logits, logits, top.unsqueeze(2).to_broadcast([P, UN, cols]), ALU.subtract).then_inc(tools.s_sum, 1)
        hold(dve, tools.s_exp, it + 1)
        turn(dve.tensor_reduce(top, logits, AX, ALU.add))
        turn(dve.reciprocal(top, top))
        return dve.tensor_tensor(K.gate[:, bass.ds(it * UN, UN), :], logits, top.unsqueeze(2).to_broadcast([P, UN, cols]), ALU.mult)
    return batch


def dense_experts(K, tag):
    nc = K.nc
    NE = 8
    CH = UN * P
    HF = CH // 2
    with Phase(nc, tag) as ph:
        consts, prep, turned = ph.sem("consts"), ph.sem("prep"), ph.sem("turned")
        w_in = [ph.sem("w_in0"), ph.sem("w_in1")]
        s_one, s_h1, s_two, s_h2, s_out, s_add = (ph.sem(n) for n in ("one", "h1", "two", "h2", "out", "add"))
        s_gt, s_gc, s_go, s_fin, s_root = (ph.sem(n) for n in ("gt", "gc", "go", "fin", "root"))
        w1, w2, wo = (ph.sb(n, [P, 2, DC, D]) for n in ("w1", "w2", "wo"))
        bo = ph.sb("bo", [NE, D])
        raw = ph.sb("raw", [P, P])
        raw2 = ph.sb("raw2", [32, P])
        cst = ph.sb("cst", [P, 10, NE, DC])
        h1 = ph.sb("h1", [P, 2, DC, HF])
        h2 = ph.sb("h2", [P, DC, CH])
        gate_t, gate_c, s_copied = ph.sb("gate_t", [NE, 2, P]), ph.sb("gate_c", [P, NE]), ph.sem("copied")
        block = ph.block()
        ES = NE * DC
        order = ["b1", "g1", "be1", "m1", "v1", "b2", "g2", "be2", "m2", "v2"]
        B = {n: cst[:, i, :, :] for i, n in enumerate(order)}
        ps_one = [[K.ps[:, 0, 0:HF], K.ps[:, 1, 0:HF]], [K.ps[:, 2, 0:HF], K.ps[:, 3, 0:HF]]]
        ps_two = [[K.ps[:, 4, 0:HF], K.ps[:, 5, 0:HF]], [K.ps[:, 6, 0:HF], K.ps[:, 7, 0:HF]]]
        ps_out = [K.ps[:, 2, 0:D], K.ps[:, 3, 0:D]]
        NCH = NT // UN

        @block.sync
        def _(sp):
            for i, n in enumerate(order):
                rows = K.inp[f"L0_ffn_{n}"].rearrange("e (c p) -> (e c) p", p=P)
                dst = raw[i * ES:(i + 1) * ES, :] if i < 8 else raw2[(i - 8) * ES:(i - 7) * ES, :]
                sp.dma_start(dst, rows).then_inc(consts, 16)
            sp.dma_start(bo[:, :], K.inp["L0_ffn_bo"]).then_inc(consts, 16)
            with sp.Fori(0, NE // 2) as eo:
                for b in range(2):
                    ahead(sp, s_out, eo * (2 * NT) if b == 0 else eo * (2 * NT))
                    for name, w in (("W1", w1), ("W2", w2), ("Wo", wo)):
                        sp.dma_start(w[:, b, :, :], K.inp[f"L0_ffn_{name}"][bass.ds(eo * 2 + b, 1), :, :].rearrange(
                            "a (c p) n -> p (a c) n", p=P)).then_inc(w_in[b], 16)

        @block.vector
        def _(dve):
            start(dve, s_add, s_gc, s_fin)
            link = Chain(dve, prep)
            dve.wait_ge(turned, 2)
            flat = cst[:, :, :, :].rearrange("p a e c -> p (a e c)")
            link(dve.tensor_copy(flat[:, 0:8 * ES], K.ps[:, 0, 0:P]))
            link(dve.tensor_copy(flat[:, 8 * ES:10 * ES], K.ps[:, 1, 0:2 * ES]))
            for g, b, be, m, v in (("g1", "b1", "be1", "m1", "v1"), ("g2", "b2", "be2", "m2", "v2")):
                link(dve.tensor_scalar(B[v], B[v], 1e-3, None, ALU.add))
            dve.wait_ge(s_root, 2)
            for g, b, be, m, v in (("g1", "b1", "be1", "m1", "v1"), ("g2", "b2", "be2", "m2", "v2")):
                link(dve.reciprocal(B[v], B[v]))
                link(dve.tensor_tensor(B[g], B[g], B[v], ALU.mult))
                link(dve.tensor_tensor(B[b], B[b], B[m], ALU.subtract))
                link(dve.tensor_tensor(B[b], B[b], B[g], ALU.mult))
                link(dve.tensor_tensor(B[be], B[be], B[b], ALU.add))
            with dve.Fori(0, NE) as e:
                with dve.Fori(0, NCH) as ch:
                    n = e * NT + ch * UN
                    for u in range(UN):
                        t = ch * UN + u
                        ahead(dve, s_out, n + u + 1)
                        dve.scalar_tensor_tensor(out=K.x[:, t, :], in0=ps_out[u % 2],
                                                 scalar=K.gate[:, t, bass.ds(e, 1)],
                                                 in1=K.x[:, t, :], op0=ALU.mult, op1=ALU.add).then_inc(s_add, 1)
            with dve.Fori(0, NT) as t:
                ahead(dve, s_gt, t + 1)
                dve.tensor_copy(gate_t[:, 0, :], K.ps[0:NE, 0, 0:P]).then_inc(s_gc, 1)
                hold(dve, s_go, t + 1)
                dve.wait_ge(s_add, NE * NT + 1)
                dve.tensor_tensor(K.x[:, t, :], K.x[:, t, :], K.ps[:, 2, 0:D], ALU.add).then_inc(s_fin, 1)

        @block.scalar
        def _(act):
            start(act, s_h1, s_h2)
            act.wait_ge(prep, 4)
            act.sqrt(B["v1"], B["v1"]).then_inc(s_root, 1)
            act.sqrt(B["v2"], B["v2"]).then_inc(s_root, 1)
            act.wait_ge(prep, 14)
            with act.Fori(0, NE) as e:
                with act.Fori(0, NCH) as ch:
                    n = e * (NCH * 4) + ch * 4
                    for h in range(2):
                        for c in range(DC):
                            hold(act, s_one, n + h * 2 + c + 1)
                            ahead(act, s_two, n if h == 0 else n)
                            act.activation(h1[:, h, c, :], ps_one[h][c], ACT.Relu, bias=B["be1"][:, bass.ds(e, 1), c],
                                           scale=B["g1"][:, bass.ds(e, 1), c]).then_inc(s_h1, 1)
                    for h in range(2):
                        for c in range(DC):
                            ahead(act, s_two, n + h * 2 + c + 1)
                            ahead(act, s_out, e * NT + ch * UN)
                            act.activation(h2[:, c, h * HF:(h + 1) * HF], ps_two[h][c], ACT.Relu,
                                           bias=B["be2"][:, bass.ds(e, 1), c],
                                           scale=B["g2"][:, bass.ds(e, 1), c]).then_inc(s_h2, 1)

        @block.tensor
        def _(pe):
            start(pe, s_two, s_out, s_gt)
            pe.wait_ge(consts, 11 * 16)
            pe.transpose(K.ps[:, 0, 0:P], raw[:, :], K.ident[:, :]).then_inc(turned, 1)
            pe.transpose(K.ps[:, 1, 0:32], raw2[:, :], K.ident[0:32, 0:32]).then_inc(turned, 1)
            pe.wait_ge(prep, 2)
            with pe.Fori(0, NE // 2) as eo:
                for b in range(2):
                    hold(pe, w_in[b], (eo + 1) * 48)
                    with pe.Fori(0, NCH) as ch:
                        n = (eo * 2 + b) * (NCH * 4) + ch * 4
                        m = (eo * 2 + b) * NT + ch * UN
                        ahead(pe, s_h1, n)
                        for h in range(2):
                            if h == 1:
                                ahead(pe, s_add, m)
                            for oc in range(DC):
                                for c in range(DC):
                                    mm = pe.matmul(ps_one[h][oc], w1[:, b, c, oc * P:(oc + 1) * P],
                                                   K.xt[:, c, bass.ds(ch * CH + h * HF, HF)], start=c == 0, stop=c == DC - 1)
                                mm.then_inc(s_one, 1)
                        for h in range(2):
                            ahead(pe, s_h1, n + h * 2 + 2)
                            ahead(pe, s_h2, n)
                            for oc in range(DC):
                                for c in range(DC):
                                    mm = pe.matmul(ps_two[h][oc], w2[:, b, c, oc * P:(oc + 1) * P], h1[:, h, c, :],
                                                   start=c == 0, stop=c == DC - 1)
                                mm.then_inc(s_two, 1)
                        for u in range(UN):
                            ahead(pe, s_h2, n + (2 if (u + 1) * P <= HF else 4))
                            if u >= 2:
                                ahead(pe, s_add, m + u - 1)
                            for c in range(DC):
                                mm = pe.matmul(ps_out[u % 2], h2[:, c, u * P:(u + 1) * P], wo[:, b, c, :],
                                               start=c == 0, stop=c == DC - 1)
                            mm.then_inc(s_out, 1)
            pe.wait_ge(s_add, NE * NT + 1)
            with pe.Fori(0, NT) as t:
                ahead(pe, s_gc, t)
                hold(pe, s_copied, t + 1)
                pe.transpose(K.ps[0:NE, 0, 0:P], gate_c[:, :], K.ident[:, :]).then_inc(s_gt, 1)
                ahead(pe, s_gc, t + 1)
                ahead(pe, s_fin, t)
                pe.matmul(K.ps[:, 2, 0:D], gate_t[:, 0, :], bo[:, :], start=True, stop=True).then_inc(s_go, 1)

        @block.gpsimd
        def _(pool):
            with pool.Fori(0, NT) as t:
                ahead(pool, s_gt, t)
                pool.tensor_copy(gate_c[:, :], K.gate[:, t, :]).then_inc(s_copied, 1)


def heads_of(ap, heads):
    f = D // heads
    return ap[:, 0:heads * (f + 1)].rearrange("p (h f) -> p h f", h=heads)


def ones_of(K, heads):
    f = D // heads
    return K.acc[:, :, 0:heads * (f + 1)].rearrange("p t (h f) -> p t h f", h=heads)[:, :, :, f]


def attention_rows(K, heads, src_name, dst_name):
    f = D // heads

    def act_post(act, t, u, ps, tools):
        return act.copy(heads_of(K.acc[:, t, :], heads)[:, :, 0:f], ps[:, 0:D].rearrange("p (h f) -> p h f", h=heads))

    def post(dve, turn, t, u, ps, tools):
        prod = tools.work[:, u, :].rearrange("p (h f) -> p h f", h=heads)
        turn(dve.tensor_tensor(tools.work[:, u, :], ps[:, 0:D], tools.vec[src_name][:, :], ALU.mult))
        turn(dve.tensor_reduce(K.score_src[:, t, 0:heads], prod, AX, ALU.add))
        turn(dve.tensor_tensor(tools.work[:, u, :], ps[:, 0:D], tools.vec[dst_name][:, :], ALU.mult))
        return dve.tensor_reduce(K.score_dst[:, t, 0:heads], prod, AX, ALU.add)

    return post, act_post, 3


def edge_weights(K, tag, heads, self_tiles):
    nc = K.nc
    f, H = D // heads, heads
    SL = 0.2
    GE = 20
    NE = KT // GE
    QB = 4
    BK = GE // QB * H
    SB = 4 if H > 1 else GE
    assert NE % 2 == 0 and SB * NT * H <= 512
    with Phase(nc, tag) as ph:
        step, lchain, split = ph.sem("step"), ph.sem("lchain"), ph.sem("split")
        s_hot, s_away, s_raw, s_sel, s_e, s_top, s_red = (
            ph.sem(n) for n in ("hot", "away", "raw", "sel", "e", "top", "red"))
        s_hot2, s_back, s_logit, s_exp, mchain, s_m = (ph.sem(n) for n in ("hot2", "back", "logit", "exp", "mchain", "m"))
        s_own, s_ownexp, lchain2 = ph.sem("own"), ph.sem("ownexp"), ph.sem("lchain2")
        rows_in, rows_again = [ph.sem(f"rows_in{b}") for b in range(2)], [ph.sem(f"rows_again{b}") for b in range(2)]
        src_b, dst_b = (ph.sb(n, [P, 2, GE * P], BF16) for n in ("src_b", "dst_b"))
        hit_src, hit_dst, away = (ph.sb(n, [P, 2, GE * P], BF16) for n in ("hit_src", "hit_dst", "away"))
        tab_src, tab_dst, tab_m = (ph.sb(n, [P, 3, NT, H], BF16) for n in ("tab_src", "tab_dst", "tab_m"))
        rest = ph.sb("rest", [P, NT, H])
        here = ph.sb("here", [P, GE, NT])
        prod, sel = ph.sb("prod", [P, SB, NT, H]), ph.sb("sel", [P, GE, H])
        ring_e = ph.sb("ring_e", [P, 2, GE, H])
        e_all, top = ph.sb("e_all", [P, KT, H]), ph.sb("top", [P, KT, H])
        masked, off = ph.sb("masked", [P, KT, H]), ph.sb("off", [P, KT])
        m, own, own_w = ph.sb("m", [P, NT, H]), ph.sb("own", [P, NT, H]), ph.sb("own_w", [P, NT, H])
        logit = ph.sb("logit", [P, 2, GE, H])
        block = ph.block()
        score_src, score_dst = K.score_src[:, :, 0:H], K.score_dst[:, :, 0:H]
        ps_dst = K.ps[:, 5, 0:GE * H].rearrange("p (u h) -> p u h", h=H)
        ps_max = [K.ps[:, 6, 0:QB * P], K.ps[:, 7, 0:QB * P]]
        ps_back = [K.ps[:, b, 0:GE * H].rearrange("p (u h) -> p u h", h=H) for b in range(2)]

        def ps_src(u):
            return K.ps[:, u // SB, (u % SB) * NT * H:(u % SB + 1) * NT * H]

        def in_parts(link, v, tab, value):
            link(v.tensor_copy(tab[:, 0, :, :], value))
            link(v.tensor_tensor(rest[:, :, :], value, tab[:, 0, :, :], ALU.subtract))
            link(v.tensor_copy(tab[:, 1, :, :], rest[:, :, :]))
            link(v.tensor_tensor(rest[:, :, :], rest[:, :, :], tab[:, 1, :, :], ALU.subtract))
            link(v.tensor_copy(tab[:, 2, :, :], rest[:, :, :]))

        @block.sync
        def _(sp):
            with sp.Fori(0, NE // 2) as it:
                for b in range(2):
                    g = it * 2 + b
                    hold(sp, s_hot, g + 1)
                    for i, dst in enumerate((src_b, dst_b)):
                        row = K.pair_rows[i, bass.ds(g * GE, GE), :].rearrange("k e -> (k e)").partition_broadcast(P)
                        sp.dma_start(dst[:, b, :], row).then_inc(rows_in[b], 16)
            sp.wait_ge(s_hot, NE + 2)
            with sp.Fori(0, NE // 2) as it:
                for b in range(2):
                    g = it * 2 + b
                    hold(sp, s_hot2, g + 1)
                    row = K.pair_rows[1, bass.ds(g * GE, GE), :].rearrange("k e -> (k e)").partition_broadcast(P)
                    sp.dma_start(dst_b[:, b, :], row).then_inc(rows_again[b], 16)

        @block.scalar
        def _(act):
            act.sem_inc(s_away, 2)
            act.sem_inc(s_exp, 2)
            with act.Fori(0, NE // 2) as it:
                for b in range(2):
                    g = it * 2 + b
                    hold(act, s_hot, g + 3)
                    hold(act, s_top, (g + 1) * BK)
                    act.activation(away[:, b, :], hit_dst[:, b, :], ACT.Copy, bias=-BIG, scale=BIG).then_inc(s_away, 1)
            act.wait_ge(s_own, 1)
            act.activation(own_w[:, :, :], own[:, :, :], ACT.Exp).then_inc(s_ownexp, 1)
            with act.Fori(0, NE // 2) as it:
                for b in range(2):
                    g = it * 2 + b
                    hold(act, s_logit, g + 3)
                    act.activation(K.edge_w[:, bass.ds(g * GE, GE), 0:H], logit[:, b, :, :], ACT.Exp).then_inc(s_exp, 1)

        @block.vector
        def _(dve):
            dve.sem_inc(s_hot, 2)
            dve.sem_inc(s_sel, 1)
            dve.sem_inc(s_red, 2)
            dve.sem_inc(s_hot2, 2)
            dve.sem_inc(s_logit, 2)
            link = Chain(dve, step)
            in_parts(link, dve, tab_src, score_src)
            in_parts(link, dve, tab_dst, score_dst)
            dve.sem_inc(split, 1)
            with dve.Fori(0, NE // 2) as it:
                turn = LoopChain(dve, lchain, it, 2 * (1 + 2 * (GE // SB) + 1))
                for b in range(2):
                    g = it * 2 + b
                    hold(dve, rows_in[b], (it + 1) * 32)
                    hold(dve, s_raw, g + 1)
                    hold(dve, s_away, g + 1)
                    turn(dve.tensor_scalar(hit_src[:, b, :], src_b[:, b, :], K.col_f[:, 0:1], None, ALU.is_equal))
                    dve.tensor_scalar(hit_dst[:, b, :], dst_b[:, b, :], K.col_f[:, 0:1], None, ALU.is_equal).then_inc(s_hot, 1)
                for b in range(2):
                    g = it * 2 + b
                    tiles = K.src_tile[:, bass.ds(g * GE, GE)].unsqueeze(2).to_broadcast([P, GE, NT])
                    turn(dve.tensor_tensor(here[:, :, :], tiles, K.row_f[:, 0:NT].unsqueeze(1).to_broadcast([P, GE, NT]),
                                           ALU.is_equal))
                    hold(dve, s_raw, g + 3)
                    for j in range(GE // SB):
                        raw = K.ps[:, j, 0:SB * NT * H].rearrange("p (u t h) -> p u t h", t=NT, h=H)
                        mine = here[:, j * SB:(j + 1) * SB, :].unsqueeze(3).to_broadcast([P, SB, NT, H])
                        turn(dve.tensor_tensor(prod[:, :, :, :], raw, mine, ALU.mult))
                        ins = dve.tensor_reduce(sel[:, j * SB:(j + 1) * SB, :], prod[:, :, :, :].rearrange("p u t h -> p u h t"),
                                                AX, ALU.add)
                        if j < GE // SB - 1:
                            turn(ins)
                    turn(ins)
                    dve.tensor_tensor(sel[:, :, :], sel[:, :, :], ps_dst, ALU.add).then_inc(s_sel, 1)
                    hold(dve, s_sel, g + 2)
                    hold(dve, s_top, (g + 1) * BK)
                    dve.scalar_tensor_tensor(out=ring_e[:, b, :, :], in0=sel[:, :, :], scalar=SL, in1=sel[:, :, :],
                                             op0=ALU.mult, op1=ALU.max).then_inc(s_e, 1)
                    hold(dve, s_e, g + 1)
                    dve.tensor_copy(e_all[:, bass.ds(g * GE, GE), :], ring_e[:, b, :, :])
                for b in range(2):
                    g = it * 2 + b
                    for j in range(GE // QB):
                        for h in range(H):
                            q = g * BK + j * H + h
                            hold(dve, s_top, q + 1 + 2 * BK)
                            dve.tensor_reduce(top[:, bass.ds(g * GE + j * QB, QB), h],
                                              ps_max[(j * H + h + b * BK) % 2].rearrange("p (u e) -> p u e", e=P),
                                              AX, ALU.max).then_inc(s_red, 1)
                turn.end()
            dve.wait_ge(s_red, NE * BK + 2)
            with dve.Fori(0, NT) as t:
                turn = LoopChain(dve, mchain, t, 3)
                turn(dve.tensor_scalar(off[:, :], K.tile_f[:, :], K.row_f[:, bass.ds(t, 1)], -BIG, ALU.not_equal, ALU.mult))
                turn(dve.tensor_tensor(masked[:, :, :], top[:, :, :], off[:, :].unsqueeze(2).to_broadcast([P, KT, H]), ALU.add))
                turn(dve.tensor_reduce(m[:, t, :], masked[:, :, :].rearrange("p k h -> p h k"), AX, ALU.max))
                turn.end()
            link(dve.tensor_tensor(own[:, :, :], score_src, score_dst, ALU.add))
            link(dve.scalar_tensor_tensor(out=own[:, :, :], in0=own[:, :, :], scalar=SL, in1=own[:, :, :],
                                          op0=ALU.mult, op1=ALU.max))
            looped = m[:, 0:self_tiles, :]
            link(dve.tensor_tensor(looped, looped, own[:, 0:self_tiles, :], ALU.max))
            link(dve.tensor_tensor(own[:, :, :], own[:, :, :], m[:, :, :], ALU.subtract))
            dve.tensor_scalar(own[:, :, :], own[:, :, :], 0.0, None, ALU.min).then_inc(s_own, 1)
            in_parts(link, dve, tab_m, m[:, :, :])
            dve.sem_inc(s_m, 1)
            dve.wait_ge(s_ownexp, 1)
            values = K.acc[:, 0:self_tiles, 0:H * (f + 1)].rearrange("p t (h f) -> p t h f", h=H)
            link(dve.tensor_tensor(values, values,
                                   own_w[:, 0:self_tiles, :].unsqueeze(3).to_broadcast([P, self_tiles, H, f + 1]), ALU.mult))
            if self_tiles < NT:
                link(dve.memset(K.acc[:, self_tiles:NT, :], 0.0))
            with dve.Fori(0, NE // 2) as it:
                turn = LoopChain(dve, lchain2, it, 2)
                for b in range(2):
                    g = it * 2 + b
                    hold(dve, rows_again[b], (it + 1) * 16)
                    hold(dve, s_back, g + 1)
                    dve.tensor_scalar(hit_dst[:, b, :], dst_b[:, b, :], K.col_f[:, 0:1], None, ALU.is_equal).then_inc(s_hot2, 1)
                for b in range(2):
                    g = it * 2 + b
                    hold(dve, s_back, g + 3)
                    hold(dve, s_exp, g + 1)
                    turn(dve.tensor_tensor(logit[:, b, :, :], e_all[:, bass.ds(g * GE, GE), :], ps_back[b], ALU.subtract))
                    dve.tensor_scalar(logit[:, b, :, :], logit[:, b, :, :], 0.0, None, ALU.min).then_inc(s_logit, 1)
                turn.end()

        @block.tensor
        def _(pe):
            pe.sem_inc(s_raw, 2)
            pe.sem_inc(s_top, 2 * BK)
            pe.sem_inc(s_back, 2)

            def node_tile(k):
                return nc.values_load(K.tile_of[0:1, bass.ds(k, 1)], engines=[pe.engine], min_val=0, max_val=NT - 1,
                                      skip_runtime_bounds_check_because="it counts NT - 1 comparisons")

            pe.wait_ge(split, 1)
            with pe.Fori(0, NE // 2) as it:
                for b in range(2):
                    g = it * 2 + b
                    hold(pe, s_hot, g + 3)
                    hold(pe, s_sel, g + 1)
                    for u in range(GE):
                        cols = slice(u * P, (u + 1) * P)
                        if u % PAIR == 0:
                            tile = node_tile(g * GE + u)
                        for i in range(3):
                            pe.matmul(ps_src(u), hit_src[:, b, cols], tab_src[:, i, :, :].rearrange("p t h -> p (t h)"),
                                      start=i == 0, stop=i == 2)
                        for i in range(3):
                            mm = pe.matmul(ps_dst[:, u, :], hit_dst[:, b, cols], tab_dst[:, i, tile, :],
                                           start=i == 0, stop=i == 2)
                    mm.then_inc(s_raw, 1)
                for b in range(2):
                    g = it * 2 + b
                    hold(pe, s_e, g + 1)
                    hold(pe, s_away, g + 3)
                    for j in range(GE // QB):
                        for h in range(H):
                            q = g * BK + j * H + h
                            bank = ps_max[(j * H + h + b * BK) % 2]
                            hold(pe, s_red, q + 1)
                            for i in range(QB):
                                u = j * QB + i
                                pe.matmul(bank[:, i * P:(i + 1) * P], K.ident_b[:, :], away[:, b, u * P:(u + 1) * P],
                                          start=True, stop=False)
                                mm = pe.matmul(bank[:, i * P:(i + 1) * P], ring_e[:, b, u, h:h + 1].to_broadcast([P, P]),
                                               K.ident[:, :], start=False, stop=True)
                            mm.then_inc(s_top, 1)
            pe.wait_ge(s_m, 1)
            with pe.Fori(0, NE // 2) as it:
                for b in range(2):
                    g = it * 2 + b
                    hold(pe, s_hot2, g + 3)
                    hold(pe, s_logit, g + 1)
                    for u in range(GE):
                        if u % PAIR == 0:
                            tile = node_tile(g * GE + u)
                        for i in range(3):
                            mm = pe.matmul(ps_back[b][:, u, :], hit_dst[:, b, u * P:(u + 1) * P], tab_m[:, i, tile, :],
                                           start=i == 0, stop=i == 2)
                    mm.then_inc(s_back, 1)


def attention_out(K, heads, bias, relu):
    f = D // heads

    def emit(dve, turn, t, out, small):
        rows = heads_of(K.acc[:, t, :], heads)
        turn(dve.tensor_scalar(small[:, 0:heads], rows[:, :, f], 0.5, None, ALU.max))
        turn(dve.reciprocal(small[:, 0:heads], small[:, 0:heads]))
        o3 = out.rearrange("p (h f) -> p h f", h=heads)
        turn(dve.tensor_tensor(o3, rows[:, :, 0:f], small[:, 0:heads].unsqueeze(2).to_broadcast([P, heads, f]), ALU.mult))
        ins = dve.tensor_tensor(out, out, bias, ALU.add)
        if relu:
            turn(ins)
            ins = dve.tensor_scalar(out, out, 0.0, None, ALU.max)
        return ins

    return emit, 3 + relu


def add_to_x(K, tag, vectors, emit, steps, to_aux=False):
    nc = K.nc
    with Phase(nc, tag) as ph:
        loaded, chain = ph.sem("loaded"), ph.sem("chain")
        vec = {n: ph.sb(f"vec_{n}", [P, c]) for n, c in vectors}
        work, small = ph.sb("work", [P, UN, D]), ph.sb("small", [P, UN, 4])
        block = ph.block()

        @block.sync
        def _(sp):
            for name, c in vectors:
                sp.dma_start(vec[name][:, :], K.inp[name].partition_broadcast(P)).then_inc(loaded, 16)

        @block.vector
        def _(dve):
            if vectors:
                dve.wait_ge(loaded, 16 * len(vectors))
            with dve.Fori(0, NT // UN) as it:
                turn = LoopChain(dve, chain, it, (steps + 1 + (not to_aux)) * UN)
                for u in range(UN):
                    t = it * UN + u
                    if to_aux:
                        turn(emit(vec)(dve, turn, t, K.aux[:, t, :], small[:, u, :]))
                        continue
                    turn(emit(vec)(dve, turn, t, work[:, u, :], small[:, u, :]))
                    turn(dve.tensor_tensor(K.x[:, t, :], K.x[:, t, :], work[:, u, :], ALU.add))
                turn.end()


def degree_roots(K):
    with Phase(K.nc, "dinv") as ph:
        a, b = ph.sem("a"), ph.sem("b")
        block = ph.block()

        @block.vector
        def _(dve):
            dve.tensor_scalar(K.dinv[:, :], K.degree[:, :], 1.0, None, ALU.add).then_inc(a, 1)
            dve.wait_ge(b, 1)
            dve.reciprocal(K.dinv[:, :], K.dinv[:, :]).then_inc(a, 1)

        @block.scalar
        def _(act):
            act.wait_ge(a, 1)
            act.sqrt(K.dinv[:, :], K.dinv[:, :]).then_inc(b, 1)


def residual(K, tag, bias_name):
    nc = K.nc
    with Phase(nc, tag) as ph:
        loaded, step = ph.sem("loaded"), ph.sem("step")
        bias = ph.sb("bias", [P, D])
        block = ph.block()

        @block.sync
        def _(sp):
            sp.dma_start(bias[:, :], K.inp[bias_name].partition_broadcast(P)).then_inc(loaded, 16)

        @block.vector
        def _(dve):
            link = Chain(dve, step)
            link(dve.tensor_tensor(K.x[:, :, :], K.x[:, :, :], K.acc[:, :, 0:D], ALU.add))
            link(dve.tensor_tensor(K.x[:, :, :], K.x[:, :, :], K.loop_out[:, :, :], ALU.add))
            dve.wait_ge(loaded, 16)
            link(dve.tensor_tensor(K.x[:, :, :], K.x[:, :, :], bias[:, :].unsqueeze(1).to_broadcast([P, NT, D]), ALU.add))


def wide_experts(K, tag, turns, pairs, HC, act, load, target):
    nc = K.nc
    CH = UN * P
    HF = CH // 2
    NCH = NT // UN
    with Phase(nc, tag) as ph:
        w_in = [ph.sem(f"w_in{b}") for b in range(pairs)]
        s_one, s_h, s_out, s_bias, s_add, s_index = (ph.sem(n) for n in ("one", "h", "out", "bias", "add", "index"))
        w1 = ph.sb("w1", [P, pairs, DC, HC * P])
        w2 = ph.sb("w2", [P, pairs, HC, D])
        b1, b2 = ph.sb("b1", [P, pairs, HC]), ph.sb("b2", [P, pairs, D])
        h = ph.sb("h", [P, HC, CH])
        y = ph.sb("y", [P, 2, D])
        block = ph.block()
        ps_one = [K.ps[:, i, 0:HF] for i in range(4)]
        ps_out = [K.ps[:, 4 + i, 0:D] for i in range(2)]

        @block.sync
        def _(sp):
            with sp.Fori(0, turns) as eo:
                for b in range(pairs):
                    ahead(sp, s_add, eo * (pairs * NT))
                    with nc.allow_non_contiguous_dma(reason="biases by partitions"):
                        load(sp, eo, b, w1[:, b, :, :], w2[:, b, :, :], b1[:, b, :], b2[:, b, :], w_in[b])

        @block.vector
        def _(dve):
            start(dve, s_add, s_bias)
            with dve.Fori(0, turns) as eo:
                for b in range(pairs):
                    hold(dve, w_in[b], (eo + 1) * 64)
                    with dve.Fori(0, NCH) as ch:
                        n = (eo * pairs + b) * NT + ch * UN
                        for u in range(UN):
                            t = ch * UN + u
                            ahead(dve, s_out, n + u + 1)
                            ahead(dve, s_add, n + u - 1 if u else n)
                            dve.tensor_tensor(y[:, u % 2, :], ps_out[u % 2], b2[:, b, :], ALU.add).then_inc(s_bias, 1)
                            ahead(dve, s_bias, n + u + 1)
                            dve.scalar_tensor_tensor(out=target[:, t, :], in0=y[:, u % 2, :],
                                                     scalar=K.gate[:, t, bass.ds(eo * pairs + b, 1)],
                                                     in1=target[:, t, :], op0=ALU.mult, op1=ALU.add).then_inc(s_add, 1)

        @block.scalar
        def _(sc):
            with sc.Fori(0, turns) as eo:
                for b in range(pairs):
                    hold(sc, w_in[b], (eo + 1) * 64)
                    with sc.Fori(0, NCH) as ch:
                        n = ((eo * pairs + b) * NCH + ch) * (HC * 2)
                        m = (eo * pairs + b) * NT + ch * UN
                        ahead(sc, s_out, m)
                        for hc in range(HC):
                            for half in range(2):
                                hold(sc, s_one, n + hc * 2 + half + 1)
                                sc.activation(h[:, hc, half * HF:(half + 1) * HF], ps_one[(hc * 2 + half) % 4], act,
                                              bias=b1[:, b, hc:hc + 1]).then_inc(s_h, 1)

        @block.tensor
        def _(pe):
            start(pe, s_out)
            with pe.Fori(0, turns) as eo:
                for b in range(pairs):
                    hold(pe, w_in[b], (eo + 1) * 64)
                    with pe.Fori(0, NCH) as ch:
                        n = ((eo * pairs + b) * NCH + ch) * (HC * 2)
                        m = (eo * pairs + b) * NT + ch * UN
                        for hc in range(HC):
                            for half in range(2):
                                q = hc * 2 + half
                                if q >= 4:
                                    hold(pe, s_h, n + q - 3)
                                for c in range(DC):
                                    mm = pe.matmul(ps_one[q % 4], w1[:, b, c, hc * P:(hc + 1) * P],
                                                   K.xt[:, c, bass.ds(ch * CH + half * HF, HF)], start=c == 0, stop=c == DC - 1)
                                mm.then_inc(s_one, 1)
                        hold(pe, s_h, n + HC * 2)
                        for u in range(UN):
                            ahead(pe, s_bias, m + u - 1 if u > 1 else m)
                            for hc in range(HC):
                                mm = pe.matmul(ps_out[u % 2], h[:, hc, u * P:(u + 1) * P], w2[:, b, hc, :],
                                               start=hc == 0, stop=hc == HC - 1)
                            mm.then_inc(s_out, 1)


def route_two(K, tag):
    nc = K.nc
    NE, CAP = 8, float(-(-N * 5 // (4 * 8)))
    with Phase(nc, tag) as ph:
        loaded, step, s_logits, s_in, s_exp = (ph.sem(n) for n in ("loaded", "step", "logits", "in", "exp"))
        wr, br = ph.sb("wr", [P, DC, NE]), ph.sb("br", [P, NE])
        total = ph.sb("total", [P, DC])
        p, el, best = ph.sb("p", [P, NE]), ph.sb("el", [P, NE]), ph.sb("best", [P, 8])
        one, pair, index = ph.sb("one", [P, 1]), ph.sb("pair", [P, 2]), ph.sb("index", [P, 8], U32)
        s_total = ph.sem("total")
        block = ph.block()

        @block.sync
        def _(sp):
            sp.dma_start(wr[:, :, :], K.inp["L1_ffn_Wr"].rearrange("(c p) e -> p c e", p=P)).then_inc(loaded, 16)
            sp.dma_start(br[:, :], K.inp["L1_ffn_br"].partition_broadcast(P)).then_inc(loaded, 16)

        @block.tensor
        def _(pe):
            pe.wait_ge(loaded, 32)
            pe.wait_ge(s_total, 1)
            for c in range(DC):
                mm = pe.matmul(K.ps[:, 0, 0:NE], total[:, c:c + 1].to_broadcast([P, P]), wr[:, c, :], start=c == 0, stop=c == DC - 1)
            mm.then_inc(s_logits, 1)

        @block.scalar
        def _(sc):
            for i, a in enumerate((p[:, :], p[:, :], pair[:, 1:2])):
                sc.wait_ge(s_in, i + 1)
                sc.activation(a, a, ACT.Exp).then_inc(s_exp, 1)

        @block.vector
        def _(dve):
            link = Chain(dve, step)
            real = K.xt[:, :, :].rearrange("p c (t n) -> p c t n", n=P)[:, :, :, 0:NPT]
            dve.tensor_reduce(total[:, :], real, mybir.AxisListType.XY, ALU.add).then_inc(s_total, 1)
            dve.wait_ge(s_logits, 1)
            link(dve.scalar_tensor_tensor(out=p[:, :], in0=K.ps[:, 0, 0:NE], scalar=1.0 / N, in1=br[:, :], op0=ALU.mult, op1=ALU.add))

            def softmax(i):
                link(dve.tensor_reduce(one[:, :], p[:, :], AX, ALU.max))
                dve.tensor_scalar(p[:, :], p[:, :], one[:, 0:1], None, ALU.subtract).then_inc(s_in, 1)
                dve.wait_ge(s_exp, i)
                link(dve.tensor_reduce(one[:, :], p[:, :], AX, ALU.add))
                link(dve.reciprocal(one[:, :], one[:, :]))
                link(dve.tensor_scalar(p[:, :], p[:, :], one[:, 0:1], None, ALU.mult))

            softmax(1)
            link(dve.tensor_scalar(el[:, :], p[:, :], float(N), CAP, ALU.mult, ALU.max))
            link(dve.reciprocal(el[:, :], el[:, :]))
            link(dve.scalar_tensor_tensor(out=p[:, :], in0=el[:, :], scalar=CAP, in1=p[:, :], op0=ALU.mult, op1=ALU.mult))
            softmax(2)
            link(dve.max(best[:, :], p[:, :]))
            link(dve.max_index(index[:, :], best[:, :], p[:, :]))
            link(dve.tensor_copy(K.pick[:, :], index[:, 0:2]))
            link(dve.memset(pair[:, 0:1], 1.0))
            dve.tensor_tensor(pair[:, 1:2], best[:, 1:2], best[:, 0:1], ALU.subtract).then_inc(s_in, 1)
            dve.wait_ge(s_exp, 3)
            link(dve.tensor_scalar(one[:, :], pair[:, 1:2], 1.0, None, ALU.add))
            link(dve.reciprocal(one[:, :], one[:, :]))
            link(dve.tensor_scalar(pair[:, :], pair[:, :], one[:, 0:1], None, ALU.mult))
            link(dve.tensor_copy(K.gate[:, :, 0:2], pair[:, :].unsqueeze(1).to_broadcast([P, NT, 2])))


def add_normed(K, tag, gamma_name, beta_name):
    nc = K.nc
    with Phase(nc, tag) as ph:
        loaded, chain, s_var, s_rstd = (ph.sem(n) for n in ("loaded", "chain", "var", "rstd"))
        gamma, beta = ph.sb("gamma", [P, D]), ph.sb("beta", [P, D])
        stats, mv = ph.sb("stats", [P, UN, 6]), ph.sb("mv", [P, UN, 2])
        block = ph.block()

        @block.sync
        def _(sp):
            sp.dma_start(gamma[:, :], K.inp[gamma_name].partition_broadcast(P)).then_inc(loaded, 16)
            sp.dma_start(beta[:, :], K.inp[beta_name].partition_broadcast(P)).then_inc(loaded, 16)

        @block.scalar
        def _(sc):
            with sc.Fori(0, NT // UN) as it:
                hold(sc, s_var, it + 1)
                sc.sqrt(mv[:, :, 1], mv[:, :, 1]).then_inc(s_rstd, 1)

        @block.vector
        def _(dve):
            dve.wait_ge(loaded, 32)
            with dve.Fori(0, NT // UN) as it:
                turn = LoopChain(dve, chain, it, 2 * UN + 1 + 4)
                row_stats(turn, dve, stats, mv, [K.aux[:, it * UN + u, :] for u in range(UN)])
                dve.tensor_scalar(mv[:, :, 1], mv[:, :, 1], LN_EPS, None, ALU.add).then_inc(s_var, 1)
                hold(dve, s_rstd, it + 1)
                turn(dve.reciprocal(mv[:, :, 1], mv[:, :, 1]))
                rows = K.aux[:, bass.ds(it * UN, UN), :]
                wide = [P, UN, D]
                turn(dve.tensor_tensor(rows, rows, mv[:, :, 0].unsqueeze(2).to_broadcast(wide), ALU.subtract))
                turn(dve.tensor_tensor(rows, rows, mv[:, :, 1].unsqueeze(2).to_broadcast(wide), ALU.mult))
                turn(dve.tensor_tensor(rows, rows, gamma[:, :].unsqueeze(1).to_broadcast(wide), ALU.mult))
                x_rows = K.x[:, bass.ds(it * UN, UN), :]
                turn(dve.tensor_tensor(x_rows, x_rows, rows, ALU.add))
                turn.end()
            dve.tensor_tensor(K.x[:, :, :], K.x[:, :, :], beta[:, :].unsqueeze(1).to_broadcast([P, NT, D]), ALU.add)


def top_two_gates(K, bias_name, cols):
    def batch(dve, turn, it, ps, tools):
        logits, best, marked = (tools.work2[:, :, i * 8:i * 8 + 8] for i in range(3))
        top = tools.small[:, :, 0]
        wide = [P, UN, cols]
        b = tools.vec[bias_name][:, :].unsqueeze(1).to_broadcast(wide)
        turn(dve.tensor_tensor(logits, ps, b, ALU.add))
        for u in range(UN):
            turn(dve.max(best[:, u, :], logits[:, u, :]))
        turn(dve.tensor_copy(top, best[:, :, 0]))
        turn(dve.memset(best[:, :, 2:8], BIG))
        for u in range(UN):
            turn(dve.match_replace(marked[:, u, :], best[:, u, :], logits[:, u, :], -BIG))
        dve.tensor_tensor(logits, logits, top.unsqueeze(2).to_broadcast(wide), ALU.subtract).then_inc(tools.s_sum, 1)
        hold(dve, tools.s_exp, it + 1)
        turn(dve.scalar_tensor_tensor(out=logits, in0=marked, scalar=-BIG, in1=logits, op0=ALU.is_equal, op1=ALU.mult))
        turn(dve.tensor_reduce(top, logits, AX, ALU.add))
        turn(dve.reciprocal(top, top))
        return dve.tensor_tensor(K.gate[:, bass.ds(it * UN, UN), :], logits, top.unsqueeze(2).to_broadcast(wide), ALU.mult)
    return batch, 6 + 2 * UN


def largest_gates(K, tag, count):
    nc = K.nc
    with Phase(nc, tag) as ph:
        step, lchain, s_row, s_copied, s_diag = (ph.sem(n) for n in ("step", "lchain", "row", "copied", "diag"))
        diag, rows = ph.sb("diag", [P, NT, NPT]), ph.sb("rows", [P, NT, NPT])
        earlier = ph.sb("earlier", [P, 2 * N])
        found, value, rank = ph.sb("found", [P, N]), ph.sb("value", [P, NT]), ph.sb("rank", [P, NT])
        block = ph.block()
        flat, flat_diag = rows[:, :, :].rearrange("p t n -> p (t n)"), diag[:, :, :].rearrange("p t n -> p (t n)")
        cuts = [(c, min(c + 4 * NPT, N)) for c in range(0, N, 4 * NPT)]

        @block.tensor
        def _(pe):
            pe.wait_ge(s_diag, 1)
            for i, (a, b) in enumerate(cuts):
                pe.matmul(K.ps[:, i, 0:b - a], K.ones[:, :], flat_diag[:, a:b], start=True, stop=True).then_inc(s_row, 1)

        @block.scalar
        def _(sc):
            for i, (a, b) in enumerate(cuts):
                sc.wait_ge(s_row, i + 1)
                sc.copy(flat[:, a:b], K.ps[:, i, 0:b - a]).then_inc(s_copied, 1)

        @block.vector
        def _(dve):
            link = Chain(dve, step)
            wide = [P, NT, NPT]
            eye = K.ident[:, 0:NPT].unsqueeze(1).to_broadcast(wide)
            dve.tensor_tensor(diag[:, :, :], eye, K.token_w[:, :].unsqueeze(2).to_broadcast(wide), ALU.mult).then_inc(s_diag, 1)
            link(dve.memset(earlier[:, 0:N], 1.0))
            link(dve.memset(earlier[:, N:2 * N], 0.0))
            link(dve.tensor_scalar(earlier[:, N:N + NPT], K.row_f[:, 0:NPT], K.col_f[:, 0:1], None, ALU.is_lt))
            link(dve.tensor_tensor(K.x[:, :, :], K.x[:, :, :], K.aux[:, :, :], ALU.add))
            dve.wait_ge(s_copied, len(cuts))
            link(dve.tensor_tensor(diag[:, :, :], rows[:, :, :], eye, ALU.mult))
            link(dve.tensor_reduce(value[:, :], diag[:, :, :], AX, ALU.add))
            with dve.Fori(0, NT) as t:
                turn = LoopChain(dve, lchain, t, 3)
                mine = value[:, bass.ds(t, 1)]
                turn(dve.scalar_tensor_tensor(out=found[:, :], in0=flat, scalar=mine, in1=earlier[:, bass.ds(N - t * NPT, N)],
                                              op0=ALU.is_equal, op1=ALU.mult))
                turn(dve.scalar_tensor_tensor(out=found[:, :], in0=flat, scalar=mine, in1=found[:, :],
                                              op0=ALU.is_gt, op1=ALU.add))
                turn(dve.tensor_reduce(rank[:, bass.ds(t, 1)], found[:, :], AX, ALU.add))
                turn.end()
            dve.scalar_tensor_tensor(out=K.gate[:, :, 0], in0=rank[:, :], scalar=float(count), in1=K.token_w[:, :],
                                     op0=ALU.is_lt, op1=ALU.mult)


def store(K, out):
    nc = K.nc
    with Phase(nc, "store") as ph:
        stored = ph.sem("stored")
        block = ph.block()

        @block.sync
        def _(sp):
            rows = out.rearrange("(t p) d -> p t d", p=NPT)
            sp.dma_start(rows[0:112], K.x[0:112, :, :]).then_inc(stored, 16)
            sp.dma_start(rows[112:NPT], K.x[112:NPT, :, :]).then_inc(stored, 16)
            sp.wait_ge(stored, 32)


def build(nc, inp, out, upto=99):
    K = Net()
    K.nc, K.inp = nc, inp
    ctx = ExitStack()
    with ctx:
        def sb(name, shape, dt=F32):
            return ctx.enter_context(nc.sbuf_tensor(name, shape, dt))

        Net.ctx = ctx
        Net.passed = {e.engine: ctx.enter_context(nc.semaphore(f"passed_{name}")) for name, e in (
            ("sp", nc.sync), ("act", nc.scalar), ("pe", nc.tensor), ("dve", nc.vector), ("pool", nc.gpsimd))}
        K.ps = ctx.enter_context(nc.psum_tensor("ps", [P, 8, 512], F32))
        K.x = sb("x_nodes", [P, NT, D])
        K.acc = sb("acc", [P, NT, TW])
        K.loop_out = K.aux = sb("aux", [P, NT, D])
        K.row_f, K.row_b = sb("row_f", [P, P]), sb("row_b", [P, P], BF16)
        K.col_f = sb("col_f", [P, 1])
        K.ident, K.ident_b = sb("ident", [P, P]), sb("ident_b", [P, P], BF16)
        K.before, K.ones = sb("before", [P, P]), sb("ones", [P, P])
        K.tile_of, K.rel_row, K.src_row = (sb(n, [P, KT], I32) for n in ("tile_of", "rel_row", "src_row"))
        K.slot_dst, K.slot_w = sb("slot_dst", [P, KT]), sb("slot_w", [P, KT])
        K.degree = sb("degree", [P, NT])
        K.rec_dram = nc.dram_tensor("rec_dram", [KT * P + EC, 4], F32).ap()
        K.rel_table = nc.dram_tensor("rel_table", [NPAD, R, D], F32).ap()
        K.node_table = nc.dram_tensor("node_table", [NPAD, D], F32).ap()
        K.att_table = nc.dram_tensor("att_table", [NPAD, TW], F32).ap()
        K.dinv = sb("dinv", [P, NT])
        K.src_tile, K.tile_f = sb("src_tile", [P, KT]), sb("tile_f", [P, KT])
        K.pair_rows = nc.dram_tensor("pair_rows", [2, KT, P], BF16).ap()
        rel_rows = K.rel_table.rearrange("n r f -> (n r) f")
        setup(K)
        sort_edges(K)
        edge_rows(K)

        def pre_norm(dve, turn, t, u, xin, mv, bias):
            return dve.tensor_scalar(xin, K.x[:, t, :], mv[:, u, 0:1], mv[:, u, 1:2], ALU.subtract, ALU.mult)

        def pre_hidden(dve, turn, t, u, xin, mv, bias):
            turn(dve.tensor_tensor(xin, K.acc[:, t, 0:D], bias[:, :], ALU.add))
            turn(dve.tensor_tensor(xin, xin, K.loop_out[:, t, :], ALU.add))
            return dve.tensor_scalar(xin, xin, 0.0, None, ALU.max)

        relation_tables(K, "rel1", "L0_gnn_w1", "L0_gnn_loop_w1", pre_norm, 2 * UN + 1, True)
        edge_sum(K, "sum1", rel_rows, K.rel_row, K.slot_w, count=True)
        relation_tables(K, "rel2", "L0_gnn_w2", "L0_gnn_loop_w2", pre_hidden, 2 * UN, False)
        edge_sum(K, "sum2", rel_rows, K.rel_row, K.slot_w)
        residual(K, "res0", "L0_gnn_b2")
        if upto >= 1:
            K.xt = sb("xt_nodes", [P, DC, NPAD])
            K.gate = sb("gate", [P, NT, 8])
            node_pass(K, "prep0", ["L0_ffn_Wr"], [("L0_ffn_br", 8)], normed(K), 0, norm=lambda t: K.x[:, t, :],
                      keep_xt=True, batch_post=softmax_gates(K, "L0_ffn_br", 8), batch_steps=4, gate_cols=8)
            dense_experts(K, "experts0")
        if upto >= 2:
            K.edge_w = sb("edge_w", [P, KT, 4])
            K.score_src, K.score_dst = sb("score_src", [P, NT, 4]), sb("score_dst", [P, NT, 4])
            degree_roots(K)

            def scaled(dve, turn, t, u, ps, tools):
                return dve.tensor_scalar(K.aux[:, t, :], ps[:, 0:D], K.dinv[:, bass.ds(t, 1)], None, ALU.mult)

            def aux_rows(it):
                return K.aux[:, bass.ds(it * UN, UN), :]

            def acc_rows(it):
                return K.acc[:, bass.ds(it * UN, UN), :]

            node_pass(K, "gcn", ["L1_gnn_W1"], [], normed(K), 0, norm=lambda t: K.x[:, t, :], post=scaled,
                      table=(K.node_table, aux_rows))
            edge_sum(K, "sum3", K.node_table, K.src_row, None)

            def gcn_out(dve, turn, t, u, xin, tools):
                turn(dve.tensor_tensor(xin, K.acc[:, t, 0:D], K.aux[:, t, :], ALU.add))
                turn(dve.scalar_tensor_tensor(out=xin, in0=xin, scalar=K.dinv[:, bass.ds(t, 1)],
                                              in1=tools.vec["L1_gnn_b1"][:, :], op0=ALU.mult, op1=ALU.add))
                return dve.tensor_scalar(xin, xin, 0.0, None, ALU.max)

            post, act_post, n = attention_rows(K, 1, "L1_gnn_att_src", "L1_gnn_att_dst")
            node_pass(K, "gat1", ["L1_gnn_W2"], [("L1_gnn_b1", D), ("L1_gnn_att_src", D), ("L1_gnn_att_dst", D)],
                      gcn_out, 2, post=post, post_steps=n, act_post=act_post, table=(K.att_table, acc_rows),
                      ones_cols=ones_of(K, 1))
            edge_weights(K, "score1", 1, NT)
            edge_sum(K, "att1", K.att_table, K.src_row, K.edge_w, heads=1)
            out1 = lambda vec: attention_out(K, 1, vec["L1_gnn_b2"][:, :], True)[0]
            add_to_x(K, "res1", [("L1_gnn_b2", D)], out1, 4)
        if upto >= 3:
            K.pick = sb("pick", [P, 2], I32)
            node_pass(K, "prep1", [], [], normed(K), 0, norm=lambda t: K.x[:, t, :], keep_xt=True, keep_xn=True)
            route_two(K, "route1")

            def load_picked(sp, eo, b, w1, w2, b1, b2, sem):
                e = nc.values_load(K.pick[0:1, b:b + 1], engines=[sp.engine], min_val=0, max_val=7)[0] if False else \
                    nc.values_load(K.pick[0:1, b:b + 1], engines=[sp.engine], min_val=0, max_val=7)
                one = bass.ds(e, 1)
                sp.dma_start(w1, K.inp["L1_ffn_W1"][one, :, :].rearrange("a (c p) n -> p (a c) n", p=P)).then_inc(sem, 16)
                sp.dma_start(w2, K.inp["L1_ffn_W2"][one, :, :].rearrange("a (c p) n -> p (a c) n", p=P)).then_inc(sem, 16)
                sp.dma_start(b1, K.inp["L1_ffn_b1"][one, :].rearrange("a (c p) -> p (a c)", p=P)).then_inc(sem, 16)
                sp.dma_start(b2, K.inp["L1_ffn_b2"][one, :].to_broadcast([P, D])).then_inc(sem, 16)

            wide_experts(K, "ffn1", 1, 2, 4, ACT.Gelu, load_picked, K.aux)
            add_normed(K, "res1b", "L1_ffn_gamma", "L1_ffn_beta")
        if upto >= 4:
            def max_k(dve, turn, t, u, ps, tools):
                h, best = tools.work[:, u, :], tools.work2[:, u, 0:8]
                turn(dve.tensor_tensor(K.x[:, t, :], K.x[:, t, :], ps[:, D:2 * D], ALU.add))
                turn(dve.tensor_copy(h, ps[:, 0:D]))
                for _ in range(MAXK // 8):
                    turn(dve.max(best, h))
                    turn(dve.match_replace(h, best, h, -BIG))
                return dve.scalar_tensor_tensor(out=K.aux[:, t, :], in0=h, scalar=-BIG, in1=ps[:, 0:D],
                                                op0=ALU.is_equal, op1=ALU.mult)

            def mean(dve, turn, t, out, small):
                turn(dve.tensor_scalar(small[:, 0:1], K.degree[:, bass.ds(t, 1)], 1.0, None, ALU.max))
                turn(dve.reciprocal(small[:, 0:1], small[:, 0:1]))
                return dve.tensor_scalar(out, K.acc[:, t, 0:D], small[:, 0:1], None, ALU.mult)

            node_pass(K, "sage", ["L2_gnn_W_neigh", "L2_gnn_W_self"], [], normed(K), 0, norm=lambda t: K.x[:, t, :],
                      post=max_k, post_steps=2 + MAXK // 4, table=(K.node_table, aux_rows))
            edge_sum(K, "sum4", K.node_table, K.src_row, None)
            add_to_x(K, "res2", [], lambda vec: mean, 2)
        if upto >= 5:
            def load_expert(sp, eo, b, w1, w2, b1, b2, sem):
                one = bass.ds(eo * 2 + b, 1)
                sp.dma_start(w1, K.inp["L2_ffn_W1"][one, :, :].rearrange("a (c p) n -> p (a c) n", p=P)).then_inc(sem, 16)
                sp.dma_start(w2, K.inp["L2_ffn_W2"][one, :, :].rearrange("a (c p) n -> p (a c) n", p=P)).then_inc(sem, 16)
                sp.dma_start(b1, K.inp["L2_ffn_b1"][one, :].rearrange("a (c p) -> p (a c)", p=P)).then_inc(sem, 16)
                sp.dma_start(b2, K.inp["L2_ffn_b2"][one, :].to_broadcast([P, D])).then_inc(sem, 16)

            gates, n = top_two_gates(K, "L2_ffn_bg", 8)
            node_pass(K, "prep2", ["L2_ffn_Wg"], [("L2_ffn_bg", 8)], normed(K), 0, norm=lambda t: K.x[:, t, :],
                      keep_xt=True, batch_post=gates, batch_steps=n, gate_cols=8)
            wide_experts(K, "ffn2", 4, 2, 8, ACT.Gelu, load_expert, K.x)
        if upto >= 6:
            LOOPED = 1250 // NPT
            post, act_post, n = attention_rows(K, 4, "L3_gnn_a1_src", "L3_gnn_a1_dst")
            node_pass(K, "gat2", ["L3_gnn_W1"], [("L3_gnn_a1_src", D), ("L3_gnn_a1_dst", D)], normed(K), 0,
                      norm=lambda t: K.x[:, t, :], post=post, post_steps=n, act_post=act_post, table=(K.att_table, acc_rows),
                      ones_cols=ones_of(K, 4))
            edge_weights(K, "score2", 4, LOOPED)
            edge_sum(K, "att2", K.att_table, K.src_row, K.edge_w, heads=4)
            out2 = lambda vec: attention_out(K, 4, vec["L3_gnn_b1"][:, :], False)[0]
            add_to_x(K, "mid", [("L3_gnn_b1", D)], out2, 3, to_aux=True)

            def mid_norm(dve, turn, t, u, xin, tools):
                turn(dve.tensor_scalar(xin, K.aux[:, t, :], tools.mv[:, u, 0:1], tools.mv[:, u, 1:2], ALU.subtract, ALU.mult))
                turn(dve.tensor_tensor(xin, xin, tools.vec["L3_gnn_ln_g"][:, :], ALU.mult))
                turn(dve.tensor_tensor(xin, xin, tools.vec["L3_gnn_ln_b"][:, :], ALU.add))
                return dve.tensor_scalar(xin, xin, 0.0, None, ALU.max)

            post, act_post, n = attention_rows(K, 1, "L3_gnn_a2_src", "L3_gnn_a2_dst")
            node_pass(K, "gat3", ["L3_gnn_W2"], [(f"L3_gnn_{v}", D) for v in ("ln_g", "ln_b", "a2_src", "a2_dst")],
                      mid_norm, 3, norm=lambda t: K.aux[:, t, :], post=post, post_steps=n, act_post=act_post,
                      table=(K.att_table, acc_rows), ones_cols=ones_of(K, 1))
            edge_weights(K, "score3", 1, LOOPED)
            edge_sum(K, "att3", K.att_table, K.src_row, K.edge_w, heads=1)
            out3 = lambda vec: attention_out(K, 1, vec["L3_gnn_b2"][:, :], False)[0]
            add_to_x(K, "res3", [("L3_gnn_b2", D)], out3, 3)
        if upto >= 7:
            K.token_w = sb("token_w", [P, NT])

            def token_weights(dve, turn, it, ps, tools):
                return dve.tensor_tensor(K.token_w[:, bass.ds(it * UN, UN)], ps[:, :, 0],
                                         tools.vec["L3_ffn_br"][:, :].to_broadcast([P, UN]), ALU.add)

            def load_only(sp, eo, b, w1, w2, b1, b2, sem):
                sp.dma_start(w1, K.inp["L3_ffn_w1"].rearrange("(c p) n -> p c n", p=P)).then_inc(sem, 16)
                sp.dma_start(w2, K.inp["L3_ffn_w2"].rearrange("(c p) n -> p c n", p=P)).then_inc(sem, 16)
                sp.dma_start(b1, K.inp["L3_ffn_b1"].rearrange("(c p) -> p c", p=P)).then_inc(sem, 16)
                sp.dma_start(b2, K.inp["L3_ffn_b2"].partition_broadcast(P)).then_inc(sem, 16)

            node_pass(K, "prep3", ["L3_ffn_wr"], [("L3_ffn_br", 1)], normed(K), 0, norm=lambda t: K.x[:, t, :],
                      keep_xt=True, keep_xn=True, batch_post=token_weights, gate_cols=1, gates_exp=False)
            largest_gates(K, "pick", N // 2 - 1)
            wide_experts(K, "ffn3", 1, 1, 8, ACT.Gelu_apprx_tanh, load_only, K.x)
        store(K, out)




def kernel(**inputs):
    import numpy as _np
    import concourse.bacc as _bacc
    from concourse import mybir as _mybir
    from concourse.bass_utils import run_bass_kernel_spmd as _run

    nc = _bacc.Bacc("TRN2", target_bir_lowering=False, num_devices=1)
    arrays, inp = {}, {}
    for name, value in inputs.items():
        if name == "L3_ffn_attention_mask":
            continue
        a = _np.ascontiguousarray(value)
        arrays[f"in_{name}"] = a
        inp[name] = nc.dram_tensor(f"in_{name}", list(a.shape), _mybir.dt.from_np(a.dtype), kind="ExternalInput").ap()
    out = nc.dram_tensor("out_0", [N, D], F32, kind="ExternalOutput").ap()
    build(nc, inp, out)
    r = _run(nc, [arrays], core_ids=[0])
    return r.results[0]["out_0"]
```

```python
from contextlib import ExitStack

import numpy as np
import concourse.bass as bass
from concourse import mybir

ALU = mybir.AluOpType
ACT = mybir.ActivationFunctionType
AX = mybir.AxisListType.X
F32 = mybir.dt.float32
BF16 = mybir.dt.bfloat16
I32 = mybir.dt.int32
U32 = mybir.dt.uint32

P = 128
D = 256
DC = D // P
N = 3125
NPT = 125
NT = N // NPT
NPAD = NT * P
E = 50000
EC = 392
R = 16
G = 4
PAIR = 2
KT = 440
CB = KT // 4
NG = KT // G
RING = 5
UN = 5
TW = D + 4
BIG = float(2 ** 100)
MAXK = 32
TB = 256
NB_X = 32
LN_EPS = 1e-5
assert (E + NT * (PAIR * P - 1)) // (PAIR * P) * PAIR <= KT and NG % RING == 0 and NT % UN == 0


class Chain:

    def __init__(self, eng, sem):
        self.eng, self.sem, self.n = eng, sem, 0

    def __call__(self, ins):
        ins.then_inc(self.sem, 1)
        self.n += 1
        self.eng.wait_ge(self.sem, self.n)


def hold(eng, sem, count):
    eng.wait_ge(sem, count)
    eng.sem_inc(Net.passed[eng.engine], 1)


def start(eng, *sems):
    for sem in sems:
        eng.sem_inc(sem, 1)


def ahead(eng, sem, count):
    hold(eng, sem, count + 1)


class LoopChain:

    def __init__(self, eng, sem, i, per):
        self.eng, self.sem, self.i, self.per, self.n = eng, sem, i, per, 0

    def __call__(self, ins):
        ins.then_inc(self.sem, 1)
        self.n += 1
        hold(self.eng, self.sem, self.i * self.per + self.n)

    def all(self, steps):
        for ins in steps:
            ins.then_inc(self.sem, 1)
        self.n += len(steps)
        hold(self.eng, self.sem, self.i * self.per + self.n)

    def end(self):
        assert self.n == self.per, f"this loop's body makes {self.n} steps, not {self.per}"


class Phase:

    def __init__(self, nc, tag):
        self.nc, self.tag, self.ctx, self.sems = nc, tag, ExitStack(), []

    def __enter__(self):
        return self

    def __exit__(self, *e):
        self.ctx.close()
        with self.nc.Block() as block:
            @block.sync
            def _(sp):
                for sem in self.sems:
                    sp.sem_clear(sem)

    def sb(self, name, shape, dt=F32):
        return self.ctx.enter_context(self.nc.sbuf_tensor(f"{self.tag}_{name}", shape, dt))

    def sem(self, name):
        self.sems.append(self.ctx.enter_context(self.nc.semaphore(f"{self.tag}_{name}")))
        return self.sems[-1]

    def by_rows(self, name, n):
        return [Net.ctx.enter_context(self.nc.semaphore(f"{self.tag}_{name}{h}")) for h in range(n)]

    def block(self):
        return self.ctx.enter_context(self.nc.Block())


class Net:

    passed = {}


def floor125(chain, v, q, tmp, qi, x):
    chain(v.tensor_scalar(qi, x, -62.0, 1.0 / NPT, ALU.add, ALU.mult))
    chain(v.tensor_copy(q, qi))
    chain(v.scalar_tensor_tensor(out=tmp, in0=q, scalar=-float(NPT), in1=x, op0=ALU.mult, op1=ALU.add))
    chain(v.scalar_tensor_tensor(out=q, in0=tmp, scalar=float(NPT), in1=q, op0=ALU.is_ge, op1=ALU.add))
    chain(v.tensor_scalar(tmp, tmp, 0.0, -1.0, ALU.is_lt, ALU.mult))
    chain(v.tensor_tensor(q, q, tmp, ALU.add))


def setup(K):
    nc = K.nc
    with Phase(nc, "setup") as ph:
        loaded, iota_done, consts = ph.sem("loaded"), ph.sem("iota_done"), ph.sem("consts")
        zeroed = ph.sem("zeroed")
        irow = ph.sb("irow", [P, P], I32)
        icol = ph.sb("icol", [P, 1], I32)
        block = ph.block()

        @block.gpsimd
        def _(pool):
            pool.iota(irow[:, :], [[1, P]], base=0, channel_multiplier=0).then_inc(iota_done, 1)
            pool.iota(icol[:, :], [[0, 1]], base=0, channel_multiplier=1).then_inc(iota_done, 1)

        @block.vector
        def _(dve):
            dve.memset(K.x[:, :, :], 0.0).then_inc(zeroed, 1)
            dve.wait_ge(iota_done, 2)
            dve.tensor_copy(K.col_f[:, :], icol[:, :]).then_inc(consts, 1)
            dve.tensor_copy(K.row_f[:, :], irow[:, :]).then_inc(consts, 1)
            dve.tensor_copy(K.row_b[:, :], irow[:, :]).then_inc(consts, 1)
            dve.memset(K.ones[:, :], 1.0).then_inc(consts, 1)
            dve.wait_ge(consts, 4)
            dve.tensor_scalar(K.ident[:, :], K.row_f[:, :], K.col_f[:, 0:1], None, ALU.is_equal).then_inc(consts, 1)
            dve.tensor_scalar(K.ident_b[:, :], K.row_f[:, :], K.col_f[:, 0:1], None, ALU.is_equal).then_inc(consts, 1)
            dve.tensor_scalar(K.before[:, :], K.row_f[:, :], K.col_f[:, 0:1], None, ALU.is_gt).then_inc(consts, 1)

        @block.sync
        def _(sp):
            x_rows = K.inp["x"].rearrange("(t p) d -> p t d", p=NPT)
            sp.wait_ge(zeroed, 1)
            sp.dma_start(K.x[0:112, :, :], x_rows[0:112]).then_inc(loaded, 16)
            sp.dma_start(K.x[112:NPT, :, :], x_rows[112:NPT]).then_inc(loaded, 16)
            sp.wait_ge(loaded, 32)


def sort_edges(K, rec, addr):
    nc = K.nc
    with Phase(nc, "sort") as ph:
        loaded, filled, defaults = ph.sem("loaded"), ph.sem("filled"), ph.sem("defaults")
        step, sums, iota_done = ph.sem("step"), ph.sem("sums"), ph.sem("iota_done")
        lstep, lstep2 = ph.sem("lstep"), ph.sem("lstep2")
        placed = ph.sem("placed")
        dst_i, src_i, et_i, ti = (ph.sb(n, [P, EC], I32) for n in ("dst_i", "src_i", "et_i", "ti"))
        dst, src, bkt, rank, tmp, tmp2, one = (
            ph.sb(n, [P, EC]) for n in ("dst", "src", "bkt", "rank", "tmp", "tmp2", "one"))
        mine, scan = ph.sb("mine", [P, UN, EC]), ph.sb("scan", [P, UN, EC])
        w = ph.sb("w", [P, EC])
        rowtot = ph.sb("rowtot", [P, 2, NT])
        tiles, ends, offs = ph.sb("tiles", [P, NT]), ph.sb("ends", [P, NT]), ph.sb("offs", [P, NT])
        tiles_i = ph.sb("tiles_i", [P, NT], I32)
        kt_i, kt, dt = ph.sb("kt_i", [P, KT], I32), ph.sb("kt", [P, KT]), ph.sb("dt", [P, KT])
        ecol_i, ecol = ph.sb("ecol_i", [P, EC], I32), ph.sb("ecol", [P, EC])
        bnum_i, bnum = ph.sb("bnum_i", [P, NT], I32), ph.sb("bnum", [P, NT])
        rec_sb = ph.sb("rec_sb", [P, KT, 4])
        block = ph.block()
        tail = E - (P - 1) * EC
        ps_tot = K.ps[:, 0, 0:NT]
        ps_before = K.ps[:, 1, 0:NT]

        @block.sync
        def _(sp):
            sp.wait_ge(filled, 5)
            for name, tile in (("dst", dst_i), ("src", src_i), ("edge_type_16", et_i), ("edge_weight1", w)):
                v = K.inp[name]
                v = v.rearrange("e o -> (e o)") if name == "edge_weight1" else v
                whole = v[0:(P - 1) * EC].rearrange("(p j) -> p j", j=EC)
                last = v[(P - 1) * EC:E].rearrange("(p j) -> p j", p=1)
                sp.dma_start(tile[0:P - 1, :], whole).then_inc(loaded, 16)
                sp.dma_start(tile[P - 1:P, 0:tail], last).then_inc(loaded, 16)
            slots = K.rec_dram[0:KT * P, :].rearrange("(p k) c -> p k c", p=P)
            sp.dma_start(slots, rec_sb[:, :, :]).then_inc(defaults, 16)
            sp.wait_ge(defaults, 16)

        @block.gpsimd
        def _(pool):
            pool.iota(kt_i[:, :], [[1, KT]], base=0, channel_multiplier=0).then_inc(iota_done, 1)
            pool.iota(ecol_i[:, :], [[1, EC]], base=0, channel_multiplier=0).then_inc(iota_done, 1)
            pool.iota(bnum_i[:, :], [[1, NT]], base=0, channel_multiplier=0).then_inc(iota_done, 1)

        @block.tensor
        def _(pe):
            pe.wait_ge(placed, 1)
            pe.matmul(ps_tot, K.ones[:, :], rowtot[:, 0, :], start=True, stop=True).then_inc(sums, 1)
            pe.matmul(ps_before, K.before[:, :], rowtot[:, 0, :], start=True, stop=True).then_inc(sums, 1)

        @block.vector
        def _(dve):
            link = Chain(dve, step)
            dve.memset(dst_i[:, :], N).then_inc(filled, 1)
            dve.memset(src_i[:, :], 0).then_inc(filled, 1)
            dve.memset(et_i[:, :], 0).then_inc(filled, 1)
            dve.memset(w[:, :], 0.0).then_inc(filled, 1)
            link(dve.memset(rec_sb[:, :, :], 0.0))
            dve.memset(rec_sb[:, :, 2:3], -1.0).then_inc(filled, 1)
            link(dve.memset(one[:, :], 1.0))
            link(dve.memset(rank[:, :], 0.0))
            dve.wait_ge(iota_done, 3)
            link(dve.tensor_copy(kt[:, :], kt_i[:, :]))
            link(dve.tensor_copy(ecol[:, :], ecol_i[:, :]))
            link(dve.tensor_copy(bnum[:, :], bnum_i[:, :]))
            dve.wait_ge(loaded, 8 * 16)
            link(dve.tensor_copy(dst[:, :], dst_i[:, :]))
            link(dve.tensor_copy(src[:, :], src_i[:, :]))
            floor125(link, dve, bkt[:, :], tmp[:, :], ti[:, :], dst[:, :])
            floor125(link, dve, tmp2[:, :], tmp[:, :], ti[:, :], src[:, :])
            link(dve.scalar_tensor_tensor(out=rec[:, :, 1], in0=tmp2[:, :], scalar=3.0, in1=src[:, :],
                                          op0=ALU.mult, op1=ALU.add))
            link(dve.tensor_copy(tmp[:, :], et_i[:, :]))
            link(dve.scalar_tensor_tensor(out=rec[:, :, 0], in0=rec[:, :, 1], scalar=float(R), in1=tmp[:, :],
                                          op0=ALU.mult, op1=ALU.add))
            link(dve.scalar_tensor_tensor(out=rec[:, :, 2], in0=bkt[:, :], scalar=-float(NPT), in1=dst[:, :],
                                          op0=ALU.mult, op1=ALU.add))
            link(dve.tensor_copy(rec[:, :, 3], w[:, :]))
            with dve.Fori(0, NT // UN) as i:
                turn = LoopChain(dve, lstep, i, 4 * UN + 1)
                turn.all([dve.tensor_scalar(mine[:, u, :], bkt[:, :], bnum[:, bass.ds(i * UN + u, 1)], None, ALU.is_equal)
                          for u in range(UN)])
                turn.all([dve.tensor_tensor_scan(scan[:, u, :], one[:, :], mine[:, u, :], 0.0, ALU.mult, ALU.add)
                          for u in range(UN)])
                turn.all([dve.tensor_copy(rowtot[:, 0, bass.ds(i * UN, UN)], scan[:, :, EC - 1])]
                         + [dve.tensor_tensor(mine[:, u, :], mine[:, u, :], scan[:, u, :], ALU.mult) for u in range(UN)])
                for u in range(UN):
                    turn(dve.tensor_tensor(rank[:, :], rank[:, :], mine[:, u, :], ALU.add))
                turn.end()
            dve.sem_inc(placed, 1)
            dve.wait_ge(sums, 2)
            link(dve.tensor_scalar(tiles_i[:, :], ps_tot, float(PAIR * P - 1), None, ALU.add))
            link(dve.tensor_scalar(tiles_i[:, :], tiles_i[:, :], 8, None, ALU.logical_shift_right))
            link(dve.tensor_scalar(tiles[:, :], tiles_i[:, :], float(PAIR), None, ALU.mult))
            link(dve.tensor_tensor_scan(ends[:, :], one[:, 0:NT], tiles[:, :], 0.0, ALU.mult, ALU.add))
            link(dve.tensor_tensor(offs[:, :], ends[:, :], tiles[:, :], ALU.subtract))
            link(dve.tensor_scalar(offs[:, :], offs[:, :], float(P), -1.0, ALU.mult, ALU.add))
            link(dve.tensor_tensor(offs[:, :], offs[:, :], ps_before, ALU.add))
            with dve.Fori(0, NT // UN) as i:
                turn = LoopChain(dve, lstep2, i, 2 * UN)
                turn.all([dve.tensor_scalar(mine[:, u, :], bkt[:, :], bnum[:, bass.ds(i * UN + u, 1)],
                                            offs[:, bass.ds(i * UN + u, 1)], ALU.is_equal, ALU.mult) for u in range(UN)])
                for u in range(UN):
                    turn(dve.tensor_tensor(rank[:, :], rank[:, :], mine[:, u, :], ALU.add))
                turn.end()
            link(dve.tensor_copy(ti[:, :], rank[:, :]))
            link(dve.tensor_scalar(ti[:, :], ti[:, :], 7, None, ALU.logical_shift_right))
            link(dve.tensor_copy(tmp[:, :], ti[:, :]))
            link(dve.scalar_tensor_tensor(out=rank[:, :], in0=tmp[:, :], scalar=-float(P), in1=rank[:, :],
                                          op0=ALU.mult, op1=ALU.add))
            link(dve.scalar_tensor_tensor(out=rank[:, :], in0=rank[:, :], scalar=float(KT), in1=tmp[:, :],
                                          op0=ALU.mult, op1=ALU.add))
            link(dve.tensor_scalar(ecol[:, :], ecol[:, :], float(KT * P), None, ALU.add))
            link(dve.scalar_tensor_tensor(out=tmp[:, :], in0=bkt[:, :], scalar=float(NT), in1=ecol[:, :],
                                          op0=ALU.is_equal, op1=ALU.mult))
            link(dve.tensor_tensor(rank[:, :], rank[:, :], tmp[:, :], ALU.add))
            link(dve.tensor_copy(addr[:, :], rank[:, :]))
            link(dve.memset(dt[:, :], 0.0))
            with dve.Fori(0, NT - 1) as b:
                hold(dve, step, link.n + b)
                dve.scalar_tensor_tensor(out=dt[:, :], in0=kt[:, :], scalar=ends[:, bass.ds(b, 1)], in1=dt[:, :],
                                         op0=ALU.is_ge, op1=ALU.add).then_inc(step, 1)
            dve.wait_ge(step, link.n + NT - 1)
            dve.tensor_copy(K.tile_of[:, :], dt[:, :])

def edge_rows(K):
    nc = K.nc
    with Phase(nc, "edge_rows") as ph:
        step, turned, copied, stored = (ph.sem(n) for n in ("step", "turned", "copied", "stored"))
        loaded, taken = ph.sem("loaded"), ph.sem("taken")
        s_last, s_last_t, s_last_of, s_counted = (ph.sem(n) for n in ("last", "last_t", "last_of", "counted"))
        rec_sb = ph.sb("rec_sb", [P, KT, 4])
        last = ph.sb("last", [NT, KT], BF16)
        whole, src_p = ph.sb("whole", [P, KT], I32), ph.sb("src_p", [P, KT])
        out = ph.sb("out", [CB, 2, 4, P], BF16)
        block = ph.block()
        ps_last = K.ps[0:CB, 0, :].bitcast(BF16)[:, 0:4 * 32].rearrange("p (c t) -> p c t", t=32)[:, :, 0:NT]
        ps_count = K.ps[:, 1, 0:NT]

        @block.vector
        def _(dve):
            dve.wait_ge(loaded, 16)
            dve.tensor_copy(K.rel_row[:, :], rec_sb[:, :, 0]).then_inc(taken, 1)
            dve.tensor_copy(K.src_row[:, :], rec_sb[:, :, 1]).then_inc(taken, 1)
            dve.tensor_copy(K.slot_dst[:, :], rec_sb[:, :, 2]).then_inc(taken, 1)
            dve.tensor_copy(K.slot_w[:, :], rec_sb[:, :, 3]).then_inc(taken, 1)
            dve.wait_ge(taken, 4)
            link = Chain(dve, step)
            link(dve.tensor_scalar(whole[:, :], K.src_row[:, :], 7, None, ALU.logical_shift_right))
            link(dve.tensor_copy(K.src_tile[:, :], whole[:, :]))
            link(dve.tensor_copy(src_p[:, :], K.src_row[:, :]))
            link(dve.scalar_tensor_tensor(out=src_p[:, :], in0=K.src_tile[:, :], scalar=-float(P), in1=src_p[:, :],
                                          op0=ALU.mult, op1=ALU.add))
            link(dve.tensor_copy(K.tile_f[:, :], K.tile_of[:, :]))
            link(dve.tensor_scalar(K.in_tile[:, :], K.tile_f[0:NT, :], K.col_f[0:NT, 0:1], None, ALU.is_equal))
            link(dve.memset(last[:, KT - 1:KT], 0.0))
            link(dve.tensor_tensor(last[:, 0:KT - 1], K.in_tile[:, 0:KT - 1], K.in_tile[:, 1:KT], ALU.mult))
            dve.tensor_tensor(last[:, :], K.in_tile[:, :], last[:, :], ALU.subtract).then_inc(s_last, 1)
            for i in range(2):
                for c in range(4):
                    dve.wait_ge(turned, i * 4 + c + 1)
                    dve.tensor_copy(out[:, i, c, :], K.ps[0:CB, i * 4 + c, 0:P]).then_inc(copied, 1)
            dve.wait_ge(s_last_t, 1)
            dve.tensor_copy(K.last_of[:, :, :], ps_last).then_inc(s_last_of, 1)
            dve.wait_ge(s_counted, 1)
            dve.tensor_scalar(K.no_edge[:, :], ps_count, -1.0, BIG, ALU.add, ALU.mult)

        @block.tensor
        def _(pe):
            pe.wait_ge(taken, 4)
            pe.wait_ge(step, 4)
            for i, rows in enumerate((src_p, K.slot_dst)):
                for c in range(4):
                    pe.transpose(K.ps[0:CB, i * 4 + c, 0:P], rows[:, c * CB:(c + 1) * CB], K.ident[:, :]).then_inc(turned, 1)
            pe.wait_ge(s_last, 1)
            pe.wait_ge(copied, 8)
            for c in range(4):
                mm = pe.transpose(ps_last[:, c, :], last[:, c * CB:(c + 1) * CB], K.ident_b[0:NT, 0:NT])
            mm.then_inc(s_last_t, 1)
            pe.wait_ge(s_last_of, 1)
            for c in range(4):
                mm = pe.matmul(ps_count, K.ones[0:CB, :], K.last_of[:, c, :], start=c == 0, stop=c == 3)
            mm.then_inc(s_counted, 1)

        @block.sync
        def _(sp):
            slots = K.rec_dram[0:KT * P, :].rearrange("(p k) c -> p k c", p=P)
            sp.dma_start(rec_sb[:, :, :], slots).then_inc(loaded, 16)
            sp.wait_ge(copied, 8)
            for i in range(2):
                sp.dma_start(K.pair_rows[i].rearrange("(c k) e -> k c e", k=CB), out[:, i, :, :]).then_inc(stored, 16)
            sp.wait_ge(stored, 32)


def row_stats(turn, v, stats, mv, xs):
    turn.all([v.bn_stats(stats[:, u, :], x) for u, x in enumerate(xs)])
    turn.all([v.bn_aggr(mv[:, u, :], stats[:, u, :]) for u in range(len(xs))])


def relation_tables(K, tag, w_name, loop_name, pre, pre_steps, norm, scatter=None):
    nc = K.nc
    U = 14
    with Phase(nc, tag) as ph:
        loaded, prep, dchain = ph.sem("loaded"), ph.sem("prep"), ph.sem("dchain")
        s_pre, s_tr, s_xt, s_mm = ph.sem("pre"), ph.sem("tr"), ph.sem("xt"), ph.sem("mm")
        ev_act, ev_dve, s_stored = ph.sem("ev_act"), ph.sem("ev_dve"), ph.sem("stored")
        w_rel = ph.sb("w_rel", [P, DC, R, 2])
        diag = ph.sb("diag", [P, DC, R, P])
        pair_i, pair_c, mask = ph.sb("pair_i", [P, P], I32), ph.sb("pair_c", [P, 1], I32), ph.sb("mask", [P, P])
        pair_f, pair_cf = ph.sb("pair_f", [P, P]), ph.sb("pair_cf", [P, 1])
        w_loop = ph.sb("w_loop", [P, DC, D])
        bias = ph.sb("bias", [P, D])
        xin, xt = ph.sb("xin", [P, UN, D]), ph.sb("xt", [P, UN, DC, P])
        stage = ph.sb("stage", [P, UN, R, DC, P])
        stats, mv = ph.sb("stats", [P, UN, 6]), ph.sb("mv", [P, UN, 2])
        s_var, s_rstd, s_free = ph.sem("var"), ph.sem("rstd"), ph.sem("free")
        if scatter is not None:
            scattered, s_ring = ph.by_rows("scattered", 2), ph.sem("ring")
            ring_rec, ring_addr = ph.sb("ring_rec", [P, 2, U, 4]), ph.sb("ring_addr", [P, 2, U], I32)
        block = ph.block()

        NQ = 9
        RG = R // 4
        ps_t = [K.ps[:, 0, 0:D], K.ps[:, 1, 0:D]]
        banks = [2, 3, 4, 5]

        @block.sync
        def _(sp):
            w = K.inp[w_name]
            with nc.allow_non_contiguous_dma(reason="small weights by block rows"):
                for c in range(DC):
                    sp.dma_start(w_rel[:, c, :, :], w.rearrange("r (c b) i o -> c (b i) r o", c=DC)[c]).then_inc(loaded, 16)
            sp.dma_start(w_loop[:, :, :], K.inp[loop_name].rearrange("(c p) n -> p c n", p=P)).then_inc(loaded, 16)
            sp.dma_start(bias[:, :], K.inp["L0_gnn_b1"].partition_broadcast(P)).then_inc(loaded, 16)
            start(sp, s_free)
            with sp.Fori(0, NT // UN) as it:
                for u in range(UN):
                    t = it * UN + u
                    ahead(sp, ev_act, (t + 1) * 4)
                    ahead(sp, ev_dve, (t + 1) * 5)
                    sp.dma_start(K.rel_table[bass.ds(t * P, P), :, :].rearrange("p r f -> p (r f)"),
                                 stage[:, u, :, :, :].rearrange("p r c f -> p (r c f)")).then_inc(s_stored, 16)
                hold(sp, s_stored, (it + 1) * (UN * 16))
                sp.sem_inc(s_free, 1)
            sp.wait_ge(s_stored, NT * 16)
            if scatter is not None:
                for h in range(2):
                    sp.wait_ge(scattered[h], EC // 2 * 16)

        @block.vector
        def _(dve):
            start(dve, ev_dve)
            link = Chain(dve, prep)
            link(dve.tensor_copy(pair_i[:, :], K.row_f[:, :]))
            link(dve.tensor_scalar(pair_i[:, :], pair_i[:, :], 1, None, ALU.logical_shift_right))
            link(dve.tensor_copy(pair_f[:, :], pair_i[:, :]))
            link(dve.tensor_copy(pair_c[:, :], K.col_f[:, :]))
            link(dve.tensor_scalar(pair_c[:, :], pair_c[:, :], 1, None, ALU.logical_shift_right))
            link(dve.tensor_copy(pair_cf[:, :], pair_c[:, :]))
            link(dve.tensor_scalar(mask[:, :], pair_f[:, :], pair_cf[:, 0:1], None, ALU.is_equal))
            dve.wait_ge(loaded, 64)
            for c in range(DC):
                link(dve.tensor_tensor(
                    diag[:, c, :, :].rearrange("p r (b o) -> p r b o", o=2),
                    w_rel[:, c, :, :].unsqueeze(2).to_broadcast([P, R, P // 2, 2]),
                    mask[:, :].rearrange("p (b o) -> p b o", o=2).unsqueeze(1).to_broadcast([P, R, P // 2, 2]),
                    ALU.mult))
            prep_done = link.n
            with dve.Fori(0, NT // UN) as it:
                turn = LoopChain(dve, dchain, it, pre_steps)
                if norm:
                    row_stats(turn, dve, stats, mv, [K.x[:, it * UN + u, :] for u in range(UN)])
                    dve.tensor_scalar(mv[:, :, 1], mv[:, :, 1], LN_EPS, None, ALU.add).then_inc(s_var, 1)
                    hold(dve, s_rstd, it + 1)
                    turn(dve.reciprocal(mv[:, :, 1], mv[:, :, 1]))
                for u in range(UN):
                    pre(dve, turn, it * UN + u, u, xin[:, u, :], mv, bias).then_inc(s_pre, 1)
                for u in range(UN):
                    t = it * UN + u
                    ahead(dve, s_free, it)
                    for q in (1, 3, 5, 7, 8):
                        ahead(dve, s_mm, t * NQ + q + 1)
                        if q < 8:
                            rg, c = q // 2, q % 2
                            out = stage[:, u, rg * 4:rg * 4 + 4, c, :]
                            ps = K.ps[:, banks[q % 4], :].rearrange("p (r f) -> p r f", r=4)
                        else:
                            out, ps = K.loop_out[:, t, :], K.ps[:, 6, 0:D]
                        dve.tensor_copy(out, ps).then_inc(ev_dve, 1)
                turn.end()

        @block.scalar
        def _(act):
            start(act, s_xt, ev_act)
            with act.Fori(0, NT // UN) as it:
                if norm:
                    hold(act, s_var, it + 1)
                    act.sqrt(mv[:, :, 1], mv[:, :, 1]).then_inc(s_rstd, 1)
                for u in range(UN):
                    t = it * UN + u
                    hold(act, s_tr, t + 1)
                    if u == 0:
                        ahead(act, s_mm, it * (UN * NQ))
                    act.copy(xt[:, u, :, :], ps_t[u % 2].rearrange("p (c f) -> p c f", c=DC)).then_inc(s_xt, 1)
                    if u == 0:
                        ahead(act, s_free, it)
                    for q in (0, 2, 4, 6):
                        ahead(act, s_mm, t * NQ + q + 1)
                        rg, c = q // 2, q % 2
                        act.copy(stage[:, u, rg * 4:rg * 4 + 4, c, :],
                                 K.ps[:, banks[q % 4], :].rearrange("p (r f) -> p r f", r=4)).then_inc(ev_act, 1)

        if scatter is not None:
            rec, addr = scatter

            @block.gpsimd
            def _(pool):
                def store(i, h):
                    part = bass.ds((i * 2 + h) * U, U)
                    pool.tensor_copy(ring_rec[:, h, :, :], rec[:, part, :]).then_inc(s_ring, 1)
                    pool.tensor_copy(ring_addr[:, h, :], addr[:, part]).then_inc(s_ring, 1)
                    hold(pool, s_ring, (i * 2 + h + 1) * 2)
                    for u in range(U):
                        pool.indirect_dma_start(
                            K.rec_dram, bass.IndirectOffsetOnAxis(ring_addr[:, h, u:u + 1], 0),
                            ring_rec[:, h, u, :], None).then_inc(scattered[h], 16)

                for h in range(2):
                    store(0, h)
                with pool.Fori(1, EC // (2 * U)) as i:
                    for h in range(2):
                        hold(pool, scattered[h], i * (U * 16))
                        store(i, h)

        @block.tensor
        def _(pe):
            start(pe, s_mm)
            pe.wait_ge(prep, 7 + DC)
            pe.wait_ge(loaded, 64)
            with pe.Fori(0, NT // UN) as it:
                for u in range(UN):
                    t = it * UN + u
                    hold(pe, s_pre, t + 1)
                    ahead(pe, s_xt, t)
                    for c in range(DC):
                        mm = pe.transpose(ps_t[u % 2][:, c * P:(c + 1) * P], xin[:, u, c * P:(c + 1) * P], K.ident[:, :])
                    mm.then_inc(s_tr, 1)
                    ahead(pe, s_xt, t + 1)
                    for q in range(NQ - 1):
                        rg, c = q // 2, q % 2
                        if q >= 4:
                            ahead(pe, *((ev_act, t * 4 + q // 2 - 1) if q % 2 == 0 else (ev_dve, t * 5 + q // 2 - 1)))
                        else:
                            ahead(pe, *((ev_act, t * 4) if q % 2 == 0 else (ev_dve, t * 5)))
                        pe.matmul(K.ps[:, banks[q % 4], :], xt[:, u, c, :],
                                  diag[:, c, rg * 4:rg * 4 + 4, :].rearrange("p r f -> p (r f)"),
                                  start=True, stop=True).then_inc(s_mm, 1)
                    for c in range(DC):
                        mm = pe.matmul(K.ps[:, 6, 0:D], xt[:, u, c, :], w_loop[:, c, :], start=c == 0, stop=c == DC - 1)
                    mm.then_inc(s_mm, 1)


def edge_sum(K, tag, table, rows, weights, count=False, heads=0):
    nc = K.nc
    SLOTS = RING * G
    GP = G // PAIR
    BANKS = RING
    W = heads * (D // heads + 1) if heads else D
    TCOLS = TW if heads else D
    with Phase(nc, tag) as ph:
        zeroed, s_idx, s_hot, s_mm, s_acc = (ph.sem(n) for n in ("zeroed", "idx", "hot", "mm", "acc"))
        s_one, s_deg = ph.sem("one"), ph.sem("deg")
        gathered = ph.by_rows("gathered", RING)
        ring_idx = ph.sb("ring_idx", [P, RING, G], I32)
        rows_in = ph.sb("rows_in", [P, RING, G, TCOLS])
        hot = ph.sb("hot", [P, RING, G, P])
        hot_b, one_b = ph.sb("hot_b", [P, RING, G, P], BF16), ph.sb("one_b", [P, 1], BF16)
        msg = ph.sb("msg", [P, RING, G, W]) if heads > 1 else rows_in
        block = ph.block()
        per = 2 if count or heads > 1 else 1

        @block.scalar
        def _(act):
            with act.Fori(0, NG // RING) as it:
                for b in range(RING):
                    g = it * RING + b
                    hold(act, s_mm, (g + 1) * G)
                    act.copy(ring_idx[:, b, :], rows[:, bass.ds(g * G, G)]).then_inc(s_idx, 1)

        @block.gpsimd
        def _(pool):
            if count:
                pool.memset(one_b[:, :], 1.0).then_inc(s_one, 1)
            with pool.Fori(0, NG // RING) as it:
                for b in range(RING):
                    g = it * RING + b
                    hold(pool, s_idx, g + 1)
                    hold(pool, s_mm, (g + 1) * G)
                    for u in range(G):
                        pool.indirect_dma_start(rows_in[:, b, u, :], None, table,
                                                bass.IndirectOffsetOnAxis(ring_idx[:, b, u:u + 1], 0)
                                                ).then_inc(gathered[b], 16)

        def one_hot(dve, it, b):
            g = it * RING + b
            hold(dve, s_mm, (g + 1) * G)
            if heads > 1:
                hold(dve, gathered[b], (it + 1) * (16 * G))
            for u in range(G):
                k = g * G + u
                dst = K.slot_dst[:, bass.ds(k, 1)]
                if weights is None or heads > 1:
                    ins = dve.tensor_scalar(hot[:, b, u, :], K.row_f[:, :], dst, None, ALU.is_equal)
                else:
                    w = weights[:, bass.ds(k, 1), 0] if heads else weights[:, bass.ds(k, 1)]
                    ins = dve.tensor_scalar(hot[:, b, u, :], K.row_f[:, :], dst, w, ALU.is_equal, ALU.mult)
                ins.then_inc(s_hot, 1)
                if heads > 1:
                    wide = weights[:, bass.ds(k, 1), :].rearrange("p a h -> p (a h)").unsqueeze(2).to_broadcast([P, heads, W // heads])
                    dve.tensor_tensor(heads_of(msg[:, b, u, :], heads), heads_of(rows_in[:, b, u, :], heads), wide,
                                      ALU.mult).then_inc(s_hot, 1)
                if count:
                    dve.tensor_scalar(hot_b[:, b, u, :], K.row_b[:, :], dst, None, ALU.is_equal).then_inc(s_hot, 1)

        def add(dve, it, b):
            g = it * RING + b
            for q in range(GP):
                n = g * GP + q
                bank = (b * GP + q) % BANKS
                tile = nc.values_load(K.tile_of[0:1, bass.ds(g * G + q * PAIR, 1)], engines=[dve.engine], min_val=0,
                                      max_val=NT - 1, skip_runtime_bounds_check_because="it counts NT - 1 comparisons")
                hold(dve, s_mm, n * PAIR + PAIR + SLOTS)
                hold(dve, s_acc, n + BANKS)
                dve.tensor_tensor(K.acc[:, tile, 0:W], K.acc[:, tile, 0:W], K.ps[:, bank, 0:W], ALU.add).then_inc(s_acc, 1)
                if count:
                    hold(dve, s_deg, n + BANKS)
                    dve.tensor_tensor(K.degree[:, bass.ds(tile, 1)], K.degree[:, bass.ds(tile, 1)],
                                      K.ps[:, bank, D:D + 1], ALU.add).then_inc(s_deg, 1)

        @block.vector
        def _(dve):
            dve.sem_inc(s_acc, BANKS)
            dve.sem_inc(s_deg, BANKS)
            if not heads:
                dve.memset(K.acc[:, :, :], 0.0).then_inc(zeroed, 1)
                if count:
                    dve.memset(K.degree[:, :], 0.0).then_inc(zeroed, 1)
                dve.wait_ge(zeroed, 2 if count else 1)
            with dve.Fori(0, NG // RING) as it:
                ahead = 2 if heads > 1 else RING
                for b in range(RING + ahead):
                    if b < RING:
                        one_hot(dve, it, b)
                    if b >= ahead:
                        add(dve, it, b - ahead)

        @block.tensor
        def _(pe):
            pe.sem_inc(s_mm, SLOTS)
            if count:
                pe.wait_ge(s_one, 1)
            with pe.Fori(0, NG // RING) as it:
                for b in range(RING):
                    g = it * RING + b
                    hold(pe, gathered[b], (it + 1) * (16 * G))
                    hold(pe, s_hot, (g + 1) * (G * per))
                    for q in range(GP):
                        n = g * GP + q
                        bank = (b * GP + q) % BANKS
                        hold(pe, s_acc, n + 1)
                        if count:
                            hold(pe, s_deg, n + 1)
                        for i in range(PAIR):
                            u = q * PAIR + i
                            mm = pe.matmul(K.ps[:, bank, 0:W], hot[:, b, u, :], msg[:, b, u, 0:W],
                                           start=i == 0, stop=i == PAIR - 1)
                            if not count:
                                mm.then_inc(s_mm, 1)
                        for i in range(PAIR if count else 0):
                            u = q * PAIR + i
                            pe.matmul(K.ps[:, bank, D:D + 1], hot_b[:, b, u, :], one_b[:, :], start=i == 0,
                                      stop=i == PAIR - 1, skip_group_check=True).then_inc(s_mm, 1)


def node_pass(K, tag, w_names, vectors, pre, pre_steps, norm=None, post=None, post_steps=0, act_post=None,
              table=None, keep_xt=False, keep_xn=False, batch_post=None, batch_steps=0, gate_cols=0, gates_exp=True,
              ones_cols=None):
    nc = K.nc
    wide = D * len(w_names) if w_names and not gate_cols else gate_cols
    with Phase(nc, tag) as ph:
        loaded, s_stored = ph.sem("loaded"), ph.sem("stored")
        dchain, bchain, s_var, s_rstd = ph.sem("dchain"), ph.sem("bchain"), ph.sem("var"), ph.sem("rstd")
        s_pre, s_tr, s_xt, s_mm = ph.sem("pre"), ph.sem("tr"), ph.sem("xt"), ph.sem("mm")
        s_ones = ph.sem("ones")
        s_post, s_apost, s_kept, s_exp = ph.sem("post"), ph.sem("apost"), ph.sem("kept"), ph.sem("exp")
        w_sb = ph.sb("w", [P, DC, max(wide, 1)])
        vec = {n: ph.sb(f"vec_{n}", [P, c]) for n, c in vectors}
        xin, xt = ph.sb("xin", [P, UN, D]), ph.sb("xt", [P, UN, DC, P])
        stats, mv = ph.sb("stats", [P, UN, 6]), ph.sb("mv", [P, UN, 2])
        tools = Net()
        tools.vec, tools.mv, tools.ph, tools.xin = vec, mv, ph, xin
        tools.s_exp, tools.s_sum = s_exp, ph.sem("sum")
        tools.work = ph.sb("work", [P, UN, D])
        tools.work2 = ph.sb("work2", [P, UN, 64])
        tools.small = ph.sb("small", [P, UN, 4])
        block = ph.block()
        n_loads = (len(w_names) + len(vectors)) * 16
        ps_t = [K.ps[:, 0, 0:D], K.ps[:, 1, 0:D]]
        ps_y = [K.ps[:, 2 + u, :] for u in range(UN)]
        has_post, has_act, products = post is not None, act_post is not None, bool(w_names)
        copy_xt = keep_xt and products

        @block.sync
        def _(sp):
            for n, name in enumerate(w_names):
                cols = wide // len(w_names)
                with nc.allow_non_contiguous_dma(reason="a weight vector by partitions"):
                    sp.dma_start(w_sb[:, :, n * cols:(n + 1) * cols],
                                 K.inp[name].rearrange("(c p) n -> p c n", p=P)).then_inc(loaded, 16)
            for name, c in vectors:
                v = K.inp[name]
                v = v.rearrange("h f -> (h f)") if len(v.shape) == 2 else v
                sp.dma_start(vec[name][:, :], v.partition_broadcast(P)).then_inc(loaded, 16)
            if table is not None:
                rows, ready = table
                if ones_cols is not None:
                    sp.wait_ge(s_ones, 1)
                with sp.Fori(0, NT // UN) as it:
                    if has_post:
                        ahead(sp, s_post, (it + 1) * UN)
                    if has_act:
                        ahead(sp, s_apost, (it + 1) * UN)
                    sp.dma_start(rows[bass.ds(it * (UN * P), UN * P), :].rearrange("(t p) f -> p t f", p=P),
                                 ready(it)).then_inc(s_stored, 16)
                sp.wait_ge(s_stored, NT // UN * 16)

        @block.vector
        def _(dve):
            start(dve, s_post)
            if ones_cols is not None:
                dve.memset(ones_cols, 1.0).then_inc(s_ones, 1)
            if n_loads:
                dve.wait_ge(loaded, n_loads)

            def front(it):
                turn = LoopChain(dve, dchain, it, pre_steps + (2 * UN + 1) * (norm is not None))
                if norm is not None:
                    row_stats(turn, dve, stats, mv, [norm(it * UN + u) for u in range(UN)])
                    dve.tensor_scalar(mv[:, :, 1], mv[:, :, 1], LN_EPS, None, ALU.add).then_inc(s_var, 1)
                    hold(dve, s_rstd, it + 1)
                    turn(dve.reciprocal(mv[:, :, 1], mv[:, :, 1]))
                if not isinstance(it, int):
                    hold(dve, s_tr, it * UN)
                if keep_xn:
                    ahead(dve, s_kept, it * (UN * 2 if copy_xt else UN))
                if pre_steps:
                    pre(dve, turn, it, xin[:, :, :], tools).then_inc(s_pre, UN)
                else:
                    for u in range(UN):
                        pre(dve, turn, it * UN + u, u, xin[:, u, :], tools).then_inc(s_pre, 1)
                turn.end()

            def back(it):
                turn = LoopChain(dve, bchain, it, post_steps + batch_steps)
                if has_post:
                    ahead(dve, s_post, it * UN)
                    if post_steps:
                        ahead(dve, s_mm, it * UN + UN)
                        post(dve, turn, it, K.ps[:, 2:2 + UN, 0:wide], tools).then_inc(s_post, UN)
                    else:
                        for u in range(UN):
                            ahead(dve, s_mm, it * UN + u + 1)
                            post(dve, turn, it * UN + u, u, ps_y[u], tools).then_inc(s_post, 1)
                if batch_post is not None:
                    ahead(dve, s_mm, it * UN + UN)
                    batch_post(dve, turn, it, K.ps[:, 2:2 + UN, 0:gate_cols], tools).then_inc(s_post, 1)
                turn.end()

            front(0)
            with dve.Fori(1, NT // UN) as it:
                front(it)
                back(it - 1)
            back(NT // UN - 1)

        @block.scalar
        def _(act):
            start(act, s_xt, s_apost)

            def front(it):
                if norm is not None:
                    hold(act, s_var, it + 1)
                    act.sqrt(mv[:, :, 1], mv[:, :, 1]).then_inc(s_rstd, 1)
                for u in range(UN):
                    t = it * UN + u
                    hold(act, s_tr, t + 1)
                    if u == 0:
                        if products:
                            ahead(act, s_mm, it * UN)
                        if copy_xt:
                            ahead(act, s_kept, it * (UN * 2 if keep_xn else UN))
                    to = xt[:, u, :, :] if products else K.xt[:, :, bass.ds(t * P, P)]
                    act.copy(to, ps_t[u % 2].rearrange("p (c f) -> p c f", c=DC)).then_inc(s_xt, 1)

            def back(it):
                if has_act:
                    for u in range(UN):
                        ahead(act, *((s_post, it * UN + u + 1) if has_post else (s_mm, it * UN + u + 1)))
                        act_post(act, it * UN + u, u, ps_y[u], tools).then_inc(s_apost, 1)
                if batch_post is not None and gates_exp:
                    hold(act, tools.s_sum, it + 1)
                    act.activation(tools.work2[:, :, 0:gate_cols], tools.work2[:, :, 0:gate_cols], ACT.Exp).then_inc(s_exp, 1)

            front(0)
            with act.Fori(1, NT // UN) as it:
                front(it)
                back(it - 1)
            back(NT // UN - 1)

        if copy_xt or keep_xn:
            @block.gpsimd
            def _(pool):
                start(pool, s_kept)
                with pool.Fori(0, NT // UN) as it:
                    for u in range(UN):
                        t = it * UN + u
                        if keep_xn:
                            hold(pool, s_pre, t + 1)
                            pool.tensor_copy(K.aux[:, t, :], xin[:, u, :]).then_inc(s_kept, 1)
                        if copy_xt:
                            ahead(pool, s_xt, t + 1)
                            pool.tensor_copy(K.xt[:, :, bass.ds(t * P, P)], xt[:, u, :, :]).then_inc(s_kept, 1)

        @block.tensor
        def _(pe):
            start(pe, s_mm)
            if n_loads:
                pe.wait_ge(loaded, n_loads)
            with pe.Fori(0, NT // UN) as it:
                for u in range(UN):
                    t = it * UN + u
                    hold(pe, s_pre, t + 1)
                    ahead(pe, s_xt, t - 1 if u > 1 else it * UN)
                    for c in range(DC):
                        mm = pe.transpose(ps_t[u % 2][:, c * P:(c + 1) * P], xin[:, u, c * P:(c + 1) * P], K.ident[:, :])
                    mm.then_inc(s_tr, 1)
                for u in range(UN if products else 0):
                    ahead(pe, s_xt, it * UN + u + 1)
                    if u == 0:
                        if has_post:
                            ahead(pe, s_post, it * UN)
                        if has_act:
                            ahead(pe, s_apost, it * UN)
                        if batch_post is not None:
                            ahead(pe, s_post, it)
                    for c in range(DC):
                        mm = pe.matmul(ps_y[u][:, 0:wide], xt[:, u, c, :], w_sb[:, c, :], start=c == 0, stop=c == DC - 1)
                    mm.then_inc(s_mm, 1)


def normed(K):
    def pre(dve, turn, t, u, xin, tools):
        return dve.tensor_scalar(xin, K.x[:, t, :], tools.mv[:, u, 0:1], tools.mv[:, u, 1:2], ALU.subtract, ALU.mult)
    return pre


def softmax_gates(K, bias_name, cols):
    def batch(dve, turn, it, ps, tools):
        logits = tools.work2[:, :, 0:cols]
        top = tools.small[:, :, 0]
        b = tools.vec[bias_name][:, :].unsqueeze(1).to_broadcast([P, UN, cols])
        turn(dve.tensor_tensor(logits, ps, b, ALU.add))
        turn(dve.tensor_reduce(top, logits, AX, ALU.max))
        dve.tensor_tensor(logits, logits, top.unsqueeze(2).to_broadcast([P, UN, cols]), ALU.subtract).then_inc(tools.s_sum, 1)
        hold(dve, tools.s_exp, it + 1)
        turn(dve.tensor_reduce(top, logits, AX, ALU.add))
        turn(dve.reciprocal(top, top))
        return dve.tensor_tensor(K.gate[:, bass.ds(it * UN, UN), :], logits, top.unsqueeze(2).to_broadcast([P, UN, cols]), ALU.mult)
    return batch


def dense_experts(K, tag):
    nc = K.nc
    NE = 8
    CH = UN * P
    HF = CH // 2
    with Phase(nc, tag) as ph:
        consts, prep, turned = ph.sem("consts"), ph.sem("prep"), ph.sem("turned")
        w_in = [ph.sem("w_in0"), ph.sem("w_in1")]
        s_one, s_h1, s_two, s_h2, s_out, s_add = (ph.sem(n) for n in ("one", "h1", "two", "h2", "out", "add"))
        s_bias, s_root = ph.sem("bias"), ph.sem("root")
        w1, w2, wo = (ph.sb(n, [P, 2, DC, D]) for n in ("w1", "w2", "wo"))
        bo, y = ph.sb("bo", [P, NE, D]), ph.sb("y", [P, 2, D])
        raw = ph.sb("raw", [P, P])
        raw2 = ph.sb("raw2", [32, P])
        cst = ph.sb("cst", [P, 10, NE, DC])
        h1 = ph.sb("h1", [P, 2, DC, HF])
        h2 = ph.sb("h2", [P, DC, CH])
        block = ph.block()
        ES = NE * DC
        order = ["b1", "g1", "be1", "m1", "v1", "b2", "g2", "be2", "m2", "v2"]
        B = {n: cst[:, i, :, :] for i, n in enumerate(order)}
        ps_one = [[K.ps[:, 0, 0:HF], K.ps[:, 1, 0:HF]], [K.ps[:, 2, 0:HF], K.ps[:, 3, 0:HF]]]
        ps_two = [[K.ps[:, 4, 0:HF], K.ps[:, 5, 0:HF]], [K.ps[:, 6, 0:HF], K.ps[:, 7, 0:HF]]]
        ps_out = [K.ps[:, 2, 0:D], K.ps[:, 3, 0:D]]
        NCH = NT // UN

        @block.sync
        def _(sp):
            for i, n in enumerate(order):
                rows = K.inp[f"L0_ffn_{n}"].rearrange("e (c p) -> (e c) p", p=P)
                dst = raw[i * ES:(i + 1) * ES, :] if i < 8 else raw2[(i - 8) * ES:(i - 7) * ES, :]
                sp.dma_start(dst, rows).then_inc(consts, 16)
            sp.dma_start(bo[:, :, :].rearrange("p e d -> p (e d)"),
                         K.inp["L0_ffn_bo"].rearrange("e d -> (e d)").partition_broadcast(P)).then_inc(consts, 16)
            with sp.Fori(0, NE // 2) as eo:
                for b in range(2):
                    ahead(sp, s_out, eo * (2 * NT) if b == 0 else eo * (2 * NT))
                    for name, w in (("W1", w1), ("W2", w2), ("Wo", wo)):
                        sp.dma_start(w[:, b, :, :], K.inp[f"L0_ffn_{name}"][bass.ds(eo * 2 + b, 1), :, :].rearrange(
                            "a (c p) n -> p (a c) n", p=P)).then_inc(w_in[b], 16)

        @block.vector
        def _(dve):
            start(dve, s_add, s_bias)
            link = Chain(dve, prep)
            dve.wait_ge(turned, 2)
            flat = cst[:, :, :, :].rearrange("p a e c -> p (a e c)")
            link(dve.tensor_copy(flat[:, 0:8 * ES], K.ps[:, 0, 0:P]))
            link(dve.tensor_copy(flat[:, 8 * ES:10 * ES], K.ps[:, 1, 0:2 * ES]))
            for g, b, be, m, v in (("g1", "b1", "be1", "m1", "v1"), ("g2", "b2", "be2", "m2", "v2")):
                link(dve.tensor_scalar(B[v], B[v], 1e-3, None, ALU.add))
            dve.wait_ge(s_root, 2)
            for g, b, be, m, v in (("g1", "b1", "be1", "m1", "v1"), ("g2", "b2", "be2", "m2", "v2")):
                link(dve.reciprocal(B[v], B[v]))
                link(dve.tensor_tensor(B[g], B[g], B[v], ALU.mult))
                link(dve.tensor_tensor(B[b], B[b], B[m], ALU.subtract))
                link(dve.tensor_tensor(B[b], B[b], B[g], ALU.mult))
                link(dve.tensor_tensor(B[be], B[be], B[b], ALU.add))
            with dve.Fori(0, NE) as e:
                with dve.Fori(0, NCH) as ch:
                    n = e * NT + ch * UN
                    for u in range(UN):
                        t = ch * UN + u
                        ahead(dve, s_out, n + u + 1)
                        ahead(dve, s_add, n + u - 1 if u else n)
                        dve.tensor_tensor(y[:, u % 2, :], ps_out[u % 2], bo[:, bass.ds(e, 1), :].rearrange("p a d -> p (a d)"),
                                          ALU.add).then_inc(s_bias, 1)
                        ahead(dve, s_bias, n + u + 1)
                        dve.scalar_tensor_tensor(out=K.x[:, t, :], in0=y[:, u % 2, :], scalar=K.gate[:, t, bass.ds(e, 1)],
                                                 in1=K.x[:, t, :], op0=ALU.mult, op1=ALU.add).then_inc(s_add, 1)

        @block.scalar
        def _(act):
            start(act, s_h1, s_h2)
            act.wait_ge(prep, 4)
            act.sqrt(B["v1"], B["v1"]).then_inc(s_root, 1)
            act.sqrt(B["v2"], B["v2"]).then_inc(s_root, 1)
            act.wait_ge(prep, 14)
            with act.Fori(0, NE) as e:
                with act.Fori(0, NCH) as ch:
                    n = e * (NCH * 4) + ch * 4
                    for h in range(2):
                        for c in range(DC):
                            hold(act, s_one, n + h * 2 + c + 1)
                            ahead(act, s_two, n if h == 0 else n)
                            act.activation(h1[:, h, c, :], ps_one[h][c], ACT.Relu, bias=B["be1"][:, bass.ds(e, 1), c],
                                           scale=B["g1"][:, bass.ds(e, 1), c]).then_inc(s_h1, 1)
                    for h in range(2):
                        for c in range(DC):
                            ahead(act, s_two, n + h * 2 + c + 1)
                            ahead(act, s_out, e * NT + ch * UN)
                            act.activation(h2[:, c, h * HF:(h + 1) * HF], ps_two[h][c], ACT.Relu,
                                           bias=B["be2"][:, bass.ds(e, 1), c],
                                           scale=B["g2"][:, bass.ds(e, 1), c]).then_inc(s_h2, 1)

        @block.tensor
        def _(pe):
            start(pe, s_two, s_out)
            pe.wait_ge(consts, 11 * 16)
            pe.transpose(K.ps[:, 0, 0:P], raw[:, :], K.ident[:, :]).then_inc(turned, 1)
            pe.transpose(K.ps[:, 1, 0:32], raw2[:, :], K.ident[0:32, 0:32]).then_inc(turned, 1)
            pe.wait_ge(prep, 2)
            with pe.Fori(0, NE // 2) as eo:
                for b in range(2):
                    hold(pe, w_in[b], (eo + 1) * 48)
                    with pe.Fori(0, NCH) as ch:
                        n = (eo * 2 + b) * (NCH * 4) + ch * 4
                        m = (eo * 2 + b) * NT + ch * UN
                        ahead(pe, s_h1, n)
                        for h in range(2):
                            if h == 1:
                                ahead(pe, s_bias, m)
                            for oc in range(DC):
                                for c in range(DC):
                                    mm = pe.matmul(ps_one[h][oc], w1[:, b, c, oc * P:(oc + 1) * P],
                                                   K.xt[:, c, bass.ds(ch * CH + h * HF, HF)], start=c == 0, stop=c == DC - 1)
                                mm.then_inc(s_one, 1)
                        for h in range(2):
                            ahead(pe, s_h1, n + h * 2 + 2)
                            ahead(pe, s_h2, n)
                            for oc in range(DC):
                                for c in range(DC):
                                    mm = pe.matmul(ps_two[h][oc], w2[:, b, c, oc * P:(oc + 1) * P], h1[:, h, c, :],
                                                   start=c == 0, stop=c == DC - 1)
                                mm.then_inc(s_two, 1)
                        for u in range(UN):
                            ahead(pe, s_h2, n + (2 if (u + 1) * P <= HF else 4))
                            if u >= 2:
                                ahead(pe, s_bias, m + u - 1)
                            for c in range(DC):
                                mm = pe.matmul(ps_out[u % 2], h2[:, c, u * P:(u + 1) * P], wo[:, b, c, :],
                                               start=c == 0, stop=c == DC - 1)
                            mm.then_inc(s_out, 1)


def heads_of(ap, heads):
    f = D // heads
    return ap[:, 0:heads * (f + 1)].rearrange("p (h f) -> p h f", h=heads)


def ones_of(K, heads):
    f = D // heads
    return K.acc[:, :, 0:heads * (f + 1)].rearrange("p t (h f) -> p t h f", h=heads)[:, :, :, f]


def attention_rows(K, heads, src_name, dst_name):
    f = D // heads

    def act_post(act, t, u, ps, tools):
        return act.copy(heads_of(K.acc[:, t, :], heads)[:, :, 0:f], ps[:, 0:D].rearrange("p (h f) -> p h f", h=heads))

    def post(dve, turn, it, ps, tools):
        tiles = bass.ds(it * UN, UN)
        prod = tools.work[:, :, :].rearrange("p u (h f) -> p u h f", h=heads)
        wide = [P, UN, D]
        turn(dve.tensor_tensor(tools.work[:, :, :], ps, tools.vec[src_name][:, :].unsqueeze(1).to_broadcast(wide), ALU.mult))
        turn(dve.tensor_reduce(K.score_src[:, tiles, 0:heads], prod, AX, ALU.add))
        turn(dve.tensor_tensor(tools.work[:, :, :], ps, tools.vec[dst_name][:, :].unsqueeze(1).to_broadcast(wide), ALU.mult))
        return dve.tensor_reduce(K.score_dst[:, tiles, 0:heads], prod, AX, ALU.add)

    return post, act_post, 3


def edge_weights(K, tag, heads, self_tiles):
    nc = K.nc
    f, H = D // heads, heads
    SL = 0.2
    GE = 20
    NE = KT // GE
    QB = 4
    BK = GE // QB * H
    SB = 4 if H > 1 else GE
    assert NE % 2 == 0 and SB * NT * H <= 512
    with Phase(nc, tag) as ph:
        step, lchain, split = ph.sem("step"), ph.sem("lchain"), ph.sem("split")
        s_hot, s_away, s_raw, s_sel, s_e, s_top, s_red = (
            ph.sem(n) for n in ("hot", "away", "raw", "sel", "e", "top", "red"))
        s_hot2, s_back, s_logit, s_exp = (ph.sem(n) for n in ("hot2", "back", "logit", "exp"))
        s_run, s_run_t, s_run_taken, s_m = (ph.sem(n) for n in ("run", "run_t", "run_taken", "m"))
        s_own, s_ownexp, lchain2 = ph.sem("own"), ph.sem("ownexp"), ph.sem("lchain2")
        s_ring, s_ring2, s_turned, s_parts_t, s_spread, s_taken, s_table = (
            ph.sem(n) for n in ("ring", "ring2", "turned", "parts_t", "spread", "taken", "table"))
        rows_in, rows_again = [ph.sem(f"rows_in{b}") for b in range(2)], [ph.sem(f"rows_again{b}") for b in range(2)]
        src_b, dst_b = (ph.sb(n, [P, 2, GE * P], BF16) for n in ("src_b", "dst_b"))
        hit_src, hit_dst, away = (ph.sb(n, [P, 2, GE * P], BF16) for n in ("hit_src", "hit_dst", "away"))
        tab_src, tab_part = ph.sb("tab_src", [P, 3, NT, H], BF16), ph.sb("tab_part", [P, 3, NT, H], BF16)
        parts_t = ph.sb("parts_t", [NT, 3, P], BF16)
        tab_tile = ph.sb("tab_tile", [P, KT, 3, H], BF16)
        ring_tile = ph.sb("ring_tile", [P, 2, GE, 3, H], BF16)
        rest = ph.sb("rest", [P, NT, H])
        spare = K.aux[:, :, :].rearrange("p t d -> p (t d)")
        here = spare[:, NT * D - GE * NT:NT * D].rearrange("p (u t) -> p u t", t=NT)
        prod, sel = ph.sb("prod", [P, SB, NT, H]), ph.sb("sel", [P, GE, H])
        target = ph.sb("target", [P, GE, H])
        ring_e = ph.sb("ring_e", [P, 2, GE, H])
        e_all, top = ph.sb("e_all", [P, KT, H]), ph.sb("top", [P, KT, H])
        begins = spare[:, 0:KT]
        running = spare[:, KT:KT + H * KT].rearrange("p (h k) -> p h k", h=H)
        running_t = spare[0:CB, (H + 1) * KT:(H + 1) * KT + H * 4 * P].rearrange("p (h c e) -> p h c e", h=H, c=4)
        m, own, own_w = ph.sb("m", [P, NT, H]), ph.sb("own", [P, NT, H]), ph.sb("own_w", [P, NT, H])
        logit = ph.sb("logit", [P, 2, GE, H])
        block = ph.block()
        score_src, score_dst = K.score_src[:, :, 0:H], K.score_dst[:, :, 0:H]
        ps_dst = K.ps[:, 5, 0:GE * 3 * H].rearrange("p (u i h) -> p u i h", h=H, i=3)
        ps_turned = K.ps[0:NT, 0, :].bitcast(BF16)
        ps_max = [K.ps[:, i, 0:QB * P] for i in ((6, 7) if H > 1 else (1, 2, 3, 4, 6))]
        NM = len(ps_max)
        parts = GE // SB
        until = [(3 * j + 1, min(3 * j + 3, 3 * parts - 2)) for j in range(parts)] if parts > 1 else [(0, 0)]
        early = until[parts - 1][1] + NM if parts > 1 else BK
        assert 2 * BK % NM == 0
        ps_back = [K.ps[:, b, 0:GE * 3 * H].rearrange("p (u i h) -> p u i h", h=H, i=3) for b in range(2)]

        ps_m = K.ps[:, 5, 0:H * NT].rearrange("p (h t) -> p h t", h=H)

        def ps_running(h):
            return K.ps[0:CB, h, :].rearrange("p (c e) -> p c e", c=4)

        def ps_src(u):
            return K.ps[:, u // SB, (u % SB) * NT * H:(u % SB + 1) * NT * H]

        def in_parts(link, v, tab, value, left):
            link(v.tensor_copy(tab[0], value))
            link(v.tensor_tensor(left, value, tab[0], ALU.subtract))
            link(v.tensor_copy(tab[1], left))
            link(v.tensor_tensor(left, left, tab[1], ALU.subtract))
            link(v.tensor_copy(tab[2], left))

        def by_edge_tile(dve, n):
            dve.sem_inc(split, 1)
            for h in range(H):
                j = n * H + h
                dve.wait_ge(s_turned, j + 1)
                dve.tensor_copy(parts_t[:, :, :], ps_turned[:, 0:3 * P].rearrange("p (i e) -> p i e", i=3)).then_inc(s_parts_t, 1)
                dve.wait_ge(s_spread, j + 1)
                link(dve.tensor_copy(tab_tile[:, :, :, h].rearrange("p k i -> p i k"), K.ps[:, 1:4, 0:KT]))
                dve.sem_inc(s_taken, 1)
            dve.sem_inc(s_table, 1)

        def spread(pe, n, parts):
            pe.wait_ge(split, n + 1)
            for h in range(H):
                j = n * H + h
                if j > 0:
                    pe.wait_ge(s_taken, j)
                for i in range(3):
                    mm = pe.transpose(ps_turned[:, i * P:(i + 1) * P], parts[:, i, :, h], K.ident_b[:, :])
                mm.then_inc(s_turned, 1)
                pe.wait_ge(s_parts_t, j + 1)
                for i in range(3):
                    mm = pe.matmul(K.ps[:, 1 + i, 0:KT], parts_t[:, i, :], K.in_tile[:, :], start=True, stop=True)
                mm.then_inc(s_spread, 1)

        link = Chain(nc.vector, step)

        @block.sync
        def _(sp):
            with sp.Fori(0, NE // 2) as it:
                for b in range(2):
                    g = it * 2 + b
                    hold(sp, s_hot, g + 1)
                    for i, dst in enumerate((src_b, dst_b)):
                        row = K.pair_rows[i, bass.ds(g * GE, GE), :].rearrange("k e -> (k e)").partition_broadcast(P)
                        sp.dma_start(dst[:, b, :], row).then_inc(rows_in[b], 16)
            sp.wait_ge(s_hot, NE + 2)
            with sp.Fori(0, NE // 2) as it:
                for b in range(2):
                    g = it * 2 + b
                    hold(sp, s_hot2, g + 1)
                    row = K.pair_rows[1, bass.ds(g * GE, GE), :].rearrange("k e -> (k e)").partition_broadcast(P)
                    sp.dma_start(dst_b[:, b, :], row).then_inc(rows_again[b], 16)

        @block.scalar
        def _(act):
            act.sem_inc(s_away, 2)
            act.sem_inc(s_exp, 2)
            act.wait_ge(s_table, 1)
            with act.Fori(0, NE // 2) as it:
                for b in range(2):
                    g = it * 2 + b
                    hold(act, s_raw, g + 1)
                    act.copy(ring_tile[:, b, :, :, :], tab_tile[:, bass.ds(g * GE, GE), :, :]).then_inc(s_ring, 1)
                    hold(act, s_hot, g + 3)
                    hold(act, s_top, (g + 1) * BK)
                    act.activation(away[:, b, :], hit_dst[:, b, :], ACT.Copy, bias=-BIG, scale=BIG).then_inc(s_away, 1)
            act.wait_ge(s_own, 1)
            act.activation(own_w[:, :, :], own[:, :, :], ACT.Exp).then_inc(s_ownexp, 1)
            act.wait_ge(s_table, 2)

            def maxima_of(it, b):
                g = it * 2 + b
                hold(act, s_back, g + 1)
                act.copy(ring_tile[:, b, :, :, :], tab_tile[:, bass.ds(g * GE, GE), :, :]).then_inc(s_ring2, 1)

            def exponentials(it, b):
                g = it * 2 + b
                hold(act, s_logit, g + 3)
                act.activation(K.edge_w[:, bass.ds(g * GE, GE), 0:H], logit[:, b, :, :], ACT.Exp).then_inc(s_exp, 1)

            for b in range(2):
                maxima_of(0, b)
            with act.Fori(0, NE // 2 - 1) as it:
                for b in range(2):
                    exponentials(it, b)
                    maxima_of(it + 1, b)
            for b in range(2):
                exponentials(NE // 2 - 1, b)

        @block.vector
        def _(dve):
            dve.sem_inc(s_hot, 2)
            dve.sem_inc(s_sel, 1)
            dve.sem_inc(s_red, NM)
            dve.sem_inc(s_hot2, 2)
            dve.sem_inc(s_logit, 2)
            in_parts(link, dve, [tab_src[:, i, :, :] for i in range(3)], score_src, rest[:, :, :])
            in_parts(link, dve, [tab_part[:, i, :, :] for i in range(3)], score_dst, rest[:, :, :])
            by_edge_tile(dve, 0)
            def hits(chain, it, k):
                g, b = it * 2 + k, k % 2
                hold(dve, rows_in[b], (it + k // 2 + 1) * 32)
                hold(dve, s_raw, g + 1)
                hold(dve, s_away, g + 1)
                chain(dve.tensor_scalar(hit_src[:, b, :], src_b[:, b, :], K.col_f[:, 0:1], None, ALU.is_equal))
                dve.tensor_scalar(hit_dst[:, b, :], dst_b[:, b, :], K.col_f[:, 0:1], None, ALU.is_equal).then_inc(s_hot, 1)

            def maxima(it, k, first, end):
                g, b = it * 2 + k, k % 2
                for q in range(first, end):
                    j, h = q // H, q % H
                    hold(dve, s_top, g * BK + q + 1 + 2 * BK)
                    dve.tensor_reduce(top[:, bass.ds(g * GE + j * QB, QB), h],
                                      ps_max[(q + b * BK) % NM].rearrange("p (u e) -> p u e", e=P), AX, ALU.max).then_inc(s_red, 1)

            def sources(chain, it, k):
                tiles = K.src_tile[:, bass.ds((it * 2 + k) * GE, GE)].unsqueeze(2).to_broadcast([P, GE, NT])
                chain(dve.tensor_tensor(here, tiles, K.row_f[:, 0:NT].unsqueeze(1).to_broadcast([P, GE, NT]), ALU.is_equal))

            def logits(chain, it, k, after=True, more=2):
                g, b = it * 2 + k, k % 2
                hold(dve, s_raw, g + 3)
                for j in range(parts):
                    raw = K.ps[:, j, 0:SB * NT * H].rearrange("p (u t h) -> p u t h", t=NT, h=H)
                    mine = here[:, j * SB:(j + 1) * SB, :].unsqueeze(3).to_broadcast([P, SB, NT, H])
                    chain(dve.tensor_tensor(prod[:, :, :, :], raw, mine, ALU.mult))
                    if after:
                        maxima(it, k - 1, until[j - 1][1] if j else 0, until[j][0])
                    chain(dve.tensor_reduce(sel[:, j * SB:(j + 1) * SB, :], prod[:, :, :, :].rearrange("p u t h -> p u h t"),
                                            AX, ALU.add))
                    if after:
                        maxima(it, k - 1, *until[j])
                dve.tensor_reduce(target[:, :, :], ps_dst.rearrange("p u i h -> p u h i"), AX, ALU.add).then_inc(s_sel, 1)
                hold(dve, s_sel, g + 2)
                chain(dve.tensor_tensor(sel[:, :, :], sel[:, :, :], target[:, :, :], ALU.add))
                hold(dve, s_top, (g + 1) * BK)
                dve.scalar_tensor_tensor(out=ring_e[:, b, :, :], in0=sel[:, :, :], scalar=SL, in1=sel[:, :, :],
                                         op0=ALU.mult, op1=ALU.max).then_inc(s_e, 1)
                hold(dve, s_e, g + 1)
                dve.tensor_copy(e_all[:, bass.ds(g * GE, GE), :], ring_e[:, b, :, :])
                if after:
                    maxima(it, k - 1, until[parts - 1][1], early)
                if more >= 2:
                    hits(chain, it, k + 2)
                if more >= 1:
                    sources(chain, it, k + 1)
                if after:
                    maxima(it, k - 1, early, BK)

            hits(link, 0, 0)
            hits(link, 0, 1)
            sources(link, 0, 0)
            logits(link, 0, 0, after=False)
            with dve.Fori(0, NE // 2 - 2) as it:
                turn = LoopChain(dve, lchain, it, 2 * (3 + 2 * parts))
                logits(turn, it, 1)
                logits(turn, it, 2)
                turn.end()
            logits(link, NE // 2 - 2, 1)
            logits(link, NE // 2 - 2, 2, more=1)
            logits(link, NE // 2 - 1, 1, more=0)
            maxima(NE // 2 - 1, 1, 0, BK)
            link(dve.memset(begins[:, 0:1], -BIG))
            link(dve.tensor_tensor(begins[:, 1:KT], K.tile_f[:, 0:KT - 1], K.tile_f[:, 1:KT], ALU.subtract))
            link(dve.tensor_scalar(begins[:, 1:KT], begins[:, 1:KT], BIG, None, ALU.mult))
            dve.wait_ge(s_red, NE * BK + NM)
            for h in range(H):
                dve.tensor_tensor_scan(running[:, h, :], begins, top[:, :, h], -BIG, ALU.add, ALU.max).then_inc(s_run, 1)
            for h in range(H):
                dve.wait_ge(s_run_t, h + 1)
                dve.tensor_copy(running_t[:, h, :, :], ps_running(h)).then_inc(s_run_taken, 1)
            dve.wait_ge(s_m, H)
            link(dve.tensor_tensor(m[:, :, :].rearrange("p t h -> p h t"), ps_m, K.no_edge[:, :].unsqueeze(1).to_broadcast([P, H, NT]),
                                   ALU.add))
            link(dve.tensor_tensor(own[:, :, :], score_src, score_dst, ALU.add))
            link(dve.scalar_tensor_tensor(out=own[:, :, :], in0=own[:, :, :], scalar=SL, in1=own[:, :, :],
                                          op0=ALU.mult, op1=ALU.max))
            looped = m[:, 0:self_tiles, :]
            link(dve.tensor_tensor(looped, looped, own[:, 0:self_tiles, :], ALU.max))
            link(dve.tensor_tensor(own[:, :, :], own[:, :, :], m[:, :, :], ALU.subtract))
            dve.tensor_scalar(own[:, :, :], own[:, :, :], 0.0, None, ALU.min).then_inc(s_own, 1)
            in_parts(link, dve, [tab_part[:, i, :, :] for i in range(3)], m[:, :, :], rest[:, :, :])
            by_edge_tile(dve, 1)
            dve.wait_ge(s_ownexp, 1)
            values = K.acc[:, 0:self_tiles, 0:H * (f + 1)].rearrange("p t (h f) -> p t h f", h=H)
            link(dve.tensor_tensor(values, values,
                                   own_w[:, 0:self_tiles, :].unsqueeze(3).to_broadcast([P, self_tiles, H, f + 1]), ALU.mult))
            if self_tiles < NT:
                link(dve.memset(K.acc[:, self_tiles:NT, :], 0.0))
            def hits_again(it, b):
                g = it * 2 + b
                hold(dve, rows_again[b], (it + 1) * 16)
                hold(dve, s_back, g + 1)
                dve.tensor_scalar(hit_dst[:, b, :], dst_b[:, b, :], K.col_f[:, 0:1], None, ALU.is_equal).then_inc(s_hot2, 1)

            def differences(chain, it, b):
                g = it * 2 + b
                hold(dve, s_back, g + 3)
                hold(dve, s_exp, g + 1)
                chain(dve.tensor_reduce(target[:, :, :], ps_back[b].rearrange("p u i h -> p u h i"), AX, ALU.add))
                chain(dve.tensor_tensor(logit[:, b, :, :], e_all[:, bass.ds(g * GE, GE), :], target[:, :, :], ALU.subtract))
                dve.tensor_scalar(logit[:, b, :, :], logit[:, b, :, :], 0.0, None, ALU.min).then_inc(s_logit, 1)

            for b in range(2):
                hits_again(0, b)
            with dve.Fori(0, NE // 2 - 1) as it:
                turn = LoopChain(dve, lchain2, it, 4)
                for b in range(2):
                    differences(turn, it, b)
                    hits_again(it + 1, b)
                turn.end()
            for b in range(2):
                differences(link, NE // 2 - 1, b)

        @block.tensor
        def _(pe):
            pe.sem_inc(s_raw, 2)
            pe.sem_inc(s_top, 2 * BK)
            pe.sem_inc(s_back, 2)

            spread(pe, 0, tab_part)

            def scores(it, k):
                g, b = it * 2 + k, k % 2
                hold(pe, s_hot, g + 3)
                hold(pe, s_ring, g + 1)
                hold(pe, s_sel, g + 1)
                for u in range(GE):
                    cols = slice(u * P, (u + 1) * P)
                    for i in range(3):
                        pe.matmul(ps_src(u), hit_src[:, b, cols], tab_src[:, i, :, :].rearrange("p t h -> p (t h)"),
                                  start=i == 0, stop=i == 2)
                    mm = pe.matmul(ps_dst[:, u, :, :].rearrange("p i h -> p (i h)"), hit_dst[:, b, cols],
                                   ring_tile[:, b, u, :, :].rearrange("p i h -> p (i h)"), start=True, stop=True)
                mm.then_inc(s_raw, 1)

            def by_rows(it, k, first, end):
                g, b = it * 2 + k, k % 2
                if first == 0:
                    hold(pe, s_e, g + 1)
                    hold(pe, s_away, g + 3)
                for q in range(first, end):
                    j, h = q // H, q % H
                    bank = ps_max[(q + b * BK) % NM]
                    hold(pe, s_red, g * BK + q + 1)
                    pe.matmul(bank, K.ident_b[:, :], away[:, b, j * QB * P:(j + 1) * QB * P], start=True, stop=False,
                              skip_group_check=True)
                    for i in range(QB):
                        mm = pe.matmul(bank[:, i * P:(i + 1) * P], ring_e[:, b, j * QB + i, h:h + 1].to_broadcast([P, P]),
                                       K.ident[:, :], start=False, stop=True, skip_group_check=True)
                    mm.then_inc(s_top, 1)

            scores(0, 0)
            scores(0, 1)
            with pe.Fori(0, NE // 2 - 1) as it:
                for k in range(2):
                    by_rows(it, k, 0, early)
                    scores(it, k + 2)
                    by_rows(it, k, early, BK)
            for k in range(2):
                by_rows(NE // 2 - 1, k, 0, BK)
            for h in range(H):
                pe.wait_ge(s_run, h + 1)
                for c in range(4):
                    mm = pe.transpose(ps_running(h)[:, c, :], running[:, h, c * CB:(c + 1) * CB], K.ident[:, :])
                mm.then_inc(s_run_t, 1)
            for h in range(H):
                pe.wait_ge(s_run_taken, h + 1)
                for c in range(4):
                    mm = pe.matmul(ps_m[:, h, :], running_t[:, h, c, :], K.last_of[:, c, :], start=c == 0, stop=c == 3)
                mm.then_inc(s_m, 1)
            spread(pe, 1, tab_part)
            with pe.Fori(0, NE // 2) as it:
                for b in range(2):
                    g = it * 2 + b
                    hold(pe, s_hot2, g + 3)
                    hold(pe, s_ring2, g + 1)
                    hold(pe, s_logit, g + 1)
                    for u in range(GE):
                        mm = pe.matmul(ps_back[b][:, u, :, :].rearrange("p i h -> p (i h)"), hit_dst[:, b, u * P:(u + 1) * P],
                                       ring_tile[:, b, u, :, :].rearrange("p i h -> p (i h)"), start=True, stop=True)
                    mm.then_inc(s_back, 1)


def finish_attention(K, tag, heads, bias_name, relu=False, to_aux=False):
    nc = K.nc
    f = D // heads
    with Phase(nc, tag) as ph:
        loaded, step = ph.sem("loaded"), ph.sem("step")
        bias, total = ph.sb("bias", [P, D]), ph.sb("total", [P, NT, heads])
        block = ph.block()

        @block.sync
        def _(sp):
            sp.dma_start(bias[:, :], K.inp[bias_name].partition_broadcast(P)).then_inc(loaded, 16)

        @block.vector
        def _(dve):
            link = Chain(dve, step)
            rows = K.acc[:, :, 0:heads * (f + 1)].rearrange("p t (h f) -> p t h f", h=heads)
            link(dve.tensor_scalar(total[:, :, :], rows[:, :, :, f], 0.5, None, ALU.max))
            link(dve.reciprocal(total[:, :, :], total[:, :, :]))
            link(dve.tensor_tensor(K.aux[:, :, :].rearrange("p t (h f) -> p t h f", h=heads), rows[:, :, :, 0:f],
                                   total[:, :, :].unsqueeze(3).to_broadcast([P, NT, heads, f]), ALU.mult))
            dve.wait_ge(loaded, 16)
            link(dve.tensor_tensor(K.aux[:, :, :], K.aux[:, :, :], bias[:, :].unsqueeze(1).to_broadcast([P, NT, D]), ALU.add))
            if relu:
                dve.scalar_tensor_tensor(out=K.x[:, :, :], in0=K.aux[:, :, :], scalar=0.0, in1=K.x[:, :, :],
                                         op0=ALU.max, op1=ALU.add)
            elif not to_aux:
                dve.tensor_tensor(K.x[:, :, :], K.x[:, :, :], K.aux[:, :, :], ALU.add)


def add_mean(K, tag):
    nc = K.nc
    with Phase(nc, tag) as ph:
        step = ph.sem("step")
        weight = ph.sb("weight", [P, NT])
        block = ph.block()

        @block.vector
        def _(dve):
            link = Chain(dve, step)
            sums = K.acc[:, :, 0:D]
            link(dve.tensor_scalar(weight[:, :], K.degree[:, :], 1.0, None, ALU.max))
            link(dve.reciprocal(weight[:, :], weight[:, :]))
            link(dve.tensor_tensor(sums, sums, weight[:, :].unsqueeze(2).to_broadcast([P, NT, D]), ALU.mult))
            dve.tensor_tensor(K.x[:, :, :], K.x[:, :, :], sums, ALU.add)


def degree_roots(K):
    with Phase(K.nc, "dinv") as ph:
        a, b = ph.sem("a"), ph.sem("b")
        block = ph.block()

        @block.vector
        def _(dve):
            dve.tensor_scalar(K.dinv[:, :], K.degree[:, :], 1.0, None, ALU.add).then_inc(a, 1)
            dve.wait_ge(b, 1)
            dve.reciprocal(K.dinv[:, :], K.dinv[:, :]).then_inc(a, 1)

        @block.scalar
        def _(act):
            act.wait_ge(a, 1)
            act.sqrt(K.dinv[:, :], K.dinv[:, :]).then_inc(b, 1)


def residual(K, tag, bias_name):
    nc = K.nc
    with Phase(nc, tag) as ph:
        loaded, step = ph.sem("loaded"), ph.sem("step")
        bias = ph.sb("bias", [P, D])
        block = ph.block()

        @block.sync
        def _(sp):
            sp.dma_start(bias[:, :], K.inp[bias_name].partition_broadcast(P)).then_inc(loaded, 16)

        @block.vector
        def _(dve):
            link = Chain(dve, step)
            link(dve.tensor_tensor(K.x[:, :, :], K.x[:, :, :], K.acc[:, :, 0:D], ALU.add))
            link(dve.tensor_tensor(K.x[:, :, :], K.x[:, :, :], K.loop_out[:, :, :], ALU.add))
            dve.wait_ge(loaded, 16)
            link(dve.tensor_tensor(K.x[:, :, :], K.x[:, :, :], bias[:, :].unsqueeze(1).to_broadcast([P, NT, D]), ALU.add))


def wide_experts(K, tag, turns, pairs, HC, act, load, target, beside=None):
    nc = K.nc
    CH = UN * P
    HF = CH // 2
    NCH = NT // UN
    with Phase(nc, tag) as ph:
        w_in = [ph.sem(f"w_in{b}") for b in range(pairs)]
        s_one, s_h, s_out, s_bias, s_add, s_index = (ph.sem(n) for n in ("one", "h", "out", "bias", "add", "index"))
        w1 = ph.sb("w1", [P, pairs, DC, HC * P])
        w2 = ph.sb("w2", [P, pairs, HC, D])
        b1, b2 = ph.sb("b1", [P, pairs, HC]), ph.sb("b2", [P, pairs, D])
        h = ph.sb("h", [P, HC, CH])
        y = ph.sb("y", [P, 2, D])
        bchain = ph.sem("beside")
        block = ph.block()
        ps_one = [K.ps[:, i, 0:HF] for i in range(4)]
        ps_out = [K.ps[:, 4 + i, 0:D] for i in range(2)]

        @block.sync
        def _(sp):
            with sp.Fori(0, turns) as eo:
                for b in range(pairs):
                    ahead(sp, s_add, eo * (pairs * NT))
                    with nc.allow_non_contiguous_dma(reason="biases by partitions"):
                        load(sp, eo, b, w1[:, b, :, :], w2[:, b, :, :], b1[:, b, :], b2[:, b, :], w_in[b])

        @block.vector
        def _(dve):
            start(dve, s_add, s_bias)
            with dve.Fori(0, turns) as eo:
                for b in range(pairs):
                    hold(dve, w_in[b], (eo + 1) * 64)
                    with dve.Fori(0, NCH) as ch:
                        n = (eo * pairs + b) * NT + ch * UN
                        if beside is not None:
                            turn = LoopChain(dve, bchain, ch, 2 * UN)
                            for u in range(UN):
                                beside(dve, turn, ch * UN + u)
                                ahead(dve, s_out, n + u + 1)
                                dve.tensor_tensor(target[:, ch * UN + u, :], ps_out[u % 2], b2[:, b, :], ALU.add).then_inc(s_bias, 1)
                            turn.end()
                        for u in range(UN if beside is None else 0):
                            t = ch * UN + u
                            ahead(dve, s_out, n + u + 1)
                            ahead(dve, s_add, n + u - 1 if u else n)
                            dve.tensor_tensor(y[:, u % 2, :], ps_out[u % 2], b2[:, b, :], ALU.add).then_inc(s_bias, 1)
                            ahead(dve, s_bias, n + u + 1)
                            dve.scalar_tensor_tensor(out=target[:, t, :], in0=y[:, u % 2, :],
                                                     scalar=K.gate[:, t, bass.ds(eo * pairs + b, 1)],
                                                     in1=target[:, t, :], op0=ALU.mult, op1=ALU.add).then_inc(s_add, 1)

        @block.scalar
        def _(sc):
            with sc.Fori(0, turns) as eo:
                for b in range(pairs):
                    hold(sc, w_in[b], (eo + 1) * 64)
                    with sc.Fori(0, NCH) as ch:
                        n = ((eo * pairs + b) * NCH + ch) * (HC * 2)
                        m = (eo * pairs + b) * NT + ch * UN
                        ahead(sc, s_out, m)
                        for hc in range(HC):
                            for half in range(2):
                                hold(sc, s_one, n + hc * 2 + half + 1)
                                sc.activation(h[:, hc, half * HF:(half + 1) * HF], ps_one[(hc * 2 + half) % 4], act,
                                              bias=b1[:, b, hc:hc + 1]).then_inc(s_h, 1)

        @block.tensor
        def _(pe):
            start(pe, s_out)
            with pe.Fori(0, turns) as eo:
                for b in range(pairs):
                    hold(pe, w_in[b], (eo + 1) * 64)
                    with pe.Fori(0, NCH) as ch:
                        n = ((eo * pairs + b) * NCH + ch) * (HC * 2)
                        m = (eo * pairs + b) * NT + ch * UN
                        for hc in range(HC):
                            for half in range(2):
                                q = hc * 2 + half
                                if q >= 4:
                                    hold(pe, s_h, n + q - 3)
                                for c in range(DC):
                                    mm = pe.matmul(ps_one[q % 4], w1[:, b, c, hc * P:(hc + 1) * P],
                                                   K.xt[:, c, bass.ds(ch * CH + half * HF, HF)], start=c == 0, stop=c == DC - 1)
                                mm.then_inc(s_one, 1)
                        hold(pe, s_h, n + HC * 2)
                        for u in range(UN):
                            ahead(pe, s_bias, m + u - 1 if u > 1 else m)
                            for hc in range(HC):
                                mm = pe.matmul(ps_out[u % 2], h[:, hc, u * P:(u + 1) * P], w2[:, b, hc, :],
                                               start=hc == 0, stop=hc == HC - 1)
                            mm.then_inc(s_out, 1)


def route_tokens(K, tag):
    nc = K.nc
    NE = 8
    NS = NB_X * TB
    with Phase(nc, tag) as ph:
        step, counted, zeroed, scan = ph.sem("step"), ph.sem("counted"), ph.sem("zeroed"), ph.sem("scan")
        s_mask, s_slots, s_ring, filled, iota_done = (ph.sem(n) for n in ("mask", "slots", "ring", "filled", "iota_done"))
        moved = ph.by_rows("moved", 1)[0]
        ZC = 8
        zero = ph.sb("zero", [P, NS * D // P // ZC])
        real, pad = ph.sb("real", [P, 1]), ph.sb("pad", [P, 1])
        one = ph.sb("one", [P, NT])
        mask, tot, incl, slot, tmp = (ph.sb(n, [P, NT, NE]) for n in ("mask", "tot", "incl", "slot", "tmp"))
        blocks_i, blocks, ends, first = ph.sb("blocks_i", [P, NE], I32), *(ph.sb(n, [P, NE]) for n in ("blocks", "ends", "first"))
        s12, to = ph.sb("s12", [P, 2, NT]), ph.sb("to", [P, 2, NT])
        differ, own = ph.sb("differ", [P, NT]), ph.sb("own", [P, NT])
        put = ph.sb("put", [P, 2, NT], I32)
        num_i, num, expert = ph.sb("num_i", [P, NB_X], I32), ph.sb("num", [P, NB_X]), ph.sb("expert", [P, NB_X])
        ring_rows, ring_put = ph.sb("ring_rows", [P, UN, D]), ph.sb("ring_put", [P, 2, UN], I32)
        block = ph.block()
        flat = lambda a: a[:, :, :].rearrange("p t e -> p (t e)")
        ps_before, ps_tot = K.ps[:, 0, 0:NT * NE], K.ps[:, 1, 0:NT * NE]

        @block.sync
        def _(sp):
            sp.wait_ge(filled, 1)
            cells = K.sorted_x[0:NS, :].rearrange("(p r) d -> p (r d)", p=P).rearrange("p (k c) -> p k c", k=ZC)
            for i in range(ZC):
                sp.dma_start(cells[:, i, :], zero[:, :]).then_inc(zeroed, 16)
            sp.wait_ge(zeroed, ZC * 16)

        @block.tensor
        def _(pe):
            pe.wait_ge(s_mask, 1)
            pe.matmul(ps_before, K.before[:, :], flat(mask), start=True, stop=True).then_inc(counted, 1)
            pe.matmul(ps_tot, K.ones[:, :], flat(mask), start=True, stop=True).then_inc(counted, 1)

        @block.vector
        def _(dve):
            link = Chain(dve, step)
            dve.memset(zero[:, :], 0.0).then_inc(filled, 1)
            link(dve.memset(one[:, :], 1.0))
            link(dve.tensor_scalar(real[:, :], K.col_f[:, :], float(NPT), None, ALU.is_lt))
            dve.tensor_scalar(flat(mask), flat(K.gate), 0.0, real[:, 0:1], ALU.is_gt, ALU.mult).then_inc(s_mask, 1)
            link(dve.tensor_scalar(pad[:, :], K.col_f[:, :], float(NPT), None, ALU.is_ge))
            dve.wait_ge(counted, 2)
            link(dve.tensor_copy(flat(tot), ps_tot))
            for e in range(NE):
                dve.tensor_tensor_scan(incl[:, :, e], one[:, :], tot[:, :, e], 0.0, ALU.mult, ALU.add).then_inc(scan, 1)
            dve.wait_ge(scan, NE)
            link(dve.tensor_scalar(blocks_i[:, :], incl[:, NT - 1, :], float(TB - 1), None, ALU.add))
            link(dve.tensor_scalar(blocks_i[:, :], blocks_i[:, :], TB.bit_length() - 1, None, ALU.logical_shift_right))
            link(dve.tensor_copy(blocks[:, :], blocks_i[:, :]))
            link(dve.tensor_tensor_scan(ends[:, :], one[:, 0:NE], blocks[:, :], 0.0, ALU.mult, ALU.add))
            link(dve.tensor_tensor(first[:, :], ends[:, :], blocks[:, :], ALU.subtract))
            link(dve.tensor_scalar(first[:, :], first[:, :], float(TB), None, ALU.mult))
            wide = [P, NT, NE]
            link(dve.tensor_tensor(incl[:, :, :], incl[:, :, :], tot[:, :, :], ALU.subtract))
            link(dve.tensor_tensor(incl[:, :, :], incl[:, :, :], first[:, :].unsqueeze(1).to_broadcast(wide), ALU.add))
            link(dve.tensor_tensor(flat(slot), flat(incl), ps_before, ALU.add))
            link(dve.scalar_tensor_tensor(out=flat(tmp), in0=flat(slot), scalar=-float(NS), in1=flat(mask), op0=ALU.add, op1=ALU.mult))
            link(dve.tensor_reduce(s12[:, 0, :], tmp[:, :, :], AX, ALU.min))
            link(dve.tensor_scalar(s12[:, 0, :], s12[:, 0, :], float(NS), None, ALU.add))
            link(dve.scalar_tensor_tensor(out=flat(tmp), in0=flat(slot), scalar=1.0, in1=flat(mask), op0=ALU.add, op1=ALU.mult))
            link(dve.tensor_reduce(s12[:, 1, :], tmp[:, :, :], AX, ALU.max))
            link(dve.tensor_scalar(s12[:, 1, :], s12[:, 1, :], -1.0, None, ALU.add))
            link(dve.tensor_tensor(differ[:, :], s12[:, 1, :], s12[:, 0, :], ALU.is_gt))
            link(dve.tensor_scalar(own[:, :], K.row_f[:, 0:NT], float(P), K.col_f[:, 0:1], ALU.mult, ALU.add))
            link(dve.tensor_scalar(own[:, :], own[:, :], float(NS), None, ALU.add))
            link(dve.tensor_scalar(to[:, 0, :], own[:, :], float(NPAD - NS), pad[:, 0:1], ALU.add, ALU.mult))
            link(dve.tensor_tensor(to[:, 0, :], to[:, 0, :], s12[:, 0, :], ALU.add))
            link(dve.tensor_tensor(to[:, 1, :], s12[:, 1, :], own[:, :], ALU.subtract))
            link(dve.tensor_tensor(to[:, 1, :], to[:, 1, :], differ[:, :], ALU.mult))
            link(dve.tensor_tensor(to[:, 1, :], to[:, 1, :], own[:, :], ALU.add))
            dve.tensor_copy(put[:, :, :], to[:, :, :]).then_inc(s_slots, 1)
            for i in range(2):
                link(dve.tensor_tensor(tmp[:, :, :], slot[:, :, :], s12[:, i, :].unsqueeze(2).to_broadcast(wide), ALU.is_equal))
                link(dve.tensor_tensor(flat(tmp), flat(tmp), flat(K.gate), ALU.mult))
                link(dve.tensor_reduce(K.slot_gate[:, i, :], tmp[:, :, :], AX, ALU.add))
            link(dve.tensor_tensor(K.slot_gate[:, 1, :], K.slot_gate[:, 1, :], differ[:, :], ALU.mult))
            dve.tensor_scalar(K.slots[:, :, :], to[:, :, :], float(NS - 1), None, ALU.min)
            dve.wait_ge(iota_done, 1)
            link(dve.tensor_copy(num[:, :], num_i[:, :]))
            link(dve.memset(expert[:, :], 0.0))
            for e in range(NE - 1):
                link(dve.scalar_tensor_tensor(out=expert[:, :], in0=num[:, :], scalar=ends[:, e:e + 1], in1=expert[:, :],
                                              op0=ALU.is_ge, op1=ALU.add))
            dve.tensor_copy(K.block_expert[:, :], expert[:, :])

        @block.gpsimd
        def _(pool):
            pool.iota(num_i[:, :], [[1, NB_X]], base=0, channel_multiplier=0).then_inc(iota_done, 1)
            pool.wait_ge(zeroed, ZC * 16)
            pool.wait_ge(s_slots, 1)

            def store(it):
                pool.tensor_copy(ring_rows[:, :, :], K.aux[:, bass.ds(it * UN, UN), :]).then_inc(s_ring, 1)
                pool.tensor_copy(ring_put[:, :, :], put[:, :, bass.ds(it * UN, UN)]).then_inc(s_ring, 1)
                hold(pool, s_ring, it * 2 + 2)
                for i in range(2):
                    for u in range(UN):
                        pool.indirect_dma_start(K.sorted_x, bass.IndirectOffsetOnAxis(ring_put[:, i, u:u + 1], 0),
                                                ring_rows[:, u, :], None).then_inc(moved, 16)

            store(0)
            with pool.Fori(1, NT // UN) as it:
                hold(pool, moved, it * (2 * UN * 16))
                store(it)
            pool.wait_ge(moved, 2 * NT * 16)


def sorted_experts(K, tag, load, act, HC):
    nc = K.nc
    QT = TB // P
    with Phase(nc, tag) as ph:
        w_in = [ph.sem(f"w_in{b}") for b in range(2)]
        s_tr, s_xt, s_one, s_h, s_out, s_y, s_free = (ph.sem(n) for n in ("tr", "xt", "one", "h", "out", "y", "free"))
        stored = ph.by_rows("stored", 1)[0]
        w1, w2 = ph.sb("w1", [P, 2, DC, HC * P]), ph.sb("w2", [P, 2, HC, D])
        b1, b2 = ph.sb("b1", [P, 2, HC]), ph.sb("b2", [P, 2, D])
        xs, xt = ph.sb("xs", [P, 2, QT, D]), ph.sb("xt", [P, 2, DC, TB])
        h, y = ph.sb("h", [P, 2, HC, TB]), ph.sb("y", [P, 2, QT, D])
        block = ph.block()
        ps_t = K.ps[:, 0:DC, 0:TB]
        ps_one = [K.ps[:, 2 + i, 0:TB] for i in range(4)]
        ps_out = [K.ps[:, 6 + i, 0:D] for i in range(2)]
        rows = K.sorted_x[0:NB_X * TB, :].rearrange("(n q p) d -> n p q d", q=QT, p=P)
        out_rows = K.sorted_y.rearrange("(n q p) d -> n p q d", q=QT, p=P)

        @block.sync
        def _(sp):
            with sp.Fori(0, NB_X // 2) as it:
                for b in range(2):
                    n = it * 2 + b
                    e = nc.values_load(K.block_expert[0:1, bass.ds(n, 1)], engines=[sp.engine], min_val=0, max_val=7,
                                       skip_runtime_bounds_check_because="it counts 7 comparisons")
                    hold(sp, s_out, (n + 1) * QT)
                    hold(sp, s_y, (n + 1) * QT)
                    with nc.allow_non_contiguous_dma(reason="biases by partitions"):
                        load(sp, e, w1[:, b, :, :], w2[:, b, :, :], b1[:, b, :], b2[:, b, :], w_in[b])
                    sp.dma_start(xs[:, b, :, :], rows[bass.ds(n, 1)].rearrange("a p q d -> p (a q) d")).then_inc(w_in[b], 16)

        @block.tensor
        def _(pe):
            pe.sem_inc(s_out, 2 * QT)
            with pe.Fori(0, NB_X // 2) as it:
                for b in range(2):
                    n = it * 2 + b
                    hold(pe, w_in[b], (it + 1) * 80)
                    hold(pe, s_xt, n + 1)
                    for q in range(QT):
                        for c in range(DC):
                            mm = pe.transpose(ps_t[:, c, q * P:(q + 1) * P], xs[:, b, q, c * P:(c + 1) * P], K.ident[:, :])
                    mm.then_inc(s_tr, 1)
                    hold(pe, s_xt, n + 2)
                    for hc in range(HC):
                        hold(pe, s_h, n * HC + hc + 1)
                        for c in range(DC):
                            mm = pe.matmul(ps_one[hc % 4], w1[:, b, c, hc * P:(hc + 1) * P], xt[:, b, c, :],
                                           start=c == 0, stop=c == DC - 1)
                        mm.then_inc(s_one, 1)
                    hold(pe, s_h, (n + 1) * HC + 4)
                    for q in range(QT):
                        hold(pe, s_y, n * QT + q + 1 + QT)
                        for hc in range(HC):
                            mm = pe.matmul(ps_out[q], h[:, b, hc, q * P:(q + 1) * P], w2[:, b, hc, :],
                                           start=hc == 0, stop=hc == HC - 1)
                        mm.then_inc(s_out, 1)

        @block.scalar
        def _(sc):
            sc.sem_inc(s_xt, 1)
            sc.sem_inc(s_h, 4)
            with sc.Fori(0, NB_X // 2) as it:
                for b in range(2):
                    n = it * 2 + b
                    hold(sc, s_tr, n + 1)
                    hold(sc, s_out, (n + 1) * QT)
                    sc.copy(xt[:, b, :, :], ps_t).then_inc(s_xt, 1)
                    hold(sc, w_in[b], (it + 1) * 80)
                    for hc in range(HC):
                        hold(sc, s_one, n * HC + hc + 1)
                        sc.activation(h[:, b, hc, :], ps_one[hc % 4], act, bias=b1[:, b, hc:hc + 1]).then_inc(s_h, 1)

        @block.vector
        def _(dve):
            dve.sem_inc(s_y, 2 * QT)
            with dve.Fori(0, NB_X // 2) as it:
                for b in range(2):
                    n = it * 2 + b
                    hold(dve, w_in[b], (it + 1) * 80)
                    hold(dve, s_free, n + 1)
                    for q in range(QT):
                        hold(dve, s_out, n * QT + q + 1 + 2 * QT)
                        dve.tensor_tensor(y[:, b, q, :], ps_out[q], b2[:, b, :], ALU.add).then_inc(s_y, 1)

        @block.gpsimd
        def _(pool):
            pool.sem_inc(s_free, 2)
            with pool.Fori(0, NB_X // 2) as it:
                for b in range(2):
                    n = it * 2 + b
                    hold(pool, s_y, (n + 1) * QT + 2 * QT)
                    pool.dma_start(out_rows[bass.ds(n, 1)].rearrange("a p q d -> p (a q) d"), y[:, b, :, :]).then_inc(stored, 16)
                    hold(pool, stored, (n + 1) * 16)
                    pool.sem_inc(s_free, 1)


def combine_experts(K, tag):
    nc = K.nc
    PARTS = 5
    with Phase(nc, tag) as ph:
        s_ring, s_add, lchain = ph.sem("ring"), ph.sem("add"), ph.sem("lchain")
        gathered = ph.by_rows("gathered", PARTS)
        ring_idx = ph.sb("ring_idx", [P, PARTS, 2], I32)
        rows_in = ph.sb("rows_in", [P, PARTS, 2, D])
        block = ph.block()

        @block.gpsimd
        def _(pool):
            with pool.Fori(0, NT // PARTS) as it:
                for b in range(PARTS):
                    t = it * PARTS + b
                    hold(pool, s_add, t + 1)
                    pool.tensor_copy(ring_idx[:, b, :], K.slots[:, :, t]).then_inc(s_ring, 1)
                    hold(pool, s_ring, t + 1)
                    for i in range(2):
                        pool.indirect_dma_start(rows_in[:, b, i, :], None, K.sorted_y,
                                                bass.IndirectOffsetOnAxis(ring_idx[:, b, i:i + 1], 0)).then_inc(gathered[b], 16)

        @block.vector
        def _(dve):
            dve.sem_inc(s_add, PARTS)
            with dve.Fori(0, NT // PARTS) as it:
                turn = LoopChain(dve, lchain, it, PARTS)
                for b in range(PARTS):
                    t = it * PARTS + b
                    hold(dve, gathered[b], (it + 1) * 32)
                    for i in range(2):
                        ins = dve.scalar_tensor_tensor(out=K.x[:, t, :], in0=rows_in[:, b, i, :],
                                                       scalar=K.slot_gate[:, i, bass.ds(t, 1)], in1=K.x[:, t, :],
                                                       op0=ALU.mult, op1=ALU.add)
                        if i == 0:
                            turn(ins)
                    ins.then_inc(s_add, 1)
                turn.end()


def route_two(K, tag):
    nc = K.nc
    NE, CAP = 8, float(-(-N * 5 // (4 * 8)))
    with Phase(nc, tag) as ph:
        loaded, step, s_logits, s_in, s_exp = (ph.sem(n) for n in ("loaded", "step", "logits", "in", "exp"))
        wr, br = ph.sb("wr", [P, DC, NE]), ph.sb("br", [P, NE])
        total = ph.sb("total", [P, DC])
        p, el, best = ph.sb("p", [P, NE]), ph.sb("el", [P, NE]), ph.sb("best", [P, 8])
        one, pair, index = ph.sb("one", [P, 1]), ph.sb("pair", [P, 2]), ph.sb("index", [P, 8], U32)
        s_total = ph.sem("total")
        block = ph.block()

        @block.sync
        def _(sp):
            sp.dma_start(wr[:, :, :], K.inp["L1_ffn_Wr"].rearrange("(c p) e -> p c e", p=P)).then_inc(loaded, 16)
            sp.dma_start(br[:, :], K.inp["L1_ffn_br"].partition_broadcast(P)).then_inc(loaded, 16)

        @block.tensor
        def _(pe):
            pe.wait_ge(loaded, 32)
            pe.wait_ge(s_total, 1)
            for c in range(DC):
                mm = pe.matmul(K.ps[:, 0, 0:NE], total[:, c:c + 1].to_broadcast([P, P]), wr[:, c, :], start=c == 0, stop=c == DC - 1)
            mm.then_inc(s_logits, 1)

        @block.scalar
        def _(sc):
            for i, a in enumerate((p[:, :], p[:, :], pair[:, 1:2])):
                sc.wait_ge(s_in, i + 1)
                sc.activation(a, a, ACT.Exp).then_inc(s_exp, 1)

        @block.vector
        def _(dve):
            link = Chain(dve, step)
            real = K.xt[:, :, :].rearrange("p c (t n) -> p c t n", n=P)[:, :, :, 0:NPT]
            dve.tensor_reduce(total[:, :], real, mybir.AxisListType.XY, ALU.add).then_inc(s_total, 1)
            dve.wait_ge(s_logits, 1)
            link(dve.scalar_tensor_tensor(out=p[:, :], in0=K.ps[:, 0, 0:NE], scalar=1.0 / N, in1=br[:, :], op0=ALU.mult, op1=ALU.add))

            def softmax(i):
                link(dve.tensor_reduce(one[:, :], p[:, :], AX, ALU.max))
                dve.tensor_scalar(p[:, :], p[:, :], one[:, 0:1], None, ALU.subtract).then_inc(s_in, 1)
                dve.wait_ge(s_exp, i)
                link(dve.tensor_reduce(one[:, :], p[:, :], AX, ALU.add))
                link(dve.reciprocal(one[:, :], one[:, :]))
                link(dve.tensor_scalar(p[:, :], p[:, :], one[:, 0:1], None, ALU.mult))

            softmax(1)
            link(dve.tensor_scalar(el[:, :], p[:, :], float(N), CAP, ALU.mult, ALU.max))
            link(dve.reciprocal(el[:, :], el[:, :]))
            link(dve.scalar_tensor_tensor(out=p[:, :], in0=el[:, :], scalar=CAP, in1=p[:, :], op0=ALU.mult, op1=ALU.mult))
            softmax(2)
            link(dve.max(best[:, :], p[:, :]))
            link(dve.max_index(index[:, :], best[:, :], p[:, :]))
            link(dve.tensor_copy(K.pick[:, :], index[:, 0:2]))
            link(dve.memset(pair[:, 0:1], 1.0))
            dve.tensor_tensor(pair[:, 1:2], best[:, 1:2], best[:, 0:1], ALU.subtract).then_inc(s_in, 1)
            dve.wait_ge(s_exp, 3)
            link(dve.tensor_scalar(one[:, :], pair[:, 1:2], 1.0, None, ALU.add))
            link(dve.reciprocal(one[:, :], one[:, :]))
            link(dve.tensor_scalar(pair[:, :], pair[:, :], one[:, 0:1], None, ALU.mult))
            link(dve.tensor_copy(K.gate[:, :, 0:2], pair[:, :].unsqueeze(1).to_broadcast([P, NT, 2])))


def add_normed(K, tag, gamma_name, beta_name):
    nc = K.nc
    with Phase(nc, tag) as ph:
        loaded, chain, s_var, s_rstd = (ph.sem(n) for n in ("loaded", "chain", "var", "rstd"))
        gamma, beta = ph.sb("gamma", [P, D]), ph.sb("beta", [P, D])
        stats, mv = ph.sb("stats", [P, UN, 6]), ph.sb("mv", [P, UN, 2])
        block = ph.block()

        @block.sync
        def _(sp):
            sp.dma_start(gamma[:, :], K.inp[gamma_name].partition_broadcast(P)).then_inc(loaded, 16)
            sp.dma_start(beta[:, :], K.inp[beta_name].partition_broadcast(P)).then_inc(loaded, 16)

        @block.scalar
        def _(sc):
            with sc.Fori(0, NT // UN) as it:
                hold(sc, s_var, it + 1)
                sc.sqrt(mv[:, :, 1], mv[:, :, 1]).then_inc(s_rstd, 1)

        @block.vector
        def _(dve):
            dve.wait_ge(loaded, 32)
            with dve.Fori(0, NT // UN) as it:
                turn = LoopChain(dve, chain, it, 2 * UN + 1 + 4)
                row_stats(turn, dve, stats, mv, [K.aux[:, it * UN + u, :] for u in range(UN)])
                dve.tensor_scalar(mv[:, :, 1], mv[:, :, 1], LN_EPS, None, ALU.add).then_inc(s_var, 1)
                hold(dve, s_rstd, it + 1)
                turn(dve.reciprocal(mv[:, :, 1], mv[:, :, 1]))
                rows = K.aux[:, bass.ds(it * UN, UN), :]
                wide = [P, UN, D]
                turn(dve.tensor_tensor(rows, rows, mv[:, :, 0].unsqueeze(2).to_broadcast(wide), ALU.subtract))
                turn(dve.tensor_tensor(rows, rows, mv[:, :, 1].unsqueeze(2).to_broadcast(wide), ALU.mult))
                turn(dve.tensor_tensor(rows, rows, gamma[:, :].unsqueeze(1).to_broadcast(wide), ALU.mult))
                x_rows = K.x[:, bass.ds(it * UN, UN), :]
                turn(dve.tensor_tensor(x_rows, x_rows, rows, ALU.add))
                turn.end()
            dve.tensor_tensor(K.x[:, :, :], K.x[:, :, :], beta[:, :].unsqueeze(1).to_broadcast([P, NT, D]), ALU.add)


def top_two_gates(K, bias_name, cols):
    def batch(dve, turn, it, ps, tools):
        logits, best, marked = (tools.work2[:, :, i * 8:i * 8 + 8] for i in range(3))
        top = tools.small[:, :, 0]
        wide = [P, UN, cols]
        b = tools.vec[bias_name][:, :].unsqueeze(1).to_broadcast(wide)
        turn(dve.tensor_tensor(logits, ps, b, ALU.add))
        for u in range(UN):
            turn(dve.max(best[:, u, :], logits[:, u, :]))
        turn(dve.tensor_copy(top, best[:, :, 0]))
        turn(dve.memset(best[:, :, 2:8], BIG))
        for u in range(UN):
            turn(dve.match_replace(marked[:, u, :], best[:, u, :], logits[:, u, :], -BIG))
        dve.tensor_tensor(logits, logits, top.unsqueeze(2).to_broadcast(wide), ALU.subtract).then_inc(tools.s_sum, 1)
        hold(dve, tools.s_exp, it + 1)
        turn(dve.scalar_tensor_tensor(out=logits, in0=marked, scalar=-BIG, in1=logits, op0=ALU.is_equal, op1=ALU.mult))
        turn(dve.tensor_reduce(top, logits, AX, ALU.add))
        turn(dve.reciprocal(top, top))
        return dve.tensor_tensor(K.gate[:, bass.ds(it * UN, UN), :], logits, top.unsqueeze(2).to_broadcast(wide), ALU.mult)
    return batch, 6 + 2 * UN


def rank_rows(K, tag):
    nc = K.nc
    with Phase(nc, tag) as ph:
        step, s_row, s_copied, s_diag = (ph.sem(n) for n in ("step", "row", "copied", "diag"))
        diag = ph.sb("diag", [P, NT, NPT])
        block = ph.block()
        flat, flat_diag = K.rank_rows, diag[:, :, :].rearrange("p t n -> p (t n)")
        cuts = [(c, min(c + 4 * NPT, N)) for c in range(0, N, 4 * NPT)]

        @block.tensor
        def _(pe):
            pe.wait_ge(s_diag, 1)
            for i, (a, b) in enumerate(cuts):
                pe.matmul(K.ps[:, i, 0:b - a], K.ones[:, :], flat_diag[:, a:b], start=True, stop=True).then_inc(s_row, 1)

        @block.scalar
        def _(sc):
            for i, (a, b) in enumerate(cuts):
                sc.wait_ge(s_row, i + 1)
                sc.copy(flat[:, a:b], K.ps[:, i, 0:b - a]).then_inc(s_copied, 1)

        @block.vector
        def _(dve):
            link = Chain(dve, step)
            wide = [P, NT, NPT]
            eye = K.ident[:, 0:NPT].unsqueeze(1).to_broadcast(wide)
            dve.tensor_tensor(diag[:, :, :], eye, K.token_w[:, :].unsqueeze(2).to_broadcast(wide), ALU.mult).then_inc(s_diag, 1)
            link(dve.memset(K.earlier[:, 0:N], 1.0))
            link(dve.memset(K.earlier[:, N:2 * N], 0.0))
            link(dve.tensor_scalar(K.earlier[:, N:N + NPT], K.row_f[:, 0:NPT], K.col_f[:, 0:1], None, ALU.is_lt))
            dve.wait_ge(s_copied, len(cuts))
            link(dve.tensor_tensor(diag[:, :, :], flat.rearrange("p (t n) -> p t n", n=NPT), eye, ALU.mult))
            link(dve.tensor_reduce(K.own_value[:, :], diag[:, :, :], AX, ALU.add))


def node_ranks(K):
    def rank(dve, turn, t):
        mine = K.own_value[:, bass.ds(t, 1)]
        turn(dve.scalar_tensor_tensor(out=K.found[:, :], in0=K.rank_rows, scalar=mine, in1=K.earlier[:, bass.ds(N - t * NPT, N)],
                                      op0=ALU.is_equal, op1=ALU.mult))
        turn(dve.scalar_tensor_tensor(out=K.found[:, :], in0=K.rank_rows, scalar=mine, in1=K.found[:, :],
                                      op0=ALU.is_gt, op1=ALU.add, accum_out=K.rank[:, bass.ds(t, 1)]))
    return rank


def add_largest(K, tag, count):
    nc = K.nc
    with Phase(nc, tag) as ph:
        step = ph.sem("step")
        gate = ph.sb("gate", [P, NT])
        block = ph.block()

        @block.vector
        def _(dve):
            link = Chain(dve, step)
            y = K.acc[:, :, 0:D]
            link(dve.scalar_tensor_tensor(out=gate[:, :], in0=K.rank[:, :], scalar=float(count), in1=K.token_w[:, :],
                                          op0=ALU.is_lt, op1=ALU.mult))
            link(dve.tensor_tensor(y, y, gate[:, :].unsqueeze(2).to_broadcast([P, NT, D]), ALU.mult))
            link(dve.tensor_tensor(K.x[:, :, :], K.x[:, :, :], K.aux[:, :, :], ALU.add))
            dve.tensor_tensor(K.x[:, :, :], K.x[:, :, :], y, ALU.add)


def add_normed(K, tag, gamma_name, beta_name):
    nc = K.nc
    with Phase(nc, tag) as ph:
        loaded, chain, s_var, s_rstd = (ph.sem(n) for n in ("loaded", "chain", "var", "rstd"))
        gamma, beta = ph.sb("gamma", [P, D]), ph.sb("beta", [P, D])
        stats, mv = ph.sb("stats", [P, UN, 6]), ph.sb("mv", [P, UN, 2])
        block = ph.block()

        @block.sync
        def _(sp):
            sp.dma_start(gamma[:, :], K.inp[gamma_name].partition_broadcast(P)).then_inc(loaded, 16)
            sp.dma_start(beta[:, :], K.inp[beta_name].partition_broadcast(P)).then_inc(loaded, 16)

        @block.scalar
        def _(sc):
            with sc.Fori(0, NT // UN) as it:
                hold(sc, s_var, it + 1)
                sc.sqrt(mv[:, :, 1], mv[:, :, 1]).then_inc(s_rstd, 1)

        @block.vector
        def _(dve):
            dve.wait_ge(loaded, 32)
            with dve.Fori(0, NT // UN) as it:
                turn = LoopChain(dve, chain, it, 2 * UN + 1 + 4)
                row_stats(turn, dve, stats, mv, [K.aux[:, it * UN + u, :] for u in range(UN)])
                dve.tensor_scalar(mv[:, :, 1], mv[:, :, 1], LN_EPS, None, ALU.add).then_inc(s_var, 1)
                hold(dve, s_rstd, it + 1)
                turn(dve.reciprocal(mv[:, :, 1], mv[:, :, 1]))
                rows = K.aux[:, bass.ds(it * UN, UN), :]
                wide = [P, UN, D]
                turn(dve.tensor_tensor(rows, rows, mv[:, :, 0].unsqueeze(2).to_broadcast(wide), ALU.subtract))
                turn(dve.tensor_tensor(rows, rows, mv[:, :, 1].unsqueeze(2).to_broadcast(wide), ALU.mult))
                turn(dve.tensor_tensor(rows, rows, gamma[:, :].unsqueeze(1).to_broadcast(wide), ALU.mult))
                x_rows = K.x[:, bass.ds(it * UN, UN), :]
                turn(dve.tensor_tensor(x_rows, x_rows, rows, ALU.add))
                turn.end()
            dve.tensor_tensor(K.x[:, :, :], K.x[:, :, :], beta[:, :].unsqueeze(1).to_broadcast([P, NT, D]), ALU.add)


def top_two_gates(K, bias_name, cols):
    def batch(dve, turn, it, ps, tools):
        logits, best, marked = (tools.work2[:, :, i * 8:i * 8 + 8] for i in range(3))
        top = tools.small[:, :, 0]
        wide = [P, UN, cols]
        b = tools.vec[bias_name][:, :].unsqueeze(1).to_broadcast(wide)
        turn(dve.tensor_tensor(logits, ps, b, ALU.add))
        for u in range(UN):
            turn(dve.max(best[:, u, :], logits[:, u, :]))
        turn(dve.tensor_copy(top, best[:, :, 0]))
        turn(dve.memset(best[:, :, 2:8], BIG))
        for u in range(UN):
            turn(dve.match_replace(marked[:, u, :], best[:, u, :], logits[:, u, :], -BIG))
        dve.tensor_tensor(logits, logits, top.unsqueeze(2).to_broadcast(wide), ALU.subtract).then_inc(tools.s_sum, 1)
        hold(dve, tools.s_exp, it + 1)
        turn(dve.scalar_tensor_tensor(out=logits, in0=marked, scalar=-BIG, in1=logits, op0=ALU.is_equal, op1=ALU.mult))
        turn(dve.tensor_reduce(top, logits, AX, ALU.add))
        turn(dve.reciprocal(top, top))
        return dve.tensor_tensor(K.gate[:, bass.ds(it * UN, UN), :], logits, top.unsqueeze(2).to_broadcast(wide), ALU.mult)
    return batch, 6 + 2 * UN


def largest_gates(K, tag, count):
    nc = K.nc
    with Phase(nc, tag) as ph:
        step, lchain, s_row, s_copied, s_diag = (ph.sem(n) for n in ("step", "lchain", "row", "copied", "diag"))
        diag, rows = ph.sb("diag", [P, NT, NPT]), ph.sb("rows", [P, NT, NPT])
        earlier = ph.sb("earlier", [P, 2 * N])
        found, value, rank = ph.sb("found", [P, N]), ph.sb("value", [P, NT]), ph.sb("rank", [P, NT])
        block = ph.block()
        flat, flat_diag = rows[:, :, :].rearrange("p t n -> p (t n)"), diag[:, :, :].rearrange("p t n -> p (t n)")
        cuts = [(c, min(c + 4 * NPT, N)) for c in range(0, N, 4 * NPT)]

        @block.tensor
        def _(pe):
            pe.wait_ge(s_diag, 1)
            for i, (a, b) in enumerate(cuts):
                pe.matmul(K.ps[:, i, 0:b - a], K.ones[:, :], flat_diag[:, a:b], start=True, stop=True).then_inc(s_row, 1)

        @block.scalar
        def _(sc):
            for i, (a, b) in enumerate(cuts):
                sc.wait_ge(s_row, i + 1)
                sc.copy(flat[:, a:b], K.ps[:, i, 0:b - a]).then_inc(s_copied, 1)

        @block.vector
        def _(dve):
            link = Chain(dve, step)
            wide = [P, NT, NPT]
            eye = K.ident[:, 0:NPT].unsqueeze(1).to_broadcast(wide)
            dve.tensor_tensor(diag[:, :, :], eye, K.token_w[:, :].unsqueeze(2).to_broadcast(wide), ALU.mult).then_inc(s_diag, 1)
            link(dve.memset(earlier[:, 0:N], 1.0))
            link(dve.memset(earlier[:, N:2 * N], 0.0))
            link(dve.tensor_scalar(earlier[:, N:N + NPT], K.row_f[:, 0:NPT], K.col_f[:, 0:1], None, ALU.is_lt))
            link(dve.tensor_tensor(K.x[:, :, :], K.x[:, :, :], K.aux[:, :, :], ALU.add))
            dve.wait_ge(s_copied, len(cuts))
            link(dve.tensor_tensor(diag[:, :, :], rows[:, :, :], eye, ALU.mult))
            link(dve.tensor_reduce(value[:, :], diag[:, :, :], AX, ALU.add))
            with dve.Fori(0, NT) as t:
                turn = LoopChain(dve, lchain, t, 3)
                mine = value[:, bass.ds(t, 1)]
                turn(dve.scalar_tensor_tensor(out=found[:, :], in0=flat, scalar=mine, in1=earlier[:, bass.ds(N - t * NPT, N)],
                                              op0=ALU.is_equal, op1=ALU.mult))
                turn(dve.scalar_tensor_tensor(out=found[:, :], in0=flat, scalar=mine, in1=found[:, :],
                                              op0=ALU.is_gt, op1=ALU.add))
                turn(dve.tensor_reduce(rank[:, bass.ds(t, 1)], found[:, :], AX, ALU.add))
                turn.end()
            dve.scalar_tensor_tensor(out=K.gate[:, :, 0], in0=rank[:, :], scalar=float(count), in1=K.token_w[:, :],
                                     op0=ALU.is_lt, op1=ALU.mult)


def store(K, out):
    nc = K.nc
    with Phase(nc, "store") as ph:
        stored = ph.sem("stored")
        block = ph.block()

        @block.sync
        def _(sp):
            rows = out.rearrange("(t p) d -> p t d", p=NPT)
            sp.dma_start(rows[0:112], K.x[0:112, :, :]).then_inc(stored, 16)
            sp.dma_start(rows[112:NPT], K.x[112:NPT, :, :]).then_inc(stored, 16)
            sp.wait_ge(stored, 32)


def build(nc, inp, out):
    K = Net()
    K.nc, K.inp = nc, inp
    ctx = ExitStack()
    with ctx:
        def sb(name, shape, dt=F32):
            return ctx.enter_context(nc.sbuf_tensor(name, shape, dt))

        Net.ctx = ctx
        Net.passed = {e.engine: ctx.enter_context(nc.semaphore(f"passed_{name}")) for name, e in (
            ("sp", nc.sync), ("act", nc.scalar), ("pe", nc.tensor), ("dve", nc.vector), ("pool", nc.gpsimd))}
        K.ps = ctx.enter_context(nc.psum_tensor("ps", [P, 8, 512], F32))
        K.x = sb("x_nodes", [P, NT, D])
        K.acc = sb("acc", [P, NT, TW])
        K.loop_out = K.aux = sb("aux", [P, NT, D])
        K.row_f, K.row_b = sb("row_f", [P, P]), sb("row_b", [P, P], BF16)
        K.col_f = sb("col_f", [P, 1])
        K.ident, K.ident_b = sb("ident", [P, P]), sb("ident_b", [P, P], BF16)
        K.before, K.ones = sb("before", [P, P]), sb("ones", [P, P])
        K.tile_of, K.rel_row, K.src_row = (sb(n, [P, KT], I32) for n in ("tile_of", "rel_row", "src_row"))
        K.slot_dst, K.slot_w = sb("slot_dst", [P, KT]), sb("slot_w", [P, KT])
        K.degree = sb("degree", [P, NT])
        K.rec_dram = nc.dram_tensor("rec_dram", [KT * P + EC, 4], F32).ap()
        K.rel_table = nc.dram_tensor("rel_table", [NPAD, R, D], F32).ap()
        K.node_table = nc.dram_tensor("node_table", [NPAD, D], F32).ap()
        K.att_table = nc.dram_tensor("att_table", [NPAD, TW], F32).ap()
        K.dinv = sb("dinv", [P, NT])
        K.pair_rows = nc.dram_tensor("pair_rows", [2, KT, P], BF16).ap()
        rel_rows = K.rel_table.rearrange("n r f -> (n r) f")
        setup(K)

        def pre_norm(dve, turn, t, u, xin, mv, bias):
            return dve.tensor_scalar(xin, K.x[:, t, :], mv[:, u, 0:1], mv[:, u, 1:2], ALU.subtract, ALU.mult)

        def pre_hidden(dve, turn, t, u, xin, mv, bias):
            turn(dve.tensor_tensor(xin, K.acc[:, t, 0:D], bias[:, :], ALU.add))
            turn(dve.tensor_tensor(xin, xin, K.loop_out[:, t, :], ALU.add))
            return dve.tensor_scalar(xin, xin, 0.0, None, ALU.max)

        with ExitStack() as scope:
            rec = scope.enter_context(nc.sbuf_tensor("rec", [P, EC, 4], F32))
            addr = scope.enter_context(nc.sbuf_tensor("addr", [P, EC], I32))
            sort_edges(K, rec, addr)
            relation_tables(K, "rel1", "L0_gnn_w1", "L0_gnn_loop_w1", pre_norm, 2 * UN + 1, True, scatter=(rec, addr))
        K.src_tile, K.tile_f = sb("src_tile", [P, KT]), sb("tile_f", [P, KT])
        K.in_tile = sb("in_tile", [NT, KT], BF16)
        K.last_of = sb("last_of", [CB, 4, NT])
        K.no_edge = sb("no_edge", [P, NT])
        edge_rows(K)
        edge_sum(K, "sum1", rel_rows, K.rel_row, K.slot_w, count=True)
        relation_tables(K, "rel2", "L0_gnn_w2", "L0_gnn_loop_w2", pre_hidden, 2 * UN, False)
        edge_sum(K, "sum2", rel_rows, K.rel_row, K.slot_w)
        residual(K, "res0", "L0_gnn_b2")

        K.xt = sb("xt_nodes", [P, DC, NPAD])
        K.gate = sb("gate", [P, NT, 8])
        node_pass(K, "prep0", ["L0_ffn_Wr"], [("L0_ffn_br", 8)], normed(K), 0, norm=lambda t: K.x[:, t, :],
                  keep_xt=True, batch_post=softmax_gates(K, "L0_ffn_br", 8), batch_steps=4, gate_cols=8)
        dense_experts(K, "experts0")

        K.edge_w = sb("edge_w", [P, KT, 4])
        K.score_src, K.score_dst = sb("score_src", [P, NT, 4]), sb("score_dst", [P, NT, 4])
        degree_roots(K)

        def scaled(dve, turn, t, u, ps, tools):
            return dve.tensor_scalar(K.aux[:, t, :], ps[:, 0:D], K.dinv[:, bass.ds(t, 1)], None, ALU.mult)

        def aux_rows(it):
            return K.aux[:, bass.ds(it * UN, UN), :]

        def acc_rows(it):
            return K.acc[:, bass.ds(it * UN, UN), :]

        node_pass(K, "gcn", ["L1_gnn_W1"], [], normed(K), 0, norm=lambda t: K.x[:, t, :], post=scaled,
                  table=(K.node_table, aux_rows))
        edge_sum(K, "sum3", K.node_table, K.src_row, None)

        def gcn_out(dve, turn, it, xin, tools):
            tiles, wide = bass.ds(it * UN, UN), [P, UN, D]
            turn(dve.tensor_tensor(xin, K.acc[:, tiles, 0:D], K.aux[:, tiles, :], ALU.add))
            turn(dve.tensor_tensor(xin, xin, K.dinv[:, tiles].unsqueeze(2).to_broadcast(wide), ALU.mult))
            turn(dve.tensor_tensor(xin, xin, tools.vec["L1_gnn_b1"][:, :].unsqueeze(1).to_broadcast(wide), ALU.add))
            return dve.tensor_scalar(xin, xin, 0.0, None, ALU.max)

        post, act_post, n = attention_rows(K, 1, "L1_gnn_att_src", "L1_gnn_att_dst")
        node_pass(K, "gat1", ["L1_gnn_W2"], [("L1_gnn_b1", D), ("L1_gnn_att_src", D), ("L1_gnn_att_dst", D)],
                  gcn_out, 3, post=post, post_steps=n, act_post=act_post, table=(K.att_table, acc_rows),
                  ones_cols=ones_of(K, 1))
        edge_weights(K, "score1", 1, NT)
        edge_sum(K, "att1", K.att_table, K.src_row, K.edge_w, heads=1)
        finish_attention(K, "res1", 1, "L1_gnn_b2", relu=True)

        K.pick = sb("pick", [P, 2], I32)
        node_pass(K, "prep1", [], [], normed(K), 0, norm=lambda t: K.x[:, t, :], keep_xt=True, keep_xn=True)
        route_two(K, "route1")

        def load_picked(sp, eo, b, w1, w2, b1, b2, sem):
            e = nc.values_load(K.pick[0:1, b:b + 1], engines=[sp.engine], min_val=0, max_val=7)
            one = bass.ds(e, 1)
            sp.dma_start(w1, K.inp["L1_ffn_W1"][one, :, :].rearrange("a (c p) n -> p (a c) n", p=P)).then_inc(sem, 16)
            sp.dma_start(w2, K.inp["L1_ffn_W2"][one, :, :].rearrange("a (c p) n -> p (a c) n", p=P)).then_inc(sem, 16)
            sp.dma_start(b1, K.inp["L1_ffn_b1"][one, :].rearrange("a (c p) -> p (a c)", p=P)).then_inc(sem, 16)
            sp.dma_start(b2, K.inp["L1_ffn_b2"][one, :].to_broadcast([P, D])).then_inc(sem, 16)

        wide_experts(K, "ffn1", 1, 2, 4, ACT.Gelu, load_picked, K.aux)
        add_normed(K, "res1b", "L1_ffn_gamma", "L1_ffn_beta")

        def max_k(dve, turn, it, ps, tools):
            tiles = bass.ds(it * UN, UN)
            h, best = tools.work[:, :, :], tools.work2[:, :, 0:8]
            turn(dve.tensor_copy(h, ps[:, :, 0:D]))
            for _ in range(MAXK // 8):
                turn.all([dve.max(best[:, u, :], h[:, u, :]) for u in range(UN)])
                turn.all([dve.match_replace(h[:, u, :], best[:, u, :], h[:, u, :], -BIG) for u in range(UN)])
            turn(dve.scalar_tensor_tensor(out=K.aux[:, tiles, :], in0=h, scalar=-BIG, in1=ps[:, :, 0:D],
                                          op0=ALU.is_equal, op1=ALU.mult))
            return dve.tensor_tensor(K.x[:, tiles, :], K.x[:, tiles, :], ps[:, :, D:2 * D], ALU.add)

        node_pass(K, "sage", ["L2_gnn_W_neigh", "L2_gnn_W_self"], [], normed(K), 0, norm=lambda t: K.x[:, t, :],
                  post=max_k, post_steps=2 + MAXK // 4 * UN, table=(K.node_table, aux_rows))
        edge_sum(K, "sum4", K.node_table, K.src_row, None)
        add_mean(K, "res2")

        K.slots, K.slot_gate = sb("slots", [P, 2, NT], I32), sb("slot_gate", [P, 2, NT])
        K.block_expert = sb("block_expert", [P, NB_X], I32)
        K.sorted_x = nc.dram_tensor("sorted_x", [NB_X * TB + 2 * NPAD, D], F32).ap()
        K.sorted_y = nc.dram_tensor("sorted_y", [NB_X * TB, D], F32).ap()

        def load_expert(sp, e, w1, w2, b1, b2, sem):
            one = bass.ds(e, 1)
            sp.dma_start(w1, K.inp["L2_ffn_W1"][one, :, :].rearrange("a (c p) n -> p (a c) n", p=P)).then_inc(sem, 16)
            sp.dma_start(w2, K.inp["L2_ffn_W2"][one, :, :].rearrange("a (c p) n -> p (a c) n", p=P)).then_inc(sem, 16)
            sp.dma_start(b1, K.inp["L2_ffn_b1"][one, :].rearrange("a (c p) -> p (a c)", p=P)).then_inc(sem, 16)
            sp.dma_start(b2, K.inp["L2_ffn_b2"][one, :].to_broadcast([P, D])).then_inc(sem, 16)

        gates, n = top_two_gates(K, "L2_ffn_bg", 8)
        node_pass(K, "prep2", ["L2_ffn_Wg"], [("L2_ffn_bg", 8)], normed(K), 0, norm=lambda t: K.x[:, t, :],
                  keep_xn=True, batch_post=gates, batch_steps=n, gate_cols=8)
        route_tokens(K, "route2")
        sorted_experts(K, "ffn2", load_expert, ACT.Gelu, 8)
        combine_experts(K, "join2")

        LOOPED = 1250 // NPT
        post, act_post, n = attention_rows(K, 4, "L3_gnn_a1_src", "L3_gnn_a1_dst")
        node_pass(K, "gat2", ["L3_gnn_W1"], [("L3_gnn_a1_src", D), ("L3_gnn_a1_dst", D)], normed(K), 0,
                  norm=lambda t: K.x[:, t, :], post=post, post_steps=n, act_post=act_post, table=(K.att_table, acc_rows),
                  ones_cols=ones_of(K, 4))
        edge_weights(K, "score2", 4, LOOPED)
        edge_sum(K, "att2", K.att_table, K.src_row, K.edge_w, heads=4)
        finish_attention(K, "mid", 4, "L3_gnn_b1", to_aux=True)

        def mid_norm(dve, turn, it, xin, tools):
            tiles, wide = bass.ds(it * UN, UN), [P, UN, D]
            turn(dve.tensor_tensor(xin, K.aux[:, tiles, :], tools.mv[:, :, 0].unsqueeze(2).to_broadcast(wide), ALU.subtract))
            turn(dve.tensor_tensor(xin, xin, tools.mv[:, :, 1].unsqueeze(2).to_broadcast(wide), ALU.mult))
            turn(dve.tensor_tensor(xin, xin, tools.vec["L3_gnn_ln_g"][:, :].unsqueeze(1).to_broadcast(wide), ALU.mult))
            turn(dve.tensor_tensor(xin, xin, tools.vec["L3_gnn_ln_b"][:, :].unsqueeze(1).to_broadcast(wide), ALU.add))
            return dve.tensor_scalar(xin, xin, 0.0, None, ALU.max)

        post, act_post, n = attention_rows(K, 1, "L3_gnn_a2_src", "L3_gnn_a2_dst")
        node_pass(K, "gat3", ["L3_gnn_W2"], [(f"L3_gnn_{v}", D) for v in ("ln_g", "ln_b", "a2_src", "a2_dst")],
                  mid_norm, 4, norm=lambda t: K.aux[:, t, :], post=post, post_steps=n, act_post=act_post,
                  table=(K.att_table, acc_rows), ones_cols=ones_of(K, 1))
        edge_weights(K, "score3", 1, LOOPED)
        edge_sum(K, "att3", K.att_table, K.src_row, K.edge_w, heads=1)
        finish_attention(K, "res3", 1, "L3_gnn_b2")

        K.token_w = sb("token_w", [P, NT])

        def token_weights(dve, turn, it, ps, tools):
            return dve.tensor_tensor(K.token_w[:, bass.ds(it * UN, UN)], ps[:, :, 0],
                                     tools.vec["L3_ffn_br"][:, :].to_broadcast([P, UN]), ALU.add)

        def load_only(sp, eo, b, w1, w2, b1, b2, sem):
            sp.dma_start(w1, K.inp["L3_ffn_w1"].rearrange("(c p) n -> p c n", p=P)).then_inc(sem, 16)
            sp.dma_start(w2, K.inp["L3_ffn_w2"].rearrange("(c p) n -> p c n", p=P)).then_inc(sem, 16)
            sp.dma_start(b1, K.inp["L3_ffn_b1"].rearrange("(c p) -> p c", p=P)).then_inc(sem, 16)
            sp.dma_start(b2, K.inp["L3_ffn_b2"].partition_broadcast(P)).then_inc(sem, 16)

        node_pass(K, "prep3", ["L3_ffn_wr"], [("L3_ffn_br", 1)], normed(K), 0, norm=lambda t: K.x[:, t, :],
                  keep_xt=True, keep_xn=True, batch_post=token_weights, gate_cols=1, gates_exp=False)
        with ExitStack() as scope:
            def scoped(name, shape, dt=F32):
                return scope.enter_context(nc.sbuf_tensor(name, shape, dt))

            K.rank_rows, K.earlier = scoped("rank_rows", [P, N])[:, :], scoped("earlier", [P, 2 * N], BF16)
            K.found, K.own_value = scoped("found", [P, N], BF16), scoped("own_value", [P, NT])
            K.rank = scoped("rank", [P, NT])
            rank_rows(K, "pick")
            wide_experts(K, "ffn3", 1, 1, 8, ACT.Gelu_apprx_tanh, load_only, K.acc[:, :, 0:D], beside=node_ranks(K))
            add_largest(K, "res4", N // 2 - 1)
        store(K, out)




def kernel(**inputs):
    import numpy as _np
    import concourse.bacc as _bacc
    from concourse import mybir as _mybir
    from concourse.bass_utils import run_bass_kernel_spmd as _run

    nc = _bacc.Bacc("TRN2", target_bir_lowering=False, num_devices=1)
    arrays, inp = {}, {}
    for name, value in inputs.items():
        if name == "L3_ffn_attention_mask":
            continue
        a = _np.ascontiguousarray(value)
        arrays[f"in_{name}"] = a
        inp[name] = nc.dram_tensor(f"in_{name}", list(a.shape), _mybir.dt.from_np(a.dtype), kind="ExternalInput").ap()
    out = nc.dram_tensor("out_0", [N, D], F32, kind="ExternalOutput").ap()
    build(nc, inp, out)
    r = _run(nc, [arrays], core_ids=[0])
    return r.results[0]["out_0"]
```
